# Optimizing a Trainium2 kernel written in Bass

```python
import numpy as np
import jax
import jax.numpy as jnp

def _softmax(x, axis=-1):
    return jax.nn.softmax(x, axis=axis)

def _gelu(x):
    return jax.nn.gelu(x, approximate=True)

def _silu(x):
    return jax.nn.silu(x)

def _sigmoid(x):
    return jax.nn.sigmoid(x)

def _layernorm(x, axis=-1, eps=1e-05):
    m = jnp.mean(x, axis=axis, keepdims=True)
    v = jnp.var(x, axis=axis, keepdims=True)
    return (x - m) / jnp.sqrt(v + eps)

def _scatter_add(tgt, idx, src, axis=0):
    return tgt.at[idx].add(src)

def _segment_sum(src, seg, n):
    return jax.ops.segment_sum(src, seg, n)
kernel_name = 'mk_seq_postln_d1_jaxref_r8_4fed11'

def setup_inputs(seed: int=0):
    np.random.seed(seed)
    _w = jnp.asarray

    def _L0_attn_setup():
        import jax, jax.numpy as jnp
        import numpy as np
        B, L, DM = (2, 128, 256)
        DIN, N, DTR, K = (256, 16, 128, 4)
        key = jax.random.key(seed)
        ks = jax.random.split(key, 8)
        s = lambda k, sh: jax.random.normal(k, sh, jnp.float32) * 0.02
        A = jnp.tile(jnp.arange(1, N + 1, dtype=jnp.float32)[None, :], (DIN, 1))
        return {'x': jax.random.normal(ks[0], (B, L, DM), jnp.float32), 'W_in': s(ks[1], (DM, 2 * DIN)), 'conv_w': s(ks[2], (DIN, DIN, K)), 'conv_b': jnp.zeros((DIN,), jnp.float32), 'W_x': s(ks[3], (DIN, DTR + 2 * N)), 'W_dt': s(ks[4], (DTR, DIN)), 'b_dt': jnp.zeros((DIN,), jnp.float32), 'A_log': jnp.log(A), 'D': jnp.ones((DIN,), jnp.float32), 'W_out': s(ks[5], (DIN, DM))}
    _L0_attn_in = _L0_attn_setup()

    def _L0_ffn_setup():
        import jax, jax.numpy as jnp
        import numpy as np
        CAPACITY = 0.125
        HEAD_DIM = 128
        N_HEADS = 16
        N_KV_HEADS = 8
        ROPE_THETA = 10000.0
        EPS = 1e-06

        def _rms_norm(x, w):
            return x * jax.lax.rsqrt(jnp.mean(x * x, axis=-1, keepdims=True) + EPS) * w

        def _rotate_half(t):
            h = t.shape[-1] // 2
            return jnp.concatenate([-t[..., h:], t[..., :h]], axis=-1)
        key = jax.random.key(seed)
        ks = jax.random.split(key, 12)
        B, T, D = (4, 512, 256)
        I = 1024
        s = 0.02
        return {'hidden_states': jax.random.normal(ks[0], (B, T, D), jnp.float32), 'w_router': jax.random.normal(ks[1], (D,), jnp.float32) * s, 'wq': jax.random.normal(ks[2], (D, N_HEADS * HEAD_DIM), jnp.float32) * s, 'bq': jnp.zeros((N_HEADS * HEAD_DIM,), jnp.float32), 'wk': jax.random.normal(ks[3], (D, N_KV_HEADS * HEAD_DIM), jnp.float32) * s, 'bk': jnp.zeros((N_KV_HEADS * HEAD_DIM,), jnp.float32), 'wv': jax.random.normal(ks[4], (D, N_KV_HEADS * HEAD_DIM), jnp.float32) * s, 'bv': jnp.zeros((N_KV_HEADS * HEAD_DIM,), jnp.float32), 'wo': jax.random.normal(ks[5], (N_HEADS * HEAD_DIM, D), jnp.float32) * s, 'w_gate': jax.random.normal(ks[6], (D, I), jnp.float32) * s, 'w_up': jax.random.normal(ks[7], (D, I), jnp.float32) * s, 'w_down': jax.random.normal(ks[8], (I, D), jnp.float32) * s, 'ln1_w': jnp.ones((D,), jnp.float32), 'ln2_w': jnp.ones((D,), jnp.float32)}
    _L0_ffn_in = _L0_ffn_setup()
    _d = {'L0_attn_x': _L0_attn_in['x'], 'L0_attn_W_in': _L0_attn_in['W_in'], 'L0_attn_conv_w': _L0_attn_in['conv_w'], 'L0_attn_conv_b': _L0_attn_in['conv_b'], 'L0_attn_W_x': _L0_attn_in['W_x'], 'L0_attn_W_dt': _L0_attn_in['W_dt'], 'L0_attn_b_dt': _L0_attn_in['b_dt'], 'L0_attn_A_log': _L0_attn_in['A_log'], 'L0_attn_D': _L0_attn_in['D'], 'L0_attn_W_out': _L0_attn_in['W_out'], 'L0_ffn_w_router': _L0_ffn_in['w_router'], 'L0_ffn_wq': _L0_ffn_in['wq'], 'L0_ffn_bq': _L0_ffn_in['bq'], 'L0_ffn_wk': _L0_ffn_in['wk'], 'L0_ffn_bk': _L0_ffn_in['bk'], 'L0_ffn_wv': _L0_ffn_in['wv'], 'L0_ffn_bv': _L0_ffn_in['bv'], 'L0_ffn_wo': _L0_ffn_in['wo'], 'L0_ffn_w_gate': _L0_ffn_in['w_gate'], 'L0_ffn_w_up': _L0_ffn_in['w_up'], 'L0_ffn_w_down': _L0_ffn_in['w_down'], 'L0_ffn_ln1_w': _L0_ffn_in['ln1_w'], 'L0_ffn_ln2_w': _L0_ffn_in['ln2_w']}
    _x0 = _d['L0_attn_x']
    _d['L0_attn_x'] = jax.random.normal(jax.random.fold_in(jax.random.key(seed), 1), (4, 512, 256), dtype=_x0.dtype)
    del _x0
    return _d

def reference(L0_attn_x, L0_attn_W_in, L0_attn_conv_w, L0_attn_conv_b, L0_attn_W_x, L0_attn_W_dt, L0_attn_b_dt, L0_attn_A_log, L0_attn_D, L0_attn_W_out, L0_ffn_w_router, L0_ffn_wq, L0_ffn_bq, L0_ffn_wk, L0_ffn_bk, L0_ffn_wv, L0_ffn_bv, L0_ffn_wo, L0_ffn_w_gate, L0_ffn_w_up, L0_ffn_w_down, L0_ffn_ln1_w, L0_ffn_ln2_w):

    def _L0_attn_ref(x, W_in, conv_w, conv_b, W_x, W_dt, b_dt, A_log, D, W_out):
        import jax, jax.numpy as jnp
        import numpy as np
        B, L, DM = (2, 128, 256)
        DIN, N, DTR, K = (256, 16, 128, 4)
        b, l, _ = x.shape
        n = A_log.shape[1]
        dtr = W_dt.shape[0]
        xz = x @ W_in
        xc, r = jnp.split(xz, 2, axis=-1)
        xt = xc.transpose(0, 2, 1)
        xconv = jax.lax.conv_general_dilated(xt, conv_w, (1,), [(conv_w.shape[2] - 1, 0)], dimension_numbers=('NCH', 'OIH', 'NCH'))
        xs = (xconv + conv_b[None, :, None]).transpose(0, 2, 1)
        u = jax.nn.silu(xs)
        A = -jnp.exp(A_log)
        dbc = u @ W_x
        delta = jax.nn.softplus(dbc[..., :dtr] @ W_dt + b_dt)
        Bm = dbc[..., dtr:dtr + n]
        Cm = dbc[..., dtr + n:]
        deltaA = jnp.exp(jnp.einsum('bld,dn->lbdn', delta, A))
        deltaBu = jnp.einsum('bld,bln->lbdn', delta * u, Bm)

        def step(h, inp):
            dA, dBu, c = inp
            h = dA * h + dBu
            return (h, jnp.einsum('bdn,bn->bd', h, c))
        h0 = jnp.zeros((b, u.shape[-1], n), u.dtype)
        _, ys = jax.lax.scan(step, h0, (deltaA, deltaBu, Cm.transpose(1, 0, 2)))
        y = ys.transpose(1, 0, 2) + u * D
        out = y * jax.nn.silu(r)
        return out @ W_out + xs

    def _L0_ffn_ref(hidden_states, w_router, wq, bq, wk, bk, wv, bv, wo, w_gate, w_up, w_down, ln1_w, ln2_w):
        import jax, jax.numpy as jnp
        import numpy as np
        CAPACITY = 0.125
        HEAD_DIM = 128
        N_HEADS = 16
        N_KV_HEADS = 8
        ROPE_THETA = 10000.0
        EPS = 1e-06

        def _rms_norm(x, w):
            return x * jax.lax.rsqrt(jnp.mean(x * x, axis=-1, keepdims=True) + EPS) * w

        def _rotate_half(t):
            h = t.shape[-1] // 2
            return jnp.concatenate([-t[..., h:], t[..., :h]], axis=-1)
        B, T, D = hidden_states.shape
        k = max(1, int(T * CAPACITY))
        scores = jnp.einsum('btd,d->bt', hidden_states, w_router)
        _, idx = jax.lax.top_k(scores, k)
        idx = jnp.sort(idx, axis=-1)
        b = jnp.arange(B)[:, None]
        sel = hidden_states[b, idx]
        sel_scores = scores[b, idx]
        S = B * k
        x = sel.reshape(S, D)
        pos = idx.reshape(S)
        inv_freq = 1.0 / ROPE_THETA ** (jnp.arange(0, HEAD_DIM, 2, dtype=jnp.float32) / HEAD_DIM)
        ang = pos.astype(jnp.float32)[:, None] * inv_freq
        cos = jnp.concatenate([jnp.cos(ang), jnp.cos(ang)], axis=-1)[:, None, :]
        sin = jnp.concatenate([jnp.sin(ang), jnp.sin(ang)], axis=-1)[:, None, :]
        h = _rms_norm(x, ln1_w)
        q = (h @ wq + bq).reshape(S, N_HEADS, HEAD_DIM)
        kk = (h @ wk + bk).reshape(S, N_KV_HEADS, HEAD_DIM)
        v = (h @ wv + bv).reshape(S, N_KV_HEADS, HEAD_DIM)
        q = q * cos + _rotate_half(q) * sin
        kk = kk * cos + _rotate_half(kk) * sin
        rep = N_HEADS // N_KV_HEADS
        kk = jnp.repeat(kk, rep, axis=1)
        v = jnp.repeat(v, rep, axis=1)
        att = jnp.einsum('shd,thd->hst', q, kk) / np.sqrt(HEAD_DIM)
        causal = jnp.tril(jnp.ones((S, S), bool))
        att = jnp.where(causal[None], att, jnp.finfo(att.dtype).min)
        att = jax.nn.softmax(att, axis=-1)
        attn_out = jnp.einsum('hst,thd->shd', att, v).reshape(S, N_HEADS * HEAD_DIM) @ wo
        x1 = x + attn_out
        h2 = _rms_norm(x1, ln2_w)
        mlp = jax.nn.silu(h2 @ w_gate) * (h2 @ w_up) @ w_down
        processed = x1 + mlp
        gate = jax.nn.sigmoid(sel_scores).reshape(S, 1)
        gated = gate * processed + (1.0 - gate) * x
        output = hidden_states.at[b, idx].set(gated.reshape(B, k, D))
        return output
    x = L0_attn_x
    x = _layernorm(x + _L0_attn_ref(x, L0_attn_W_in, L0_attn_conv_w, L0_attn_conv_b, L0_attn_W_x, L0_attn_W_dt, L0_attn_b_dt, L0_attn_A_log, L0_attn_D, L0_attn_W_out), axis=-1)
    x = _layernorm(x + _L0_ffn_ref(x, L0_ffn_w_router, L0_ffn_wq, L0_ffn_bq, L0_ffn_wk, L0_ffn_bk, L0_ffn_wv, L0_ffn_bv, L0_ffn_wo, L0_ffn_w_gate, L0_ffn_w_up, L0_ffn_w_down, L0_ffn_ln1_w, L0_ffn_ln2_w), axis=-1)
    return x

_drawn_inputs = setup_inputs


def setup_inputs(seed=0):
    import zlib

    import numpy as np

    out = dict(_drawn_inputs(seed))
    spreads = {'L0_attn_conv_b': (0.0, 0.1),
     'L0_attn_b_dt': (0.0, 0.8),
     'L0_attn_D': (1.0, 0.6),
     'L0_ffn_bq': (0.0, 0.8),
     'L0_ffn_bk': (0.0, 0.8),
     'L0_ffn_bv': (0.0, 0.77),
     'L0_ffn_ln1_w': (1.0, 0.6),
     'L0_ffn_ln2_w': (1.0, 0.6)}
    factors = {'L0_attn_W_x': 8.0,
     'L0_attn_W_dt': 33.708,
     'L0_attn_A_log': 8.0,
     'L0_attn_W_out': 8.0,
     'L0_ffn_w_router': 4.34,
     'L0_ffn_wq': 8.0,
     'L0_ffn_wk': 8.0,
     'L0_ffn_wv': 6.99,
     'L0_ffn_wo': 4.197,
     'L0_ffn_w_gate': 8.0,
     'L0_ffn_w_up': 8.0,
     'L0_ffn_w_down': 8.0}
    for name, (base, spread) in spreads.items():
        noise = np.random.default_rng([zlib.crc32(name.encode()), seed]).standard_normal(out[name].shape)
        drawn = base * np.exp(spread * noise) if base else spread * noise
        out[name] = jnp.asarray(drawn.astype(out[name].dtype))
    for name, factor in factors.items():
        out[name] = (out[name] * factor).astype(out[name].dtype)
    return out
```

```python
from contextlib import ExitStack

import numpy as np

import concourse.bass as bass
from concourse import mybir

F32 = mybir.dt.float32
BF16 = mybir.dt.bfloat16
ALU = mybir.AluOpType
ACT = mybir.ActivationFunctionType
AX = mybir.AxisListType

P = 128
HEAD_DIM = 128
N_HEADS = 16
N_KV = 8
CAPACITY = 0.125
ROPE_THETA = 10000.0
LN_EPS = 1e-5
RMS_EPS = 1e-6
ROUND = 1.5 * 2.0**23
TWO_PI = 2.0 * np.pi
NEG = -1.0e38

FRONT_AT = {0: ("xT0",), 1: ("xT1",), 2: ("xc0",), 3: ("xc1",), 4: ("r0", "r1"), 5: ("cv0",), 6: ("cv1",),
            7: ("silu",), 8: ("dt", "bc"), 9: ("dl0", "dl1"), 10: ("sp",), 13: ("du0",), 14: ("du1",)}
FRONT = [x for n in sorted(FRONT_AT) for x in FRONT_AT[n]]
TAIL_AT = {1: ("yt0",), 2: ("yt1",), 3: ("o0",), 4: ("o1",), 5: ("ln",), 8: ("sb",), 10: ("pf",), 12: ("ga",)}
TAIL = [x for n in sorted(TAIL_AT) for x in TAIL_AT[n]]
NO_FILL = ("silu", "sp", "ln")


class Fills:

    def __init__(self):
        self.at = {}
        self.uses = [0] * 8

    def add(self, name, bank):
        self.at[name] = (bank, self.uses[bank])
        self.uses[bank] += 1


def two_pi_parts():
    a = float(np.float32(np.round(TWO_PI * 2**8) / 2**8))
    b = float(np.float32(np.round((TWO_PI - a) * 2**20) / 2**20))
    return a, b, float(np.float32(TWO_PI - a - b))


def block_kernel(nc, x, W_in, conv_w, conv_b, W_x, W_dt, b_dt, A_log, D, W_out, w_router, wq, bq, wk, bk, wv, bv,
                 wo, w_gate, w_up, w_down, ln1_w, ln2_w, inv_freq, out):
    B, L, DM = x.shape
    DIN, NST = A_log.shape
    TAPS = conv_w.shape[2]
    DTR = W_dt.shape[0]
    FF = w_gate.shape[1]
    C = L // P
    KD = DM // P
    K = max(1, int(L * CAPACITY))
    S = B * K
    ST = S // P
    PAD = TAPS - 1
    NCOL = DM + 1
    HQK = N_HEADS + N_KV
    FC = FF // P
    assert DIN == DM and C == 4 and KD == 2 and DTR == P and K == 64 and ST == 2

    fills = Fills()
    rest = [0]

    def add_rest(name):
        fills.add(name, 6 + rest[0] % 2)
        rest[0] += 1

    def add_pieces(b, pieces):
        for piece in pieces:
            if piece not in NO_FILL:
                add_rest((piece, b))

    add_rest("vec")
    for k in range(TAPS):
        add_rest(("cw", k))
    add_pieces(0, FRONT)
    for b in range(B):
        for n in range(NST):
            t = b * NST + n
            for h in range(KD):
                fills.add(("bu", t, h), h)
            if t >= 1:
                for cp in range(2):
                    fills.add(("hT", t - 1, cp), 2 + 2 * ((t - 1) % 2) + cp)
            if b >= 1:
                add_pieces(b - 1, TAIL_AT.get(n, ()))
            if b + 1 < B:
                add_pieces(b + 1, FRONT_AT.get(n, ()))
    T_LAST = B * NST - 1
    for cp in range(2):
        fills.add(("hT", T_LAST, cp), 2 + 2 * (T_LAST % 2) + cp)
    add_pieces(B - 1, TAIL)
    fills.add("h1T", 0)
    for p in range(ST):
        fills.add(("selT", p), 1 + p)
    for j in range(HQK // 2):
        fills.add(("qk", j), 3 + j % 3)
    for v in range(4):
        fills.add(("v", v), 6 + v % 2)
    for i in range(N_HEADS + 3):
        if i < N_HEADS:
            fills.add(("sc", i), i % 2)
        if 1 <= i <= N_HEADS:
            fills.add(("pT", i - 1), 2 + (i - 1) % 2)
        if 2 <= i <= N_HEADS + 1:
            fills.add(("o", i - 2), 4 + (i - 2) % 2)
    for p in range(ST):
        fills.add(("wo", p), 6 + p)
    fills.add("h2T", 0)
    for f in range(FC):
        fills.add(("gu", f), 1 + f % 4)
    for p in range(ST):
        fills.add(("dn", p), 6 + p)
    for i in range(B * C // 2):
        fills.add(("put", i), i % 6)

    with ExitStack() as ctx:
        def sb(name, shape, dt=F32):
            return ctx.enter_context(nc.sbuf_tensor(name, shape, dt))

        def sem(name):
            return ctx.enter_context(nc.semaphore(name))

        bank = [ctx.enter_context(nc.psum_tensor(f"bank{i}", [P, 512], F32)) for i in range(8)]
        filled = [sem(f"filled{i}") for i in range(8)]
        drained = [sem(f"drained{i}") for i in range(8)]

        def at(name):
            return bank[fills.at[name][0]]

        def wait_free(pe, name):
            i, k = fills.at[name]
            if k:
                pe.wait_ge(drained[i], k)

        def fill_done(name, ins):
            ins.then_inc(filled[fills.at[name][0]], 1)

        def wait_filled(eng, name):
            i, k = fills.at[name]
            eng.wait_ge(filled[i], k + 1)

        def drain_done(name, ins):
            ins.then_inc(drained[fills.at[name][0]], 1)

        def wait_drained(eng, name):
            i, k = fills.at[name]
            eng.wait_ge(drained[i], k + 1)

        ident = sb("ident", [P, P])
        ident16 = sb("ident16", [P, P], BF16)
        ones = sb("ones", [P, P])
        before = sb("before", [P, P])
        EARLIER = C * L // 2
        earlier_words = sb("earlier_words", [P, EARLIER])
        earlier = earlier_words[:].bitcast(BF16).rearrange("p (c j) -> p c j", c=C)
        causal = sb("causal", [P, P], BF16)
        slot_no = sb("slot_no", [P, K])
        token_no = sb("token_no", [P, C])
        half_pow = sb("half_pow", [P, C])
        def parts(name, shapes):
            whole = sb(name, [P, sum(int(np.prod(s)) for s in shapes)])
            cut, a = [], 0
            for s in shapes:
                n = int(np.prod(s))
                ap = whole[:, a:a + n]
                if len(s) == 2:
                    ap = ap.rearrange("p (a b) -> p a b", a=s[0])
                elif len(s) == 3:
                    ap = ap.rearrange("p (a b c) -> p a b c", a=s[0], b=s[1])
                cut.append(ap)
                a += n
            return whole, cut

        conv_raw = sb("conv_raw", [P, KD, DIN * TAPS])
        front_a, (conv_t, w_in_s, xT) = parts("front_a", [(TAPS, KD, DIN), (KD, 2 * DIN), (KD, L)])
        front_b, (rT, pre, sp_e, sp_l, xsT) = parts("front_b", [(KD, L)] * 5)
        front_c, (xcT, sp_w) = parts("front_c", [(KD, PAD + L), (KD, L)])
        w_x_s = sb("w_x_s", [P, KD, DTR + 2 * NST])
        w_dt_s = sb("w_dt_s", [P, DIN])
        w_out_s = sb("w_out_s", [P, KD, DM])
        NVEC = 5 * KD + N_HEADS + 2 * N_KV
        vec_rows = sb("vec_rows", [NVEC, P])
        vec = sb("vec", [P, NVEC])
        CB, BDT, DSK, LN1, LN2 = (i * KD for i in range(5))
        BQ = 5 * KD
        BV = BQ + HQK
        a_neg = sb("a_neg", [P, KD, NST])
        a_exp = sb("a_exp", [P, KD, NST])
        router = sb("router", [P, DM])
        freq = sb("freq", [P, HEAD_DIM // 2])
        cos_tab = sb("cos_tab", [P, C, HEAD_DIM])
        sin_tab = sb("sin_tab", [P, C, HEAD_DIM])
        copies = [parts(f"copy{i}", [(KD, L)] * 4 + [(C, DM)] * 2) for i in range(2)]
        silu_r, uT, resT, delta, du_rows, x_rows = ([copies[i][1][j] for i in range(2)] for j in range(6))
        dtT = sb("dtT", [P, L])
        bc_rows = sb("bc_rows", [P, 2, C, 2 * NST])
        NDA = 8
        scan_in = sb("scan_in", [P, NDA * L + 2 * C * DM])
        decay = scan_in[:, 0:NDA * L].rearrange("p (s l) -> p s l", s=NDA)
        bu_rows = scan_in[:, NDA * L:].rearrange("p (s c d) -> p s c d", s=2, c=C)
        state_buf = sb("state", [P, 4 * L])
        state = state_buf[:].rearrange("p (s l) -> p s l", s=4)
        y_buf = sb("y", [P, 2 * C * DM])
        y_rows = y_buf[:].rearrange("p (s c d) -> p s c d", s=2, c=C)
        gT_buf = sb("gT", [P, KD * L])
        gT = gT_buf[:].rearrange("p (k l) -> p k l", k=KD)
        z = sb("z", [P, C, DM])
        stats = sb("stats", [P, C, 6])
        mv = sb("mv", [P, C, 2])
        rstd = sb("rstd", [P, C])
        x1 = sb("x1", [P, B * C, NCOL])
        junk = sb("junk", [P, 2, L])
        score_diag = sb("score_diag", [P, C, P])
        ranks = sb("ranks", [P, 2, C])
        chosen = sb("chosen", [P, C])
        place = sb("place", [P, C])
        onehot = sb("onehot", [P, B // 2, C, 2 * K])
        sel = sb("sel", [P, ST, NCOL])
        cosT = sb("cosT", [P, S])
        sinT = sb("sinT", [P, S])
        ss = sb("ss", [P, ST])
        rrms = sb("rrms", [P, ST])
        top = sb("top", [P, N_HEADS, 2])
        bias = sb("bias", [P, N_HEADS, 2])
        sums = sb("sums", [P, N_HEADS, 2])
        rsum = sb("rsum", [P, N_HEADS, 2])
        x_att = sb("x_att", [P, ST, DM])
        gate_s = sb("gate_s", [P, 2, S])
        gate = sb("gate", [P, ST, 2])
        w_dn = conv_raw[:].rearrange("p a b -> p (a b)").rearrange("p (f n) -> p f n", f=FC)
        w_gu = front_a[:].rearrange("p (k n) -> p k n", k=KD)
        w_o = front_b[:, 0:N_HEADS * DM].rearrange("p (h n) -> p h n", h=N_HEADS)
        w_v = front_c[:, 0:KD * N_KV * HEAD_DIM].rearrange("p (k n) -> p k n", k=KD)
        w_qk = copies[0][0][:].rearrange("p (k n) -> p k n", k=KD)
        qkT = scan_in[:].rearrange("p (h s) -> p h s", h=HQK)
        mT = scan_in[:, 0:FC * S].rearrange("p (f s) -> p f s", f=FC)
        oT = copies[1][0][:, 0:N_HEADS * S].rearrange("p (h s) -> p h s", h=N_HEADS)
        v_rows = copies[1][0][:, N_HEADS * S:].rearrange("p (t n) -> p t n", t=ST)
        qk_raw = state_buf[:, 0:4 * S].rearrange("p (a b s) -> p a b s", a=2, b=2)
        qk_swap = state_buf[:, 4 * S:].rearrange("p (a b s) -> p a b s", a=2, b=2)
        probs = y_buf[:, 0:6 * P].rearrange("p (a s) -> p a s", a=2)
        probsT = y_buf[:, 6 * P:12 * P].rearrange("p (a s) -> p a s", a=2)
        out_rows = y_rows
        selT = gT_buf[:].rearrange("p (t l) -> p t l", t=ST)
        change = score_diag[:].rearrange("p a b -> p (a b)").rearrange("p (t d) -> p t d", t=ST)
        h_rows = earlier_words[:, 0:ST * DM].rearrange("p (t d) -> p t d", t=ST)
        hT = earlier_words[:, ST * DM:].rearrange("p (k s) -> p k s", k=KD)

        in_x = [sem(f"in_x{i}") for i in range(2)]
        in_w = {n: sem(f"in_{n}") for n in ("w_in", "conv", "vec", "w_x", "w_dt", "w_out", "a", "router", "freq",
                                            "w_qk", "w_v", "w_o", "w_gu", "w_dn")}
        consts = sem("consts")
        conv_pad = sem("conv_pad")
        a_ready = sem("a_ready")
        tables = sem("tables")
        angles = sem("angles")
        dve_seq = sem("dve_seq")
        act_seq = sem("act_seq")
        pool_seq = sem("pool_seq")
        silu_ready = sem("silu_ready")
        res_ready = sem("res_ready")
        sp_exp = sem("sp_exp")
        sp_one = sem("sp_one")
        sp_log = sem("sp_log")
        sp_max = sem("sp_max")
        du_ready = sem("du_ready")
        bu_made = sem("bu_made")
        decay_made = sem("decay_made")
        skip_added = sem("skip_added")
        g_ready = sem("g_ready")
        var_ready = sem("var_ready")
        rstd_ready = sem("rstd_ready")
        x1_ready = sem("x1_ready")
        diag_ready = sem("diag_ready")
        chosen_ready = sem("chosen_ready")
        onehot_ready = sem("onehot_ready")
        sel_stat = sem("sel_stat")
        sel_rstd = sem("sel_rstd")
        h_ready = sem("h_ready")
        rope_parts = sem("rope_parts")
        roped = sem("roped")
        top_ready = sem("top_ready")
        exped = sem("exped")
        rsum_ready = sem("rsum_ready")
        normed = sem("normed")
        gate_act = sem("gate_act")
        gate_exp = sem("gate_exp")
        m_ready = sem("m_ready")
        change_ready = sem("change_ready")
        out_var = sem("out_var")
        out_rstd = sem("out_rstd")
        out_ready = sem("out_ready")
        stored = [sem(f"stored{i}") for i in range(2)]

        N_CONST = 9

        block = ctx.enter_context(nc.Block())

        @block.sync
        def _(sp):
            def load_x(b):
                if b >= 2:
                    wait_filled(sp, ("xT1", b - 2))
                sp.dma_start(x_rows[b % 2], x[b].rearrange("(c p) d -> p c d", p=P)).then_inc(in_x[b % 2], 16)

            def load(name, dst, src):
                sp.dma_start(dst, src).then_inc(in_w[name], 16)

            load_x(0)
            load("w_in", w_in_s, W_in.rearrange("(k p) n -> p k n", p=P))
            load("conv", conv_raw[:], conv_w.rearrange("(k p) i t -> p k (i t)", p=P))
            row = 0
            for v, n in ((conv_b, KD), (b_dt, KD), (D, KD), (ln1_w, KD), (ln2_w, KD), (bq, N_HEADS), (bk, N_KV), (bv, N_KV)):
                load("vec", vec_rows[row:row + n, :], v.rearrange("(r p) -> r p", p=P))
                row += n
            load("w_x", w_x_s[:], W_x.rearrange("(k p) n -> p k n", p=P))
            load("w_dt", w_dt_s[:], W_dt)
            load("a", a_exp[:], A_log.rearrange("(k p) n -> p k n", p=P))
            load("freq", freq[:], inv_freq.rearrange("(o n) -> o n", o=1).partition_broadcast(P))
            load("w_out", w_out_s[:], W_out.rearrange("(k p) n -> p k n", p=P))
            load_x(1)
            load("router", router[:], w_router.rearrange("(o n) -> o n", o=1).partition_broadcast(P))
            sp.wait_ge(tables, 4)
            load("w_dn", w_dn, w_down.rearrange("(f p) n -> p f n", p=P))
            for b in range(2, B):
                load_x(b)
            wait_filled(sp, ("du1", B - 1))
            sp.wait_ge(sp_max, B)
            sp.wait_ge(du_ready, B)
            sp.wait_ge(res_ready, B)
            load("w_v", w_v, wv.rearrange("(k p) n -> p k n", p=P))
            load("w_o", w_o, wo.rearrange("(h p) n -> p h n", p=P))
            load("w_gu", w_gu[:, :, 0:FF], w_gate.rearrange("(k p) n -> p k n", p=P))
            load("w_gu", w_gu[:, :, FF:], w_up.rearrange("(k p) n -> p k n", p=P))
            wait_drained(sp, ("o1", B - 2))
            load("w_qk", w_qk[:, :, 0:N_HEADS * HEAD_DIM], wq.rearrange("(k p) n -> p k n", p=P))
            load("w_qk", w_qk[:, :, N_HEADS * HEAD_DIM:], wk.rearrange("(k p) n -> p k n", p=P))
            for b in range(B):
                sp.wait_ge(out_ready, C * (b + 1))
                sp.dma_start(out[b].rearrange("(c p) d -> p c d", p=P), out_rows[:, b % 2]).then_inc(stored[b % 2], 16)
            for i in range(2):
                sp.wait_ge(stored[i], 16 * (B // 2))

        @block.tensor
        def _(pe):
            def turn(dst, src):
                return pe.transpose(dst, src, ident[:])

            pe.wait_ge(consts, N_CONST)

            def front(b, piece):
                o = int(piece[-1]) if piece[-1].isdigit() else 0
                name = (piece, b)
                if piece in NO_FILL:
                    return
                wait_free(pe, name)
                t = at(name)
                if piece in ("xT0", "xT1"):
                    pe.wait_ge(in_x[b % 2], 16 * (b // 2 + 1))
                    for c in range(C):
                        mm = turn(t[:, c * P:(c + 1) * P], x_rows[b % 2][:, c, o * P:(o + 1) * P])
                elif piece in ("xc0", "xc1", "r0", "r1"):
                    pe.wait_ge(in_w["w_in"], 16)
                    wait_drained(pe, ("xT0", b))
                    wait_drained(pe, ("xT1", b))
                    col = (0 if piece[0] == "x" else DIN) + o * P
                    for k in range(KD):
                        mm = pe.matmul(t[:], w_in_s[:, k, col:col + P], xT[:, k, :], start=(k == 0), stop=(k == KD - 1))
                elif piece in ("cv0", "cv1"):
                    wait_drained(pe, ("xc0", b))
                    wait_drained(pe, ("xc1", b))
                    pe.wait_ge(conv_pad, 1)
                    for j in range(TAPS * KD):
                        k, i = j // KD, j % KD
                        if b == 0:
                            wait_drained(pe, ("cw", k))
                        mm = pe.matmul(t[:], conv_t[:, k, i, o * P:(o + 1) * P], xcT[:, i, k:k + L],
                                       start=(j == 0), stop=(j == TAPS * KD - 1))
                elif piece == "dt":
                    pe.wait_ge(in_w["w_x"], 16)
                    pe.wait_ge(silu_ready, b + 1)
                    for k in range(KD):
                        mm = pe.matmul(t[:], w_x_s[:, k, 0:DTR], uT[b % 2][:, k, :], start=(k == 0), stop=(k == KD - 1))
                elif piece == "bc":
                    for c in range(C):
                        for k in range(KD):
                            mm = pe.matmul(t[:, c * 2 * NST:(c + 1) * 2 * NST], uT[b % 2][:, k, c * P:(c + 1) * P],
                                           w_x_s[:, k, DTR:DTR + 2 * NST], start=(k == 0), stop=(k == KD - 1))
                elif piece in ("dl0", "dl1"):
                    pe.wait_ge(in_w["w_dt"], 16)
                    wait_drained(pe, ("dt", b))
                    mm = pe.matmul(t[:], w_dt_s[:, o * P:(o + 1) * P], dtT[:], start=True, stop=True)
                elif piece in ("du0", "du1"):
                    pe.wait_ge(du_ready, b + 1)
                    for c in range(2):
                        for k in range(KD):
                            a = c * DM + k * P
                            mm = turn(t[:, a:a + P], sp_w[:, k, (2 * o + c) * P:(2 * o + c + 1) * P])
                fill_done(name, mm)

            def tail(b, piece):
                o = int(piece[-1]) if piece[-1].isdigit() else 0
                name = (piece, b)
                if piece in NO_FILL:
                    return
                wait_free(pe, name)
                t = at(name)
                if piece in ("yt0", "yt1"):
                    wait_drained(pe, ("hT", (b + 1) * NST - 1, 0))
                    wait_drained(pe, ("hT", (b + 1) * NST - 1, 1))
                    for c in range(C):
                        mm = turn(t[:, c * P:(c + 1) * P], y_rows[:, b % 2, c, o * P:(o + 1) * P])
                elif piece in ("o0", "o1"):
                    pe.wait_ge(in_w["w_out"], 16)
                    pe.wait_ge(g_ready, KD * (b + 1))
                    pe.wait_ge(res_ready, b + 1)
                    for i in range(2):
                        cols = slice((2 * o + i) * P, (2 * o + i + 1) * P)
                        for k in range(KD):
                            mm = pe.matmul(t[:, i * DM:(i + 1) * DM], gT[:, k, cols], w_out_s[:, k, :],
                                           start=(k == 0), stop=(k == KD - 1))
                        for k in range(KD):
                            a = i * DM + k * P
                            mm = pe.matmul(t[:, a:a + P], resT[b % 2][:, k, cols], ident[:], start=False,
                                           stop=True, skip_group_check=True)
                elif piece == "sb":
                    pe.wait_ge(diag_ready, C * (b + 1))
                    mm = pe.matmul(t[:], ones[:], score_diag[:].rearrange("p c j -> p (c j)"), start=True, stop=True)
                elif piece == "pf":
                    pe.wait_ge(chosen_ready, b + 1)
                    mm = pe.matmul(t[:, 0:C], before[:], chosen[:], start=True, stop=True)
                    for w in range(1, C):
                        mm = pe.matmul(t[:, w:C], ones[:], chosen[:, 0:C - w], start=False, stop=True,
                                       skip_group_check=True)
                elif piece == "ga":
                    pe.wait_ge(onehot_ready, C * (b + 1))
                    pe.wait_ge(tables, 4)
                    r = K * (b % 2)
                    for c in range(C):
                        pick = onehot[:, b // 2, c, r:r + K]
                        mm = pe.matmul(t[r:r + K, 0:NCOL], pick, x1[:, C * b + c, :], start=(c == 0), stop=(c == C - 1))
                    for i, tab in enumerate((cos_tab, sin_tab)):
                        a = NCOL + 1 + i * K
                        for c in range(C):
                            mm = pe.matmul(t[:, a:a + K], tab[:, c, :], onehot[:, b // 2, c, r:r + K],
                                           start=(c == 0), stop=(c == C - 1), skip_group_check=True)
                fill_done(name, mm)

            def turn_bu(t, h):
                name = ("bu", t, h)
                wait_free(pe, name)
                pe.wait_ge(bu_made, C * (t + 1))
                for c in range(C):
                    mm = turn(at(name)[:, c * P:(c + 1) * P], bu_rows[:, t % 2, c, h * P:(h + 1) * P])
                fill_done(name, mm)

            def turn_state(t):
                for h in range(KD):
                    wait_drained(pe, ("bu", t, h))
                for cp in range(2):
                    name = ("hT", t, cp)
                    wait_free(pe, name)
                    for i in range(2):
                        for h in range(KD):
                            a = i * DM + h * P
                            c = 2 * cp + i
                            mm = turn(at(name)[:, a:a + P], state[:, 2 * (t % 2) + h, c * P:(c + 1) * P])
                    fill_done(name, mm)

            pe.wait_ge(in_w["vec"], 16 * 8)
            fill_done("vec", pe.transpose(at("vec")[:, 0:NVEC], vec_rows[:], ident[0:NVEC, 0:NVEC]))
            pe.wait_ge(in_w["conv"], 16)
            taps = conv_raw[:].rearrange("p o (i t) -> p o i t", t=TAPS)
            for k in range(TAPS):
                wait_free(pe, ("cw", k))
                for i in range(KD):
                    for o in range(KD):
                        a = i * DIN + o * P
                        mm = turn(at(("cw", k))[:, a:a + P], taps[:, o, i * P:(i + 1) * P, k])
                fill_done(("cw", k), mm)
            for piece in FRONT:
                front(0, piece)
            for b in range(B):
                for n in range(NST):
                    t = b * NST + n
                    for h in range(KD):
                        turn_bu(t, h)
                    if t >= 1:
                        turn_state(t - 1)
                    if b >= 1:
                        for piece in TAIL_AT.get(n, ()):
                            tail(b - 1, piece)
                    if b + 1 < B:
                        for piece in FRONT_AT.get(n, ()):
                            front(b + 1, piece)
            turn_state(T_LAST)
            for piece in TAIL:
                tail(B - 1, piece)

            def rows_to_T(name, count):
                wait_free(pe, name)
                pe.wait_ge(h_ready, count)
                for k in range(KD):
                    for p in range(ST):
                        a = k * S + p * P
                        mm = turn(at(name)[:, a:a + P], h_rows[:, p, k * P:(k + 1) * P])
                fill_done(name, mm)

            rows_to_T("h1T", ST)
            for p in range(ST):
                wait_free(pe, ("selT", p))
                for c in range(C):
                    mm = turn(at(("selT", p))[:, c * P:(c + 1) * P], onehot[:, p, c, :])
                fill_done(("selT", p), mm)
            pe.wait_ge(in_w["w_qk"], 32)
            wait_drained(pe, "h1T")
            for j in range(HQK // 2):
                wait_free(pe, ("qk", j))
                for i in range(2):
                    head = 2 * j + i
                    for k in range(KD):
                        mm = pe.matmul(at(("qk", j))[:, i * S:(i + 1) * S], w_qk[:, k, head * P:(head + 1) * P],
                                       hT[:, k, :], start=(k == 0), stop=(k == KD - 1))
                fill_done(("qk", j), mm)
            pe.wait_ge(in_w["w_v"], 16)
            for v in range(4):
                p, half = v // 2, v % 2
                wait_free(pe, ("v", v))
                for k in range(KD):
                    mm = pe.matmul(at(("v", v))[:], hT[:, k, p * P:(p + 1) * P], w_v[:, k, half * 512:(half + 1) * 512],
                                   start=(k == 0), stop=(k == KD - 1))
                fill_done(("v", v), mm)

            def scores(h):
                name = ("sc", h)
                t = at(name)
                q, k = h, N_HEADS + h // (N_HEADS // N_KV)
                wait_free(pe, name)
                pe.wait_ge(roped, k // 2 + 1)
                pe.matmul(t[:, 0:P], qkT[:, q, 0:P], qkT[:, k, 0:P], start=True, stop=False)
                pe.matmul(t[:, 0:P], ident16[:], causal[:], start=False, stop=True)
                pe.matmul(t[:, P:P + S], qkT[:, q, P:S], qkT[:, k, :], start=True, stop=True)
                mm = pe.matmul(t[:, S:S + P], ident16[:], causal[:], start=False, stop=True, skip_group_check=True)
                fill_done(name, mm)

            def turn_probs(h):
                name = ("pT", h)
                wait_free(pe, name)
                pe.wait_ge(normed, 2 * (h + 1))
                for i, a in enumerate((0, P, S)):
                    mm = turn(at(name)[:, i * P:(i + 1) * P], probs[:, h % 2, a:a + P])
                fill_done(name, mm)

            def mix(h):
                name = ("o", h)
                kv = h // (N_HEADS // N_KV)
                wait_free(pe, name)
                wait_drained(pe, ("pT", h))
                if h == 0:
                    for v in range(4):
                        wait_drained(pe, ("v", v))
                pe.matmul(at(name)[:, 0:S], v_rows[:, 0, kv * P:(kv + 1) * P], probsT[:, h % 2, 0:S], start=True, stop=True)
                mm = pe.matmul(at(name)[:, P:S], v_rows[:, 1, kv * P:(kv + 1) * P], probsT[:, h % 2, S:S + P],
                               start=False, stop=True, skip_group_check=True)
                fill_done(name, mm)

            def project(h):
                wait_drained(pe, ("o", h))
                for p in range(ST):
                    if h == 0:
                        wait_free(pe, ("wo", p))
                    mm = pe.matmul(at(("wo", p))[:, 0:DM], oT[:, h, p * P:(p + 1) * P], w_o[:, h, :],
                                   start=(h == 0), stop=(h == N_HEADS - 1))
                    if h == N_HEADS - 1:
                        fill_done(("wo", p), mm)

            pe.wait_ge(in_w["w_o"], 16)
            for i in range(N_HEADS + 3):
                if i < N_HEADS:
                    scores(i)
                if 1 <= i <= N_HEADS:
                    turn_probs(i - 1)
                if 2 <= i <= N_HEADS + 1:
                    mix(i - 2)
                if i >= 3:
                    project(i - 3)
            rows_to_T("h2T", 2 * ST)
            pe.wait_ge(in_w["w_gu"], 32)
            wait_drained(pe, "h2T")
            for f in range(FC):
                wait_free(pe, ("gu", f))
                for i in range(2):
                    col = i * FF + f * P
                    for k in range(KD):
                        mm = pe.matmul(at(("gu", f))[:, i * S:(i + 1) * S], w_gu[:, k, col:col + P], hT[:, k, :],
                                       start=(k == 0), stop=(k == KD - 1))
                fill_done(("gu", f), mm)
            pe.wait_ge(in_w["w_dn"], 16)
            for f in range(FC):
                pe.wait_ge(m_ready, f + 1)
                for p in range(ST):
                    if f == 0:
                        wait_free(pe, ("dn", p))
                    mm = pe.matmul(at(("dn", p))[:, 0:DM], mT[:, f, p * P:(p + 1) * P], w_dn[:, f, :],
                                   start=(f == 0), stop=(f == FC - 1))
                    if f == FC - 1:
                        fill_done(("dn", p), mm)
            for i in range(B * C // 2):
                b, p = 2 * i // C, 2 * i // C // 2
                r = K * (b % 2)
                name = ("put", i)
                wait_free(pe, name)
                wait_drained(pe, ("selT", p))
                pe.wait_ge(change_ready, p + 1)
                for j in range(2):
                    c = (2 * i + j) % C
                    mm = pe.matmul(at(name)[:, j * DM:(j + 1) * DM], selT[r:r + K, p, c * P:(c + 1) * P],
                                   change[r:r + K, p, :], start=True, stop=True)
                fill_done(name, mm)

        @block.scalar
        def _(act):
            seq = [0]

            def link(ins):
                seq[0] += 1
                ins.then_inc(act_seq, 1)
                act.wait_ge(act_seq, seq[0])

            def copy_out(name, dst, src=None, func=ACT.Copy, **kw):
                wait_filled(act, name)
                drain_done(name, act.activation(dst, at(name)[:] if src is None else src, func, **kw))

            def flat(ap):
                return ap.rearrange("p a b -> p (a b)")

            def front(b, piece):
                o = int(piece[-1]) if piece[-1].isdigit() else 0
                name = (piece, b)
                if piece in ("xT0", "xT1"):
                    if b >= 1:
                        act.wait_ge(res_ready, b)
                    copy_out(name, xT[:, o, :])
                elif piece in ("xc0", "xc1"):
                    copy_out(name, xcT[:, o, PAD:])
                elif piece in ("r0", "r1"):
                    copy_out(name, rT[:, o, :])
                elif piece in ("cv0", "cv1"):
                    if b == 0 and o == 0:
                        wait_drained(act, "vec")
                    if b >= 1:
                        act.wait_ge(res_ready, b)
                    copy_out(name, xsT[:, o, :], func=ACT.Identity, bias=vec[:, CB + o:CB + o + 1])
                elif piece == "silu":
                    wait_drained(act, ("cv1", b))
                    wait_drained(act, ("cv0", b))
                    wait_drained(act, ("r1", b))
                    wait_drained(act, ("r0", b))
                    if b >= 2:
                        act.wait_ge(g_ready, KD * (b - 1))
                    act.activation(silu_r[b % 2], rT, ACT.Silu)
                    act.activation(uT[b % 2], xsT, ACT.Silu).then_inc(silu_ready, 1)
                    act.preload_act_table_set("natural_log_exp_and_others")
                elif piece == "dt":
                    copy_out(name, dtT[:])
                elif piece == "bc":
                    copy_out(name, flat(bc_rows[:, b % 2]), at(name)[:, 0:C * 2 * NST])
                elif piece in ("dl0", "dl1"):
                    if b >= 1:
                        act.wait_ge(sp_max, b)
                    copy_out(name, pre[:, o, :], func=ACT.Identity, bias=vec[:, BDT + o:BDT + o + 1])
                elif piece == "sp":
                    wait_drained(act, ("dl0", b))
                    wait_drained(act, ("dl1", b))
                    if b >= 1:
                        wait_filled(act, ("du1", b - 1))
                    link(act.activation(sp_l, pre, ACT.Abs))
                    act.activation(sp_e, sp_l, ACT.Exp, scale=-1.0).then_inc(sp_exp, 1)
                    act.wait_ge(sp_one, b + 1)
                    act.wait_ge(sp_exp, b + 1)
                    act.activation(sp_l, sp_w, ACT.Ln).then_inc(sp_log, 1)
                elif piece in ("du0", "du1"):
                    copy_out(name, flat(du_rows[b % 2][:, 2 * o:2 * o + 2, :]))

            def tail(b, piece):
                name = (piece, b)
                if piece in ("o0", "o1"):
                    o = int(piece[-1])
                    if b >= 1:
                        act.wait_ge(x1_ready, b)
                    copy_out(name, flat(z[:, 2 * o:2 * o + 2, :]))
                elif piece == "ga":
                    r = K * (b % 2)
                    wait_filled(act, name)
                    act.activation(sel[r:r + K, b // 2, :], at(name)[r:r + K, 0:NCOL], ACT.Copy)
                    act.activation(cosT[:, b * K:(b + 1) * K], at(name)[:, NCOL + 1:NCOL + 1 + K], ACT.Copy)
                    drain_done(name, act.activation(sinT[:, b * K:(b + 1) * K],
                                                    at(name)[:, NCOL + 1 + K:NCOL + 1 + 2 * K], ACT.Copy))

            def make_decay(t):
                b, n = t // NST, t % NST
                for h in range(KD):
                    u = KD * t + h
                    if n == 0 and h == 0:
                        act.wait_ge(sp_max, b + 1)
                        act.wait_ge(du_ready, b + 1)
                    if u >= NDA:
                        v = u - NDA
                        wait_drained(act, ("bu", v // KD, v % KD))
                    act.activation(decay[:, u % NDA, :], delta[b % 2][:, h, :], ACT.Exp,
                                   scale=a_neg[:, h, n:n + 1]).then_inc(decay_made, 1)

            act.wait_ge(in_w["a"], 16)
            link(act.activation(a_exp[:], a_exp[:], ACT.Exp))
            act.activation(a_neg[:], a_exp[:], ACT.Copy, scale=-1.0).then_inc(a_ready, 1)
            copy_out("vec", vec[:], at("vec")[:, 0:NVEC])
            for k in range(TAPS):
                copy_out(("cw", k), flat(conv_t[:, k]))
            half = HEAD_DIM // 2
            act.wait_ge(angles, 1)
            ang = conv_raw[:, 0, 0:C * 2 * half].rearrange("p (c f) -> p c f", c=C)
            for tab, f0, sign in ((cos_tab, 0, 1.0), (sin_tab, half, -1.0)):
                act.activation(tab[:, :, 0:half], ang[:, :, f0:f0 + half], ACT.Sin, scale=sign).then_inc(tables, 1)
                act.activation(tab[:, :, half:], ang[:, :, f0:f0 + half], ACT.Sin).then_inc(tables, 1)
            for piece in FRONT:
                front(0, piece)
            act.wait_ge(a_ready, 1)
            LEAD = NDA // KD - 1
            for t in range(LEAD):
                make_decay(t)
            for b in range(B):
                for n in range(NST):
                    t = b * NST + n
                    if t + LEAD < B * NST:
                        make_decay(t + LEAD)
                    if b >= 1:
                        for piece in TAIL_AT.get(n, ()):
                            tail(b - 1, piece)
                    if b + 1 < B:
                        for piece in FRONT_AT.get(n, ()):
                            front(b + 1, piece)
            for piece in TAIL:
                tail(B - 1, piece)

            def rows_to_T(name, w):
                wait_filled(act, name)
                act.activation(hT[:, 0, :], at(name)[:, 0:S], ACT.Copy, scale=vec[:, w:w + 1])
                drain_done(name, act.activation(hT[:, 1, :], at(name)[:, S:], ACT.Copy, scale=vec[:, w + 1:w + 2]))

            rows_to_T("h1T", LN1)
            for p in range(ST):
                copy_out(("selT", p), selT[:, p, :])
            mid = HEAD_DIM // 2
            for j in range(HQK // 2):
                name = ("qk", j)
                wait_filled(act, name)
                if j >= 2:
                    act.wait_ge(roped, j - 1)
                for i in range(2):
                    w = BQ + 2 * j + i
                    src = at(name)[:, i * S:(i + 1) * S]
                    act.activation(qk_raw[:, j % 2, i, :], src, ACT.Identity, bias=vec[:, w:w + 1])
                    act.activation(qk_swap[0:mid, j % 2, i, :], src[mid:, :], ACT.Identity, bias=vec[mid:, w:w + 1])
                    last = act.activation(qk_swap[mid:, j % 2, i, :], src[0:mid, :], ACT.Identity, bias=vec[0:mid, w:w + 1])
                drain_done(name, last)
            for v in range(4):
                copy_out(("v", v), v_rows[:, v // 2, (v % 2) * 512:(v % 2 + 1) * 512])
            scale = float(HEAD_DIM) ** -0.5
            for i in range(N_HEADS + 2):
                if i < N_HEADS:
                    h = i
                    act.wait_ge(top_ready, h + 1)
                    wait_filled(act, ("sc", h))
                    if h >= 2:
                        wait_filled(act, ("pT", h - 2))
                    act.activation(probs[:, h % 2, 0:P], at(("sc", h))[:, 0:P], ACT.Exp, bias=bias[:, h, 0:1],
                                   scale=scale, accum_out=sums[:, h, 0:1])
                    drain_done(("sc", h), act.activation(probs[:, h % 2, P:], at(("sc", h))[:, P:P + S], ACT.Exp,
                                                         bias=bias[:, h, 1:2], scale=scale, accum_out=sums[:, h, 1:2]))
                if i >= 2:
                    h = i - 2
                    w = BV + h // (N_HEADS // N_KV)
                    copy_out(("o", h), oT[:, h, :], at(("o", h))[:, 0:S], func=ACT.Identity, bias=vec[:, w:w + 1])
            act.activation(gate[:, :, 0:1], sel[:, :, DM:DM + 1], ACT.Exp, scale=-1.0).then_inc(gate_exp, 1)
            rows_to_T("h2T", LN2)
            for f in range(FC):
                wait_filled(act, ("gu", f))
                if f >= 2:
                    act.wait_ge(m_ready, f - 1)
                act.activation(gate_s[:, f % 2, :], at(("gu", f))[:, 0:S], ACT.Silu).then_inc(gate_act, 1)

        @block.vector
        def _(dve):
            seq = [0]

            def link(ins):
                seq[0] += 1
                ins.then_inc(dve_seq, 1)
                dve.wait_ge(dve_seq, seq[0])

            def scan(t):
                for h in range(KD):
                    name = ("bu", t, h)
                    wait_filled(dve, name)
                    dve.wait_ge(decay_made, KD * t + h + 1)
                    if t >= 2:
                        wait_filled(dve, ("hT", t - 2, 1))
                    drain_done(name, dve.tensor_tensor_scan(
                        state[:, 2 * (t % 2) + h, :], decay[:, (KD * t + h) % NDA, :], at(name)[:], 0.0, ALU.mult, ALU.add))

            def weigh(t):
                b, n = t // NST, t % NST
                for c in range(C):
                    name = ("hT", t, c // 2)
                    src = at(name)[:, (c % 2) * DM:(c % 2 + 1) * DM]
                    y = y_rows[:, b % 2, c, :]
                    weight = bc_rows[:, b % 2, c, NST + n:NST + n + 1]
                    wait_filled(dve, name)
                    if n == 0:
                        if b >= 2:
                            wait_filled(dve, ("yt1", b - 2))
                        last = dve.tensor_scalar(y, src, weight, None, ALU.mult)
                    else:
                        wait_drained(dve, ("hT", t - 1, c // 2))
                        last = dve.scalar_tensor_tensor(out=y, in0=src, scalar=weight, in1=y, op0=ALU.mult, op1=ALU.add)
                    if c % 2:
                        drain_done(name, last)

            def front(b, piece):
                if piece == "sp":
                    dve.wait_ge(sp_log, b + 1)
                    dve.scalar_tensor_tensor(out=sp_l, in0=pre, scalar=0.0, in1=sp_l, op0=ALU.max,
                                             op1=ALU.add).then_inc(sp_max, 1)

            def tail(b, piece):
                o = int(piece[-1]) if piece[-1].isdigit() else 0
                name = (piece, b)
                if piece in ("yt0", "yt1"):
                    wait_filled(dve, name)
                    if b >= 1:
                        wait_filled(dve, ("o1", b - 1))
                    ins = dve.scalar_tensor_tensor(out=gT[:, o, :], in0=uT[b % 2][:, o, :],
                                                   scalar=vec[:, DSK + o:DSK + o + 1], in1=at(name)[:],
                                                   op0=ALU.mult, op1=ALU.add)
                    drain_done(name, ins)
                elif piece == "ln":
                    layer_norm_stats(("o0", b), ("o1", b), var_ready)
                    dve.wait_ge(rstd_ready, b + 1)
                    for c in range(C):
                        ins = dve.tensor_scalar(x1[:, C * b + c, 0:DM], z[:, c, :], mv[:, c, 0:1], rstd[:, c:c + 1],
                                                ALU.subtract, ALU.mult)
                    link(ins)
                    if b == 0:
                        dve.wait_ge(in_w["router"], 16)
                    for c in range(C):
                        ins = dve.tensor_tensor_reduce(junk[:, c % 2, (c // 2) * DM:(c // 2 + 1) * DM], x1[:, C * b + c, 0:DM],
                                                       router[:], 1.0, 0.0, ALU.mult, ALU.add, x1[:, C * b + c, DM:DM + 1])
                    ins.then_inc(x1_ready, 1)
                elif piece == "sb":
                    wait_filled(dve, name)
                    dve.wait_ge(x1_ready, b + 1)
                    for c in range(C):
                        score = x1[:, C * b + c, DM:DM + 1]
                        link(dve.tensor_scalar(junk[:, 0, :], at(name)[:], score, 0.0, ALU.is_gt, ALU.add,
                                               accum_out=ranks[:, 0, c:c + 1]))
                        ins = dve.scalar_tensor_tensor(out=junk[:, 1, :], in0=at(name)[:], scalar=score,
                                                       in1=earlier[:, c, :], op0=ALU.is_equal, op1=ALU.mult,
                                                       accum_out=ranks[:, 1, c:c + 1])
                        if c == C - 1:
                            drain_done(name, ins)
                            wait_drained(dve, name)
                        else:
                            link(ins)
                    link(dve.tensor_tensor(ranks[:, 0, :], ranks[:, 0, :], ranks[:, 1, :], ALU.add))
                    dve.tensor_scalar(chosen[:], ranks[:, 0, :], float(K), None, ALU.is_lt).then_inc(chosen_ready, 1)
                elif piece == "pf":
                    dve.wait_ge(chosen_ready, b + 1)
                    link(dve.tensor_scalar(ranks[:, 1, :], chosen[:], -1000.0, 1000.0, ALU.mult, ALU.add))
                    wait_filled(dve, name)
                    drain_done(name, dve.tensor_tensor(place[:], at(name)[:, 0:C], ranks[:, 1, :], ALU.add))
                    wait_drained(dve, name)
                    r = K * (b % 2)
                    for c in range(C):
                        dve.tensor_scalar(onehot[:, b // 2, c, r:r + K], slot_no[:], place[:, c:c + 1], None,
                                          ALU.is_equal).then_inc(onehot_ready, 1)

            def layer_norm_stats(name0, name1, signal):
                wait_drained(dve, name0)
                wait_drained(dve, name1)
                for c in range(C):
                    ins = dve.bn_stats(stats[:, c, :], z[:, c, :])
                link(ins)
                for c in range(C):
                    ins = dve.bn_aggr(mv[:, c, :], stats[:, c, :])
                ins.then_inc(signal, 1)

            half = HEAD_DIM // 2
            dve.wait_ge(consts, N_CONST)
            dve.wait_ge(in_w["freq"], 16)
            wait_filled(dve, ("cw", TAPS - 1))
            ang = conv_raw[:, 0, 0:C * 2 * half].rearrange("p (c f) -> p c f", c=C)
            turns = conv_raw[:, 1, 0:C * 2 * half].rearrange("p (c f) -> p c f", c=C)
            for c in range(C):
                for f0 in (0, half):
                    ins = dve.tensor_scalar(ang[:, c, f0:f0 + half], freq[:], token_no[:, c:c + 1], None, ALU.mult)
            link(ins)
            link(dve.tensor_scalar(turns[:, :, 0:half], ang[:, :, 0:half], 1.0 / TWO_PI, 0.25, ALU.mult, ALU.add))
            link(dve.tensor_scalar(turns[:, :, half:], ang[:, :, half:], 1.0 / TWO_PI, None, ALU.mult))
            link(dve.tensor_scalar(turns, turns, ROUND, None, ALU.add))
            link(dve.tensor_scalar(turns, turns, -ROUND, None, ALU.add))
            for part in two_pi_parts():
                link(dve.scalar_tensor_tensor(out=ang, in0=turns, scalar=-part, in1=ang, op0=ALU.mult, op1=ALU.add))
            link(dve.tensor_scalar(ang[:, :, 0:half], ang[:, :, 0:half], float(np.pi / 2), None, ALU.add))
            dve.tensor_scalar(ang, ang, -3.1415925, 3.1415925, ALU.max, ALU.min).then_inc(angles, 1)

            for piece in FRONT:
                front(0, piece)
            for b in range(B):
                for n in range(NST):
                    t = b * NST + n
                    scan(t)
                    if t >= 1:
                        weigh(t - 1)
                    if b >= 1:
                        for piece in TAIL_AT.get(n, ()):
                            tail(b - 1, piece)
                    if b + 1 < B:
                        for piece in FRONT_AT.get(n, ()):
                            front(b + 1, piece)
            weigh(T_LAST)
            for piece in TAIL:
                tail(B - 1, piece)

            def rms(count, src):
                for p in range(ST):
                    ins = dve.tensor_tensor_reduce(junk[:, 0, p * DM:(p + 1) * DM], src[p], src[p], 1.0, 0.0, ALU.mult,
                                                   ALU.add, ss[:, p:p + 1])
                ins.then_inc(sel_stat, 1)
                dve.wait_ge(sel_rstd, count)
                for p in range(ST):
                    dve.tensor_scalar(h_rows[:, p, :], src[p], rrms[:, p:p + 1], None, ALU.mult).then_inc(h_ready, 1)

            for b in range(B):
                wait_drained(dve, ("ga", b))
            rms(1, [sel[:, p, 0:DM] for p in range(ST)])
            for j in range(HQK // 2):
                wait_drained(dve, ("qk", j))
                if j >= 2:
                    dve.wait_ge(roped, j - 1)
                for src, tab in ((qk_raw, cosT), (qk_swap, sinT)):
                    part = src[:, j % 2]
                    dve.tensor_tensor(part, part, tab[:].unsqueeze(1).to_broadcast([P, 2, S]), ALU.mult)\
                       .then_inc(rope_parts, 1)
            scale = float(HEAD_DIM) ** -0.5
            for i in range(N_HEADS + 1):
                if i < N_HEADS:
                    h = i
                    wait_filled(dve, ("sc", h))
                    dve.tensor_reduce(top[:, h, 0:1], at(("sc", h))[:, 0:P], AX.X, ALU.max)
                    link(dve.tensor_reduce(top[:, h, 1:2], at(("sc", h))[:, P:P + S], AX.X, ALU.max))
                    dve.tensor_scalar(bias[:, h, :], top[:, h, :], -scale, None, ALU.mult).then_inc(top_ready, 1)
                if i >= 1:
                    h = i - 1
                    wait_drained(dve, ("sc", h))
                    dve.reciprocal(rsum[:, h, :], sums[:, h, :]).then_inc(rsum_ready, 1)
                    wait_filled(dve, ("pT", h))
                    if h >= 2:
                        wait_filled(dve, ("o", h - 2))
                    drain_done(("pT", h), dve.tensor_copy(probsT[:, h % 2, :], at(("pT", h))[:, 0:3 * P]))
            for p in range(ST):
                wait_filled(dve, ("wo", p))
                drain_done(("wo", p), dve.tensor_tensor(x_att[:, p, :], at(("wo", p))[:, 0:DM], sel[:, p, 0:DM], ALU.add))
            for p in range(ST):
                wait_drained(dve, ("wo", p))
            wait_filled(dve, "h1T")
            rms(2, [x_att[:, p, :] for p in range(ST)])
            dve.wait_ge(gate_exp, 1)
            link(dve.tensor_scalar(gate[:, :, 0:1], gate[:, :, 0:1], 1.0, None, ALU.add))
            link(dve.reciprocal(gate[:, :, 1:2], gate[:, :, 0:1]))
            for f in range(FC):
                dve.wait_ge(gate_act, f + 1)
                wait_filled(dve, ("gu", f))
                ins = dve.tensor_tensor(mT[:, f, :], gate_s[:, f % 2, :], at(("gu", f))[:, S:], ALU.mult)
                drain_done(("gu", f), ins)
                wait_drained(dve, ("gu", f))
                dve.sem_inc(m_ready, 1)
            for p in range(ST):
                wait_filled(dve, ("dn", p))
                drain_done(("dn", p), dve.tensor_tensor(x_att[:, p, :], at(("dn", p))[:, 0:DM], x_att[:, p, :], ALU.add))
                wait_drained(dve, ("dn", p))
                link(dve.tensor_tensor(x_att[:, p, :], x_att[:, p, :], sel[:, p, 0:DM], ALU.subtract))
                dve.tensor_scalar(change[:, p, :], x_att[:, p, :], gate[:, p, 1:2], None, ALU.mult)\
                   .then_inc(change_ready, 1)
            for b in range(B):
                if b >= 1:
                    dve.wait_ge(out_ready, C * b)
                for j in range(2):
                    i = 2 * b + j
                    wait_filled(dve, ("put", i))
                    src = at(("put", i))[:].rearrange("p (c d) -> p c d", c=2)
                    drain_done(("put", i), dve.scalar_tensor_tensor(
                        out=z[:, 2 * j:2 * j + 2, :], in0=x1[:, 2 * i:2 * i + 2, 0:DM], scalar=2.0, in1=src,
                        op0=ALU.mult, op1=ALU.add))
                layer_norm_stats(("put", 2 * b), ("put", 2 * b + 1), out_var)
                dve.wait_ge(out_rstd, b + 1)
                if b >= 2:
                    dve.wait_ge(stored[b % 2], 16 * (b // 2))
                for c in range(C):
                    dve.tensor_scalar(out_rows[:, b % 2, c, :], z[:, c, :], mv[:, c, 0:1], rstd[:, c:c + 1],
                                      ALU.subtract, ALU.mult).then_inc(out_ready, 1)

        @block.gpsimd
        def _(pool):
            seq = [0]

            def link(ins):
                seq[0] += 1
                ins.then_inc(pool_seq, 1)
                pool.wait_ge(pool_seq, seq[0])

            def const(ins):
                ins.then_inc(consts, 1)

            link(pool.memset(ones[:], 1.0))
            const(pool.affine_select(ident[:], ones[:], [[-1, P]], ALU.is_equal, 0.0, base=0, channel_multiplier=1))
            const(pool.affine_select(before[:], ones[:], [[1, P]], ALU.is_gt, 0.0, base=0, channel_multiplier=-1))
            const(pool.affine_select(ident16[:], ones[:], [[-1, P]], ALU.is_equal, 0.0, base=0, channel_multiplier=1))
            link(pool.memset(causal[:], 0.0))
            const(pool.affine_select(causal[:], causal[:], [[-1, P]], ALU.is_ge, NEG, base=0, channel_multiplier=1))
            link(pool.memset(earlier[:], 1.0))
            for c in range(C):
                ins = pool.affine_select(earlier[:, c, :], earlier[:, c, :], [[-1, L]], ALU.is_gt, 0.0, base=P * c,
                                         channel_multiplier=1)
            const(ins)
            const(pool.iota(slot_no[:], [[1, K]], base=0, channel_multiplier=0, allow_small_or_imprecise_dtypes=True))
            const(pool.iota(token_no[:], [[P, C]], base=0, channel_multiplier=1, allow_small_or_imprecise_dtypes=True))
            const(pool.memset(half_pow[:], -0.5))
            const(pool.memset(sums[:], 0.0))
            pool.memset(xcT[:, :, 0:PAD], 0.0).then_inc(conv_pad, 1)

            def front(b, piece):
                if piece == "silu":
                    for name in ("xT0", "xT1", "cv0", "cv1"):
                        wait_drained(pool, (name, b))
                    if b >= 2:
                        wait_filled(pool, ("o1", b - 2))
                    pool.tensor_tensor(resT[b % 2], xT, xsT, ALU.add).then_inc(res_ready, 1)
                elif piece == "sp":
                    pool.wait_ge(sp_exp, b + 1)
                    if b >= 1:
                        wait_filled(pool, ("du1", b - 1))
                    pool.tensor_scalar(sp_w, sp_e, 1.0, 1.0, ALU.add, ALU.mult).then_inc(sp_one, 1)
                    pool.wait_ge(sp_log, b + 1)
                    link(pool.tensor_scalar(sp_w, sp_w, -1.0, 1.0, ALU.add, ALU.mult))
                    link(pool.tensor_tensor(sp_e, sp_e, sp_w, ALU.subtract))
                    pool.wait_ge(sp_max, b + 1)
                    link(pool.tensor_tensor(delta[b % 2], sp_l, sp_e, ALU.add))
                    pool.wait_ge(silu_ready, b + 1)
                    pool.tensor_tensor(sp_w, delta[b % 2], uT[b % 2], ALU.mult).then_inc(du_ready, 1)

            def make_bu(t):
                b, n = t // NST, t % NST
                if n == 0:
                    wait_drained(pool, ("bc", b))
                    wait_drained(pool, ("du0", b))
                    wait_drained(pool, ("du1", b))
                if t >= 2:
                    for h in range(KD):
                        wait_filled(pool, ("bu", t - 2, h))
                for c in range(C):
                    pool.tensor_scalar(bu_rows[:, t % 2, c, :], du_rows[b % 2][:, c, :], bc_rows[:, b % 2, c, n:n + 1],
                                       1.0, ALU.mult, ALU.mult).then_inc(bu_made, 1)

            def inv_sqrt(dst, var, eps, scale=1.0):
                link(pool.tensor_scalar(dst, var, scale, eps, ALU.mult, ALU.add))
                return pool.tensor_tensor(dst, dst, half_pow[:, 0:dst.shape[1]], ALU.pow)

            def tail(b, piece):
                if piece in ("yt0", "yt1"):
                    o = int(piece[-1])
                    wait_drained(pool, (piece, b))
                    pool.wait_ge(silu_ready, b + 1)
                    pool.tensor_tensor(gT[:, o, :], gT[:, o, :], silu_r[b % 2][:, o, :], ALU.mult).then_inc(g_ready, 1)
                elif piece == "ln":
                    pool.wait_ge(var_ready, b + 1)
                    inv_sqrt(rstd[:], mv[:, :, 1:2].rearrange("p c o -> p (c o)"), LN_EPS).then_inc(rstd_ready, 1)
                    pool.wait_ge(x1_ready, b + 1)
                    if b >= 1:
                        wait_filled(pool, ("sb", b - 1))
                    for c in range(C):
                        pool.tensor_scalar(score_diag[:, c, :], ident[:], x1[:, C * b + c, DM:DM + 1], 1.0,
                                           ALU.mult, ALU.mult).then_inc(diag_ready, 1)

            for piece in FRONT:
                front(0, piece)
            make_bu(0)
            for b in range(B):
                for n in range(NST):
                    t = b * NST + n
                    if b >= 1:
                        for piece in TAIL_AT.get(n, ()):
                            tail(b - 1, piece)
                    if b + 1 < B:
                        for piece in FRONT_AT.get(n, ()):
                            front(b + 1, piece)
                    if t < T_LAST:
                        make_bu(t + 1)
            for piece in TAIL:
                tail(B - 1, piece)

            def rms(count):
                pool.wait_ge(sel_stat, count)
                inv_sqrt(rrms[:], ss[:], RMS_EPS, 1.0 / DM).then_inc(sel_rstd, 1)

            rms(1)
            for j in range(HQK // 2):
                pool.wait_ge(rope_parts, 2 * (j + 1))
                pool.tensor_tensor(qkT[:, 2 * j:2 * j + 2, :], qk_raw[:, j % 2], qk_swap[:, j % 2], ALU.add).then_inc(roped, 1)
            for h in range(N_HEADS):
                pool.wait_ge(rsum_ready, h + 1)
                pool.tensor_scalar(probs[:, h % 2, 0:P], probs[:, h % 2, 0:P], rsum[:, h, 0:1], 1.0, ALU.mult,
                                   ALU.mult).then_inc(normed, 1)
                pool.tensor_scalar(probs[:, h % 2, P:], probs[:, h % 2, P:], rsum[:, h, 1:2], 1.0, ALU.mult,
                                   ALU.mult).then_inc(normed, 1)
            rms(2)
            for b in range(B):
                pool.wait_ge(out_var, b + 1)
                inv_sqrt(rstd[:], mv[:, :, 1:2].rearrange("p c o -> p (c o)"), LN_EPS).then_inc(out_rstd, 1)


_OUTS = [((4, 512, 256), "float32")]


def kernel(**inputs):
    import concourse.bacc as _bacc
    from concourse.bass_utils import run_bass_kernel_spmd as _run

    nc = _bacc.Bacc("TRN2", target_bir_lowering=False, num_devices=1)
    order = ["L0_attn_" + n for n in ("x", "W_in", "conv_w", "conv_b", "W_x", "W_dt", "b_dt", "A_log", "D", "W_out")]
    order += ["L0_ffn_" + n for n in ("w_router", "wq", "bq", "wk", "bk", "wv", "bv", "wo", "w_gate", "w_up", "w_down",
                                      "ln1_w", "ln2_w")]
    arrays, args = {}, []
    for name in order:
        a = np.ascontiguousarray(inputs[name])
        arrays[f"in_{name}"] = a
        args.append(nc.dram_tensor(f"in_{name}", a.shape, mybir.dt.from_np(a.dtype), kind="ExternalInput").ap())
    freq = (1.0 / ROPE_THETA ** (np.arange(0, HEAD_DIM, 2, dtype=np.float32) / HEAD_DIM)).astype(np.float32)
    arrays["in_inv_freq"] = freq
    args.append(nc.dram_tensor("in_inv_freq", freq.shape, F32, kind="ExternalInput").ap())
    shape, dtype = _OUTS[0]
    args.append(nc.dram_tensor("out_0", shape, mybir.dt.from_np(np.dtype(dtype)), kind="ExternalOutput").ap())
    block_kernel(nc, *args)
    r = _run(nc, [arrays], core_ids=[0])
    return r.results[0]["out_0"]
```

```python
from contextlib import ExitStack

import numpy as np

import concourse.bass as bass
from concourse import mybir

F32 = mybir.dt.float32
BF16 = mybir.dt.bfloat16
ALU = mybir.AluOpType
ACT = mybir.ActivationFunctionType
AX = mybir.AxisListType

P = 128
HEAD_DIM = 128
N_HEADS = 16
N_KV = 8
CAPACITY = 0.125
ROPE_THETA = 10000.0
LN_EPS = 1e-5
RMS_EPS = 1e-6
ROUND = 1.5 * 2.0**23
TWO_PI = 2.0 * np.pi
LAG_TURN, LAG_MIX, LAG_OUT = 2, 3, 4
NEG = -1.0e38

FRONT_AT = {0: ("xT0", "xT1"), 1: ("cv0a", "cv0b"), 2: ("cv0c", "cv0d"), 3: ("cv1a", "cv1b"), 4: ("cv1c", "cv1d"),
            5: ("su",), 6: ("dt", "bc"), 7: ("cr", "dl0", "dl1"), 8: ("s1",), 9: ("s2", "r0"), 10: ("s3", "r1"),
            11: ("s4", "sr"), 12: ("s5",), 13: ("s6",), 14: ("rs",)}
FRONT = [x for n in sorted(FRONT_AT) for x in FRONT_AT[n]]
TAIL_AT = {1: ("yt0", "yt1"), 4: ("o0",), 6: ("o1",), 7: ("ln",), 10: ("sb",), 12: ("pf",), 13: ("ga", "cs")}
TAIL = [x for n in sorted(TAIL_AT) for x in TAIL_AT[n]]
NO_FILL = ("su", "sr", "s1", "s2", "s3", "s4", "s5", "s6", "rs", "ln")


class Fills:

    def __init__(self):
        self.at = {}
        self.uses = [0] * 8

    def add(self, name, bank):
        self.at[name] = (bank, self.uses[bank])
        self.uses[bank] += 1


def two_pi_parts():
    a = float(np.float32(np.round(TWO_PI * 2**8) / 2**8))
    b = float(np.float32(np.round((TWO_PI - a) * 2**20) / 2**20))
    return a, b, float(np.float32(TWO_PI - a - b))


def block_kernel(nc, x, W_in, conv_w, conv_b, W_x, W_dt, b_dt, A_log, D, W_out, w_router, wq, bq, wk, bk, wv, bv,
                 wo, w_gate, w_up, w_down, ln1_w, ln2_w, inv_freq, out):
    B, L, DM = x.shape
    DIN, NST = A_log.shape
    TAPS = conv_w.shape[2]
    DTR = W_dt.shape[0]
    FF = w_gate.shape[1]
    C = L // P
    KD = DM // P
    K = max(1, int(L * CAPACITY))
    S = B * K
    ST = S // P
    PAD = TAPS - 1
    NCOL = DM + 1
    HQK = N_HEADS + N_KV
    FC = FF // P
    assert DIN == DM and C == 4 and KD == 2 and DTR == P and K == 64 and ST == 2

    fills = Fills()
    rest = [0]

    def add_rest(name):
        fills.add(name, 6 + rest[0] % 2)
        rest[0] += 1

    def add_pieces(b, pieces):
        for piece in pieces:
            if piece == "cs" and b % 2 == 0:
                continue
            if piece[:2] == "cv":
                if piece[-1] == "a":
                    fills.add((piece[:3], b), 1)
            elif piece not in NO_FILL:
                add_rest((piece, b))

    add_rest("vec")
    for k in range(TAPS):
        add_rest(("cw", k))
    add_rest("wT")
    for i in range(4):
        add_rest(("vc", i))
    add_pieces(0, FRONT)
    for t in range(2):
        fills.add(("bb", t), 0)
    for b in range(B):
        for n in range(NST):
            t = b * NST + n
            if t + 2 < B * NST:
                fills.add(("bb", t + 2), 0)
            if t >= 1:
                for cp in range(2):
                    fills.add(("hT", t - 1, cp), 2 + 2 * ((t - 1) % 2) + cp)
            if b >= 1:
                add_pieces(b - 1, TAIL_AT.get(n, ()))
            if b + 1 < B:
                add_pieces(b + 1, FRONT_AT.get(n, ()))
    T_LAST = B * NST - 1
    for cp in range(2):
        fills.add(("hT", T_LAST, cp), 2 + 2 * (T_LAST % 2) + cp)
    add_pieces(B - 1, TAIL)
    fills.add("h1T", 0)
    for p in range(ST):
        fills.add(("selT", p), 1 + p)
    for j in range(HQK // 2):
        fills.add(("qk", j), 3 + j % 3)
    for v in range(4):
        fills.add(("v", v), 6 + v % 2)
    for i in range(N_HEADS + LAG_OUT):
        if i < N_HEADS:
            fills.add(("sc", i), i % 3)
        if 0 <= i - LAG_TURN < N_HEADS:
            fills.add(("pT", i - LAG_TURN), 3 + (i - LAG_TURN) % 2)
        if 0 <= i - LAG_MIX < N_HEADS:
            fills.add(("o", i - LAG_MIX), 5)
    for p in range(ST):
        fills.add(("wo", p), 6 + p)
    fills.add("h2T", 0)
    for f in range(FC):
        fills.add(("gu", f), 1 + f % 4)
    for p in range(ST):
        fills.add(("dn", p), 6 + p)
    for i in range(B * C // 2):
        fills.add(("put", i), i % 6)

    with ExitStack() as ctx:
        def sb(name, shape, dt=F32):
            return ctx.enter_context(nc.sbuf_tensor(name, shape, dt))

        def sem(name):
            return ctx.enter_context(nc.semaphore(name))

        bank = [ctx.enter_context(nc.psum_tensor(f"bank{i}", [P, 512], F32)) for i in range(8)]
        filled = [sem(f"filled{i}") for i in range(8)]
        drained = [sem(f"drained{i}") for i in range(8)]

        def at(name):
            return bank[fills.at[name][0]]

        def wait_free(pe, name):
            i, k = fills.at[name]
            if k:
                pe.wait_ge(drained[i], k)

        def fill_done(name, ins):
            ins.then_inc(filled[fills.at[name][0]], 1)

        def wait_filled(eng, name):
            i, k = fills.at[name]
            eng.wait_ge(filled[i], k + 1)

        def drain_done(name, ins):
            ins.then_inc(drained[fills.at[name][0]], 1)

        def wait_drained(eng, name):
            i, k = fills.at[name]
            eng.wait_ge(drained[i], k + 1)

        ident = sb("ident", [P, P])
        ident16 = sb("ident16", [P, P], BF16)
        ones = sb("ones", [P, P])
        before = sb("before", [P, P])
        EARLIER = C * L // 2
        earlier_words = sb("earlier_words", [P, EARLIER])
        earlier = earlier_words[:].bitcast(BF16).rearrange("p (c j) -> p c j", c=C)
        causal = sb("causal", [P, P], BF16)
        slot_no = sb("slot_no", [P, K])
        token_no = sb("token_no", [P, C])
        half_pow = sb("half_pow", [P, C])
        def parts(name, shapes):
            whole = sb(name, [P, sum(int(np.prod(s)) for s in shapes)])
            cut, a = [], 0
            for s in shapes:
                n = int(np.prod(s))
                ap = whole[:, a:a + n]
                if len(s) == 2:
                    ap = ap.rearrange("p (a b) -> p a b", a=s[0])
                elif len(s) == 3:
                    ap = ap.rearrange("p (a b c) -> p a b c", a=s[0], b=s[1])
                cut.append(ap)
                a += n
            return whole, cut

        conv_raw = sb("conv_raw", [P, KD, DIN * TAPS])
        front_a, (conv_t, w_in_s, w_inT, _) = parts("front_a", [(TAPS, KD, DIN), (KD, 2 * DIN), (KD, DM), (KD, DM)])
        conv_x = conv_raw[:].rearrange("p a b -> p (a b)").rearrange("p (t k o) -> p t k o", t=TAPS, k=KD)
        front_b, (rT, pre, sp_e, sp_l, xsT) = parts("front_b", [(KD, L)] * 5)
        front_c, (xT, sp_w) = parts("front_c", [(KD, PAD + L), (KD, L)])
        w_x_s = sb("w_x_s", [P, KD, DTR + 2 * NST])
        w_dt_s = sb("w_dt_s", [P, DIN])
        w_out_s = sb("w_out_s", [P, KD, DM])
        NVEC = 5 * KD + N_HEADS + 2 * N_KV
        vec_rows = sb("vec_rows", [NVEC, P])
        vec = sb("vec", [P, NVEC])
        CB, BDT, DSK, LN1, LN2 = (i * KD for i in range(5))
        BQ = 5 * KD
        BV = BQ + HQK
        a_neg = sb("a_neg", [P, KD, NST])
        a_exp = sb("a_exp", [P, KD, NST])
        router = sb("router", [P, DM])
        freq = sb("freq", [P, HEAD_DIM // 2])
        cos_tab = sb("cos_tab", [P, C, HEAD_DIM])
        sin_tab = sb("sin_tab", [P, C, HEAD_DIM])
        copies = [parts(f"copy{i}", [(KD, L)] * 5 + [(C, DM)]) for i in range(2)]
        silu_r, uT, resT, delta, duT, x_rows = ([copies[i][1][j] for i in range(2)] for j in range(6))
        dtT = sb("dtT", [P, L])
        bc_rows = sb("bc_rows", [P, 2, C, 2 * NST])
        NDA = 6
        scan_in = sb("scan_in", [P, NDA * L + 2 * KD * L + 2 * L])
        decay = scan_in[:, 0:NDA * L].rearrange("p (s l) -> p s l", s=NDA)
        bu = scan_in[:, NDA * L:(NDA + 2 * KD) * L].rearrange("p (s k l) -> p s k l", s=2, k=KD)
        PIECE = 32
        NPIECE = 2 * PIECE + NST
        pieces = sb("pieces", [NPIECE, 2, L], BF16)
        spread = sb("spread", [NPIECE, NST, P], BF16)
        bcT = sb("bcT", [2 * NST, L])
        rest1 = sb("rest1", [NST, L])
        mid16 = sb("mid16", [NST, L], BF16)
        b_wide = scan_in[:, (NDA + 2 * KD) * L:].rearrange("p (s l) -> p s l", s=2)
        state_buf = sb("state", [P, 4 * L])
        state = state_buf[:].rearrange("p (s l) -> p s l", s=4)
        y_buf = sb("y", [P, 2 * C * DM])
        y_rows = y_buf[:].rearrange("p (s c d) -> p s c d", s=2, c=C)
        gT_buf = sb("gT", [P, KD * L])
        gT = gT_buf[:].rearrange("p (k l) -> p k l", k=KD)
        z = sb("z", [P, C, DM])
        stats = sb("stats", [P, C, 6])
        mv = sb("mv", [P, C, 2])
        rstd = sb("rstd", [P, C])
        x1 = sb("x1", [P, B * C, NCOL])
        junk = sb("junk", [P, 2, L], BF16)
        score_diag = sb("score_diag", [P, C, P])
        ranks = sb("ranks", [P, 2, C])
        chosen = sb("chosen", [P, C])
        place = sb("place", [P, C])
        onehot = sb("onehot", [P, B // 2, C, 2 * K])
        sel = sb("sel", [P, ST, NCOL])
        cosT = sb("cosT", [P, S])
        sinT = sb("sinT", [P, S])
        ss = sb("ss", [P, ST])
        rrms = sb("rrms", [P, ST])
        top = sb("top", [P, N_HEADS, 2])
        bias = sb("bias", [P, N_HEADS, 2])
        sums = sb("sums", [P, N_HEADS, 2])
        rsum = sb("rsum", [P, N_HEADS, 2])
        gate = sb("gate", [P, ST, 2])
        w_dn = conv_raw[:].rearrange("p a b -> p (a b)").rearrange("p (f n) -> p f n", f=FC)
        w_gu = front_a[:].rearrange("p (k n) -> p k n", k=KD)
        w_o = front_b[:, 0:N_HEADS * DM].rearrange("p (h n) -> p h n", h=N_HEADS)
        w_v = front_c[:, 0:KD * N_KV * HEAD_DIM].rearrange("p (k n) -> p k n", k=KD)
        w_qk = copies[0][0][:].rearrange("p (k n) -> p k n", k=KD)
        qkT = scan_in[:].rearrange("p (h s) -> p h s", h=HQK)
        mT = scan_in[:, 0:FC * S].rearrange("p (f s) -> p f s", f=FC)
        oT = copies[1][0][:, 0:N_HEADS * S].rearrange("p (h s) -> p h s", h=N_HEADS)
        v_rows = copies[1][0][:, N_HEADS * S:].rearrange("p (t n) -> p t n", t=ST)
        qk_raw = state_buf[:, 0:4 * S].rearrange("p (a b s) -> p a b s", a=2, b=2)
        qk_swap = state_buf[:, 4 * S:].rearrange("p (a b s) -> p a b s", a=2, b=2)
        probs = y_buf[:, 0:9 * P].rearrange("p (a s) -> p a s", a=3)
        probsT = y_buf[:, 9 * P:15 * P].rearrange("p (a s) -> p a s", a=2)
        x_att = state_buf[:, 0:ST * DM].rearrange("p (t d) -> p t d", t=ST)
        gate_s = state_buf[:, ST * DM:ST * DM + 2 * S].rearrange("p (a s) -> p a s", a=2)
        out_rows = y_rows
        selT = gT_buf[:].rearrange("p (t l) -> p t l", t=ST)
        change = score_diag[:].rearrange("p a b -> p (a b)").rearrange("p (t d) -> p t d", t=ST)
        h_rows = earlier_words[:, 0:ST * DM].rearrange("p (t d) -> p t d", t=ST)
        hT = earlier_words[:, ST * DM:].rearrange("p (k s) -> p k s", k=KD)

        in_x = [sem(f"in_x{i}") for i in range(2)]
        in_w = {n: sem(f"in_{n}") for n in ("w_in", "conv", "vec", "w_x", "w_dt", "w_out", "a", "router", "freq",
                                            "w_qk", "w_v", "w_o", "w_gu", "w_dn")}
        consts = sem("consts")
        conv_pad = sem("conv_pad")
        a_ready = sem("a_ready")
        tables = sem("tables")
        angles = sem("angles")
        dve_seq = sem("dve_seq")
        act_seq = sem("act_seq")
        pool_seq = sem("pool_seq")
        u_ready = sem("u_ready")
        silu_ready = sem("silu_ready")
        res_ready = sem("res_ready")
        sp_exp = sem("sp_exp")
        sp_one = sem("sp_one")
        sp_log = sem("sp_log")
        sp_max = sem("sp_max")
        du_ready = sem("du_ready")
        bu_made = sem("bu_made")
        scanned = sem("scanned")
        pieces_clear = sem("pieces_clear")
        top16 = sem("top16")
        rest_made = sem("rest_made")
        mid_made = sem("mid_made")
        low16 = sem("low16")
        decay_made = sem("decay_made")
        skip_added = sem("skip_added")
        g_ready = sem("g_ready")
        var_ready = sem("var_ready")
        rstd_ready = sem("rstd_ready")
        x1_ready = sem("x1_ready")
        diag_ready = sem("diag_ready")
        chosen_ready = sem("chosen_ready")
        onehot_ready = sem("onehot_ready")
        sel_stat = sem("sel_stat")
        sel_rstd = sem("sel_rstd")
        h_ready = sem("h_ready")
        rope_parts = sem("rope_parts")
        roped = sem("roped")
        top_ready = sem("top_ready")
        exped = sem("exped")
        rsum_ready = sem("rsum_ready")
        normed = sem("normed")
        gate_act = sem("gate_act")
        gate_exp = sem("gate_exp")
        m_ready = sem("m_ready")
        change_ready = sem("change_ready")
        out_var = sem("out_var")
        out_rstd = sem("out_rstd")
        out_ready = sem("out_ready")
        stored = [sem(f"stored{i}") for i in range(2)]

        N_CONST = 9

        block = ctx.enter_context(nc.Block())

        @block.sync
        def _(sp):
            def load_x(b):
                if b >= 2:
                    wait_filled(sp, ("xT1", b - 2))
                sp.dma_start(x_rows[b % 2], x[b].rearrange("(c p) d -> p c d", p=P)).then_inc(in_x[b % 2], 16)

            def load(name, dst, src):
                sp.dma_start(dst, src).then_inc(in_w[name], 16)

            load_x(0)
            load("w_in", w_in_s, W_in.rearrange("(k p) n -> p k n", p=P))
            load("conv", conv_raw[:], conv_w.rearrange("(k p) i t -> p k (i t)", p=P))
            row = 0
            for v, n in ((conv_b, KD), (b_dt, KD), (D, KD), (ln1_w, KD), (ln2_w, KD), (bq, N_HEADS), (bk, N_KV), (bv, N_KV)):
                load("vec", vec_rows[row:row + n, :], v.rearrange("(r p) -> r p", p=P))
                row += n
            load("w_x", w_x_s[:], W_x.rearrange("(k p) n -> p k n", p=P))
            load("w_dt", w_dt_s[:], W_dt)
            load("a", a_exp[:], A_log.rearrange("(k p) n -> p k n", p=P))
            load("freq", freq[:], inv_freq.rearrange("(o n) -> o n", o=1).partition_broadcast(P))
            load("w_out", w_out_s[:], W_out.rearrange("(k p) n -> p k n", p=P))
            load_x(1)
            load("router", router[:], w_router.rearrange("(o n) -> o n", o=1).partition_broadcast(P))
            for b in range(2, B):
                load_x(b)
            wait_filled(sp, ("r1", B - 1))
            wait_filled(sp, ("dl1", B - 1))
            sp.wait_ge(silu_ready, B)
            sp.wait_ge(sp_max, B)
            sp.wait_ge(du_ready, B)
            sp.wait_ge(res_ready, B)
            load("w_v", w_v, wv.rearrange("(k p) n -> p k n", p=P))
            load("w_o", w_o, wo.rearrange("(h p) n -> p h n", p=P))
            load("w_gu", w_gu[:, :, 0:FF], w_gate.rearrange("(k p) n -> p k n", p=P))
            load("w_gu", w_gu[:, :, FF:], w_up.rearrange("(k p) n -> p k n", p=P))
            load("w_dn", w_dn, w_down.rearrange("(f p) n -> p f n", p=P))
            wait_drained(sp, ("o1", B - 2))
            load("w_qk", w_qk[:, :, 0:N_HEADS * HEAD_DIM], wq.rearrange("(k p) n -> p k n", p=P))
            load("w_qk", w_qk[:, :, N_HEADS * HEAD_DIM:], wk.rearrange("(k p) n -> p k n", p=P))
            for b in range(B):
                sp.wait_ge(out_ready, C * (b + 1))
                sp.dma_start(out[b].rearrange("(c p) d -> p c d", p=P), out_rows[:, b % 2]).then_inc(stored[b % 2], 16)
            for i in range(2):
                sp.wait_ge(stored[i], 16 * (B // 2))

        @block.tensor
        def _(pe):
            def turn(dst, src):
                return pe.transpose(dst, src, ident[:])

            pe.wait_ge(consts, N_CONST)

            def convolve(b, o, quarter):
                name = (f"cv{o}", b)
                if quarter == 0:
                    wait_free(pe, name)
                    wait_drained(pe, ("xT0", b))
                    wait_drained(pe, ("xT1", b))
                    pe.wait_ge(conv_pad, 1)
                for j in range(2 * quarter, 2 * quarter + 2):
                    k, i = j // KD, j % KD
                    if b == 0:
                        wait_drained(pe, ("vc", 2 * i + k // 2))
                    mm = pe.matmul(at(name)[:], conv_x[:, k, i, o * P:(o + 1) * P], xT[:, i, k:k + L],
                                   start=(j == 0), stop=(j == TAPS * KD - 1))
                if quarter == 3:
                    fill_done(name, mm)

            def front(b, piece):
                o = int(piece[-1]) if piece[-1].isdigit() else 0
                name = (piece, b)
                if piece in NO_FILL:
                    return
                if piece[:2] == "cv":
                    return convolve(b, int(piece[2]), "abcd".index(piece[3]))
                wait_free(pe, name)
                t = at(name)
                if piece in ("xT0", "xT1"):
                    pe.wait_ge(in_x[b % 2], 16 * (b // 2 + 1))
                    for c in range(C):
                        mm = turn(t[:, c * P:(c + 1) * P], x_rows[b % 2][:, c, o * P:(o + 1) * P])
                elif piece in ("r0", "r1"):
                    for k in range(KD):
                        mm = pe.matmul(t[:], w_in_s[:, k, DIN + o * P:DIN + (o + 1) * P], xT[:, k, PAD:],
                                       start=(k == 0), stop=(k == KD - 1))
                elif piece == "dt":
                    pe.wait_ge(in_w["w_x"], 16)
                    pe.wait_ge(u_ready, b + 1)
                    for k in range(KD):
                        mm = pe.matmul(t[:], w_x_s[:, k, 0:DTR], uT[b % 2][:, k, :], start=(k == 0), stop=(k == KD - 1))
                elif piece == "bc":
                    for k in range(KD):
                        mm = pe.matmul(t[0:2 * NST, :], w_x_s[:, k, DTR:DTR + 2 * NST], uT[b % 2][:, k, :],
                                       start=(k == 0), stop=(k == KD - 1))
                elif piece == "cr":
                    wait_drained(pe, ("bc", b))
                    for c in range(C):
                        mm = pe.transpose(t[:, c * 2 * NST:(c + 1) * 2 * NST], bcT[:, c * P:(c + 1) * P],
                                          ident[0:2 * NST, 0:2 * NST])
                elif piece in ("dl0", "dl1"):
                    pe.wait_ge(in_w["w_dt"], 16)
                    wait_drained(pe, ("dt", b))
                    mm = pe.matmul(t[:], w_dt_s[:, o * P:(o + 1) * P], dtT[:], start=True, stop=True)
                fill_done(name, mm)

            def tail(b, piece):
                o = int(piece[-1]) if piece[-1].isdigit() else 0
                name = (piece, b)
                if piece in NO_FILL or (piece == "cs" and b % 2 == 0):
                    return
                wait_free(pe, name)
                t = at(name)
                if piece in ("yt0", "yt1"):
                    wait_drained(pe, ("hT", (b + 1) * NST - 1, 0))
                    wait_drained(pe, ("hT", (b + 1) * NST - 1, 1))
                    for c in range(C):
                        mm = turn(t[:, c * P:(c + 1) * P], y_rows[:, b % 2, c, o * P:(o + 1) * P])
                elif piece in ("o0", "o1"):
                    pe.wait_ge(in_w["w_out"], 16)
                    pe.wait_ge(g_ready, KD * (b + 1))
                    pe.wait_ge(res_ready, b + 1)
                    for i in range(2):
                        cols = slice((2 * o + i) * P, (2 * o + i + 1) * P)
                        for k in range(KD):
                            mm = pe.matmul(t[:, i * DM:(i + 1) * DM], gT[:, k, cols], w_out_s[:, k, :],
                                           start=(k == 0), stop=(k == KD - 1))
                        for k in range(KD):
                            a = i * DM + k * P
                            mm = pe.matmul(t[:, a:a + P], resT[b % 2][:, k, cols], ident[:], start=False,
                                           stop=True, skip_group_check=True)
                elif piece == "sb":
                    pe.wait_ge(diag_ready, C * (b + 1))
                    mm = pe.matmul(t[:], ones[:], score_diag[:].rearrange("p c j -> p (c j)"), start=True, stop=True)
                elif piece == "pf":
                    pe.wait_ge(chosen_ready, b + 1)
                    mm = pe.matmul(t[:, 0:C], before[:], chosen[:], start=True, stop=True)
                    for w in range(1, C):
                        mm = pe.matmul(t[:, w:C], ones[:], chosen[:, 0:C - w], start=False, stop=True,
                                       skip_group_check=True)
                elif piece == "ga":
                    pe.wait_ge(onehot_ready, C * (b + 1))
                    r = K * (b % 2)
                    for c in range(C):
                        mm = pe.matmul(t[r:r + K, 0:NCOL], onehot[:, b // 2, c, r:r + K], x1[:, C * b + c, :],
                                       start=(c == 0), stop=(c == C - 1))
                elif piece == "cs":
                    pe.wait_ge(tables, 4)
                    for i, tab in enumerate((cos_tab, sin_tab)):
                        for c in range(C):
                            mm = pe.matmul(t[:, i * P:(i + 1) * P], tab[:, c, :], onehot[:, b // 2, c, :],
                                           start=(c == 0), stop=(c == C - 1))
                fill_done(name, mm)

            def widen(t):
                b, n = t // NST, t % NST
                name = ("bb", t)
                wait_free(pe, name)
                if n == 0:
                    pe.wait_ge(mid_made, 2 * (b + 1))
                    pe.wait_ge(low16, b + 1)
                fill_done(name, pe.matmul(at(name)[:], spread[:, n, :], pieces[:, b % 2, :], start=True, stop=True))

            def turn_state(t):
                pe.wait_ge(scanned, KD * (t + 1))
                for cp in range(2):
                    name = ("hT", t, cp)
                    wait_free(pe, name)
                    for i in range(2):
                        for h in range(KD):
                            a = i * DM + h * P
                            c = 2 * cp + i
                            mm = turn(at(name)[:, a:a + P], state[:, 2 * (t % 2) + h, c * P:(c + 1) * P])
                    fill_done(name, mm)

            pe.wait_ge(in_w["vec"], 16 * 8)
            fill_done("vec", pe.transpose(at("vec")[:, 0:NVEC], vec_rows[:], ident[0:NVEC, 0:NVEC]))
            pe.wait_ge(in_w["conv"], 16)
            taps = conv_raw[:].rearrange("p o (i t) -> p o i t", t=TAPS)
            for k in range(TAPS):
                wait_free(pe, ("cw", k))
                for i in range(KD):
                    for o in range(KD):
                        a = i * DIN + o * P
                        mm = turn(at(("cw", k))[:, a:a + P], taps[:, o, i * P:(i + 1) * P, k])
                fill_done(("cw", k), mm)
            wait_free(pe, "wT")
            pe.wait_ge(in_w["w_in"], 16)
            for i in range(KD):
                for j in range(KD):
                    a = i * DM + j * P
                    mm = turn(at("wT")[:, a:a + P], w_in_s[:, j, i * P:(i + 1) * P])
            fill_done("wT", mm)
            wait_drained(pe, "wT")
            for v in range(4):
                j, k = v // 2, 2 * (v % 2)
                wait_free(pe, ("vc", v))
                wait_drained(pe, ("cw", k))
                wait_drained(pe, ("cw", k + 1))
                for i in range(KD):
                    mm = pe.matmul(at(("vc", v))[:].rearrange("p (t o) -> p t o", t=2), w_inT[:, i, j * P:(j + 1) * P],
                                   conv_t[:, k:k + 2, i, :], start=(i == 0), stop=(i == KD - 1))
                fill_done(("vc", v), mm)
            for piece in FRONT:
                front(0, piece)
            pe.wait_ge(pieces_clear, 2)
            widen(0)
            widen(1)
            for b in range(B):
                for n in range(NST):
                    t = b * NST + n
                    if t + 2 < B * NST:
                        widen(t + 2)
                    if t >= 1:
                        turn_state(t - 1)
                    if b >= 1:
                        for piece in TAIL_AT.get(n, ()):
                            tail(b - 1, piece)
                    if b + 1 < B:
                        for piece in FRONT_AT.get(n, ()):
                            front(b + 1, piece)
            turn_state(T_LAST)
            for piece in TAIL:
                tail(B - 1, piece)

            def rows_to_T(name, count):
                wait_free(pe, name)
                pe.wait_ge(h_ready, count)
                for k in range(KD):
                    for p in range(ST):
                        a = k * S + p * P
                        mm = turn(at(name)[:, a:a + P], h_rows[:, p, k * P:(k + 1) * P])
                fill_done(name, mm)

            rows_to_T("h1T", ST)
            for p in range(ST):
                wait_free(pe, ("selT", p))
                for c in range(C):
                    mm = turn(at(("selT", p))[:, c * P:(c + 1) * P], onehot[:, p, c, :])
                fill_done(("selT", p), mm)
            pe.wait_ge(in_w["w_qk"], 32)
            wait_drained(pe, "h1T")
            for j in range(HQK // 2):
                wait_free(pe, ("qk", j))
                for i in range(2):
                    head = 2 * j + i
                    for k in range(KD):
                        mm = pe.matmul(at(("qk", j))[:, i * S:(i + 1) * S], w_qk[:, k, head * P:(head + 1) * P],
                                       hT[:, k, :], start=(k == 0), stop=(k == KD - 1))
                fill_done(("qk", j), mm)
            pe.wait_ge(in_w["w_v"], 16)
            for v in range(4):
                p, half = v // 2, v % 2
                wait_free(pe, ("v", v))
                for k in range(KD):
                    mm = pe.matmul(at(("v", v))[:], hT[:, k, p * P:(p + 1) * P], w_v[:, k, half * 512:(half + 1) * 512],
                                   start=(k == 0), stop=(k == KD - 1))
                fill_done(("v", v), mm)

            def scores(h):
                name = ("sc", h)
                t = at(name)
                q, k = h, N_HEADS + h // (N_HEADS // N_KV)
                wait_free(pe, name)
                pe.wait_ge(roped, k // 2 + 1)
                pe.matmul(t[:, 0:P], qkT[:, q, 0:P], qkT[:, k, 0:P], start=True, stop=False)
                pe.matmul(t[:, 0:P], ident16[:], causal[:], start=False, stop=True)
                pe.matmul(t[:, P:P + S], qkT[:, q, P:S], qkT[:, k, :], start=True, stop=True)
                mm = pe.matmul(t[:, S:S + P], ident16[:], causal[:], start=False, stop=True, skip_group_check=True)
                fill_done(name, mm)

            def turn_probs(h):
                name = ("pT", h)
                wait_free(pe, name)
                pe.wait_ge(normed, 2 * (h + 1))
                for i, a in enumerate((0, P, S)):
                    mm = turn(at(name)[:, i * P:(i + 1) * P], probs[:, h % 3, a:a + P])
                fill_done(name, mm)

            def mix(h):
                name = ("o", h)
                kv = h // (N_HEADS // N_KV)
                wait_free(pe, name)
                wait_drained(pe, ("pT", h))
                if h == 0:
                    for v in range(4):
                        wait_drained(pe, ("v", v))
                pe.matmul(at(name)[:, 0:S], v_rows[:, 0, kv * P:(kv + 1) * P], probsT[:, h % 2, 0:S], start=True, stop=True)
                mm = pe.matmul(at(name)[:, P:S], v_rows[:, 1, kv * P:(kv + 1) * P], probsT[:, h % 2, S:S + P],
                               start=False, stop=True, skip_group_check=True)
                fill_done(name, mm)

            def project(h):
                wait_drained(pe, ("o", h))
                for p in range(ST):
                    if h == 0:
                        wait_free(pe, ("wo", p))
                    mm = pe.matmul(at(("wo", p))[:, 0:DM], oT[:, h, p * P:(p + 1) * P], w_o[:, h, :],
                                   start=(h == 0), stop=(h == N_HEADS - 1))
                    if h == N_HEADS - 1:
                        fill_done(("wo", p), mm)

            pe.wait_ge(in_w["w_o"], 16)
            for i in range(N_HEADS + LAG_OUT):
                if i < N_HEADS:
                    scores(i)
                if 0 <= i - LAG_TURN < N_HEADS:
                    turn_probs(i - LAG_TURN)
                if 0 <= i - LAG_MIX < N_HEADS:
                    mix(i - LAG_MIX)
                if i >= LAG_OUT:
                    project(i - LAG_OUT)
            rows_to_T("h2T", 2 * ST)
            pe.wait_ge(in_w["w_gu"], 32)
            wait_drained(pe, "h2T")
            for f in range(FC):
                wait_free(pe, ("gu", f))
                for i in range(2):
                    col = i * FF + f * P
                    for k in range(KD):
                        mm = pe.matmul(at(("gu", f))[:, i * S:(i + 1) * S], w_gu[:, k, col:col + P], hT[:, k, :],
                                       start=(k == 0), stop=(k == KD - 1))
                fill_done(("gu", f), mm)
            pe.wait_ge(in_w["w_dn"], 16)
            for f in range(FC):
                pe.wait_ge(m_ready, f + 1)
                for p in range(ST):
                    if f == 0:
                        wait_free(pe, ("dn", p))
                    mm = pe.matmul(at(("dn", p))[:, 0:DM], mT[:, f, p * P:(p + 1) * P], w_dn[:, f, :],
                                   start=(f == 0), stop=(f == FC - 1))
                    if f == FC - 1:
                        fill_done(("dn", p), mm)
            for i in range(B * C // 2):
                b, p = 2 * i // C, 2 * i // C // 2
                r = K * (b % 2)
                name = ("put", i)
                wait_free(pe, name)
                wait_drained(pe, ("selT", p))
                pe.wait_ge(change_ready, p + 1)
                for j in range(2):
                    c = (2 * i + j) % C
                    mm = pe.matmul(at(name)[:, j * DM:(j + 1) * DM], selT[r:r + K, p, c * P:(c + 1) * P],
                                   change[r:r + K, p, :], start=True, stop=True)
                fill_done(name, mm)

        @block.scalar
        def _(act):
            seq = [0]

            def link(ins):
                seq[0] += 1
                ins.then_inc(act_seq, 1)
                act.wait_ge(act_seq, seq[0])

            def copy_out(name, dst, src=None, func=ACT.Copy, **kw):
                wait_filled(act, name)
                drain_done(name, act.activation(dst, at(name)[:] if src is None else src, func, **kw))

            def flat(ap):
                return ap.rearrange("p a b -> p (a b)")

            def front(b, piece):
                o = int(piece[-1]) if piece[-1].isdigit() else 0
                name = (piece, b)
                if piece in ("xT0", "xT1"):
                    if b >= 1:
                        act.wait_ge(res_ready, b)
                    copy_out(name, xT[:, o, PAD:])
                elif piece in ("r0", "r1"):
                    if b >= 1:
                        act.wait_ge(silu_ready, b)
                    copy_out(name, rT[:, o, :])
                elif piece in ("cv0d", "cv1d"):
                    o = int(piece[2])
                    if b == 0 and o == 0:
                        wait_drained(act, "vec")
                    if b >= 1:
                        act.wait_ge(res_ready, b)
                    copy_out((piece[:3], b), xsT[:, o, :], func=ACT.Identity, bias=vec[:, CB + o:CB + o + 1])
                elif piece == "su":
                    wait_drained(act, ("cv1", b))
                    act.activation(uT[b % 2], xsT, ACT.Silu).then_inc(u_ready, 1)
                elif piece == "sr":
                    wait_drained(act, ("r1", b))
                    wait_drained(act, ("r0", b))
                    if b >= 2:
                        act.wait_ge(g_ready, KD * (b - 1))
                    act.activation(silu_r[b % 2], rT, ACT.Silu).then_inc(silu_ready, 1)
                    if b == 0:
                        rope_tables()
                    act.preload_act_table_set("natural_log_exp_and_others")
                elif piece == "dt":
                    act.preload_act_table_set("natural_log_exp_and_others")
                    copy_out(name, dtT[:])
                elif piece == "bc":
                    copy_out(name, bcT[:], at(name)[0:2 * NST, :])
                    wait_drained(act, name)
                    if b == 0:
                        act.wait_ge(pieces_clear, 1)
                    act.activation(pieces[0:NST, b % 2, :], bcT[0:NST, :], ACT.Copy).then_inc(top16, 1)
                elif piece == "cr":
                    copy_out(name, flat(bc_rows[:, b % 2]), at(name)[:, 0:C * 2 * NST])
                    act.wait_ge(rest_made, b + 1)
                    act.activation(mid16[:], rest1[:], ACT.Copy).then_inc(mid_made, 1)
                    act.activation(pieces[PIECE:PIECE + NST, b % 2, :], rest1[:], ACT.Copy).then_inc(mid_made, 1)
                elif piece in ("dl0", "dl1"):
                    if b >= 1:
                        act.wait_ge(sp_max, b)
                    copy_out(name, pre[:, o, :], func=ACT.Identity, bias=vec[:, BDT + o:BDT + o + 1])
                elif piece == "s1":
                    wait_drained(act, ("dl0", b))
                    wait_drained(act, ("dl1", b))
                    if b >= 1:
                        act.wait_ge(du_ready, b)
                    link(act.activation(sp_l, pre, ACT.Abs))
                    act.activation(sp_e, sp_l, ACT.Exp, scale=-1.0).then_inc(sp_exp, 1)
                elif piece == "s3":
                    act.wait_ge(sp_one, b + 1)
                    act.wait_ge(sp_exp, b + 1)
                    act.activation(sp_l, sp_w, ACT.Ln).then_inc(sp_log, 1)

            def rope_tables():
                half = HEAD_DIM // 2
                act.wait_ge(angles, 1)
                ang = z[:, 0:2, :].rearrange("p a b -> p (a b)").rearrange("p (c f) -> p c f", c=C)
                for tab, f0, sign in ((cos_tab, 0, 1.0), (sin_tab, half, -1.0)):
                    act.activation(tab[:, :, 0:half], ang[:, :, f0:f0 + half], ACT.Sin, scale=sign).then_inc(tables, 1)
                    act.activation(tab[:, :, half:], ang[:, :, f0:f0 + half], ACT.Sin).then_inc(tables, 1)

            def tail(b, piece):
                name = (piece, b)
                if piece in ("o0", "o1"):
                    o = int(piece[-1])
                    if b >= 1:
                        act.wait_ge(x1_ready, b)
                    copy_out(name, flat(z[:, 2 * o:2 * o + 2, :]))
                elif piece == "ga":
                    r = K * (b % 2)
                    wait_filled(act, name)
                    drain_done(name, act.activation(sel[r:r + K, b // 2, :], at(name)[r:r + K, 0:NCOL], ACT.Copy))
                elif piece == "cs" and b % 2 == 1:
                    wait_filled(act, name)
                    act.activation(cosT[:, (b // 2) * P:(b // 2 + 1) * P], at(name)[:, 0:P], ACT.Copy)
                    drain_done(name, act.activation(sinT[:, (b // 2) * P:(b // 2 + 1) * P], at(name)[:, P:2 * P], ACT.Copy))

            def copy_wide(t):
                if t >= 2:
                    act.wait_ge(bu_made, t - 1)
                copy_out(("bb", t), b_wide[:, t % 2, :])

            def make_decay(t):
                b, n = t // NST, t % NST
                for h in range(KD):
                    u = KD * t + h
                    if n == 0 and h == 0:
                        act.wait_ge(sp_max, b + 1)
                        act.wait_ge(du_ready, b + 1)
                    if u >= NDA:
                        act.wait_ge(scanned, u - NDA + 1)
                    act.activation(decay[:, u % NDA, :], delta[b % 2][:, h, :], ACT.Exp,
                                   scale=a_neg[:, h, n:n + 1]).then_inc(decay_made, 1)

            act.wait_ge(in_w["a"], 16)
            link(act.activation(a_exp[:], a_exp[:], ACT.Exp))
            act.activation(a_neg[:], a_exp[:], ACT.Copy, scale=-1.0).then_inc(a_ready, 1)
            copy_out("vec", vec[:], at("vec")[:, 0:NVEC])
            for k in range(TAPS):
                copy_out(("cw", k), flat(conv_t[:, k]))
            copy_out("wT", flat(w_inT))
            for v in range(4):
                j, k = v // 2, 2 * (v % 2)
                copy_out(("vc", v), conv_x[:, k:k + 2, j, :], at(("vc", v))[:].rearrange("p (t o) -> p t o", t=2))
            for piece in FRONT:
                front(0, piece)
            copy_wide(0)
            copy_wide(1)
            act.wait_ge(a_ready, 1)
            LEAD = NDA // KD - 1
            for t in range(LEAD):
                make_decay(t)
            for b in range(B):
                for n in range(NST):
                    t = b * NST + n
                    if t + 2 < B * NST:
                        copy_wide(t + 2)
                    if t + LEAD < B * NST:
                        make_decay(t + LEAD)
                    if b >= 1:
                        for piece in TAIL_AT.get(n, ()):
                            tail(b - 1, piece)
                    if b + 1 < B:
                        for piece in FRONT_AT.get(n, ()):
                            front(b + 1, piece)
            for piece in TAIL:
                tail(B - 1, piece)

            def rows_to_T(name, w):
                wait_filled(act, name)
                act.activation(hT[:, 0, :], at(name)[:, 0:S], ACT.Copy, scale=vec[:, w:w + 1])
                drain_done(name, act.activation(hT[:, 1, :], at(name)[:, S:], ACT.Copy, scale=vec[:, w + 1:w + 2]))

            rows_to_T("h1T", LN1)
            for p in range(ST):
                copy_out(("selT", p), selT[:, p, :])
            mid = HEAD_DIM // 2
            for j in range(HQK // 2):
                name = ("qk", j)
                wait_filled(act, name)
                if j >= 2:
                    act.wait_ge(roped, j - 1)
                for i in range(2):
                    w = BQ + 2 * j + i
                    src = at(name)[:, i * S:(i + 1) * S]
                    act.activation(qk_raw[:, j % 2, i, :], src, ACT.Identity, bias=vec[:, w:w + 1])
                    act.activation(qk_swap[0:mid, j % 2, i, :], src[mid:, :], ACT.Identity, bias=vec[mid:, w:w + 1])
                    last = act.activation(qk_swap[mid:, j % 2, i, :], src[0:mid, :], ACT.Identity, bias=vec[0:mid, w:w + 1])
                drain_done(name, last)
            for v in range(4):
                copy_out(("v", v), v_rows[:, v // 2, (v % 2) * 512:(v % 2 + 1) * 512])
            scale = float(HEAD_DIM) ** -0.5
            for i in range(N_HEADS + LAG_MIX):
                if i < N_HEADS:
                    h = i
                    act.wait_ge(top_ready, h + 1)
                    wait_filled(act, ("sc", h))
                    if h >= 3:
                        wait_filled(act, ("pT", h - 3))
                    act.activation(probs[:, h % 3, 0:P], at(("sc", h))[:, 0:P], ACT.Exp, bias=bias[:, h, 0:1],
                                   scale=scale, accum_out=sums[:, h, 0:1])
                    drain_done(("sc", h), act.activation(probs[:, h % 3, P:], at(("sc", h))[:, P:P + S], ACT.Exp,
                                                         bias=bias[:, h, 1:2], scale=scale, accum_out=sums[:, h, 1:2]))
                if i >= LAG_MIX:
                    h = i - LAG_MIX
                    w = BV + h // (N_HEADS // N_KV)
                    copy_out(("o", h), oT[:, h, :], at(("o", h))[:, 0:S], func=ACT.Identity, bias=vec[:, w:w + 1])
            act.activation(gate[:, :, 0:1], sel[:, :, DM:DM + 1], ACT.Exp, scale=-1.0).then_inc(gate_exp, 1)
            rows_to_T("h2T", LN2)
            for f in range(FC):
                wait_filled(act, ("gu", f))
                if f >= 2:
                    act.wait_ge(m_ready, f - 1)
                act.activation(gate_s[:, f % 2, :], at(("gu", f))[:, 0:S], ACT.Silu).then_inc(gate_act, 1)

        @block.vector
        def _(dve):
            seq = [0]

            def link(ins):
                seq[0] += 1
                ins.then_inc(dve_seq, 1)
                dve.wait_ge(dve_seq, seq[0])

            def scan(t):
                for h in range(KD):
                    dve.wait_ge(bu_made, t + 1)
                    dve.wait_ge(decay_made, KD * t + h + 1)
                    if t >= 2:
                        wait_filled(dve, ("hT", t - 2, 1))
                    dve.tensor_tensor_scan(state[:, 2 * (t % 2) + h, :], decay[:, (KD * t + h) % NDA, :],
                                           bu[:, t % 2, h, :], 0.0, ALU.mult, ALU.add).then_inc(scanned, 1)

            def weigh(t):
                b, n = t // NST, t % NST
                for c in range(C):
                    name = ("hT", t, c // 2)
                    src = at(name)[:, (c % 2) * DM:(c % 2 + 1) * DM]
                    y = y_rows[:, b % 2, c, :]
                    weight = bc_rows[:, b % 2, c, NST + n:NST + n + 1]
                    wait_filled(dve, name)
                    if n == 0:
                        if b >= 2:
                            wait_filled(dve, ("yt1", b - 2))
                        last = dve.tensor_scalar(y, src, weight, None, ALU.mult)
                    else:
                        wait_drained(dve, ("hT", t - 1, c // 2))
                        last = dve.scalar_tensor_tensor(out=y, in0=src, scalar=weight, in1=y, op0=ALU.mult, op1=ALU.add)
                    if c % 2:
                        drain_done(name, last)

            def front(b, piece):
                if piece == "bc":
                    dve.wait_ge(top16, b + 1)
                    if b >= 1:
                        dve.wait_ge(mid_made, 2 * b)
                    dve.tensor_tensor(rest1[:], bcT[0:NST, :], pieces[0:NST, b % 2, :], ALU.subtract).then_inc(rest_made, 1)
                elif piece == "cr":
                    dve.wait_ge(mid_made, 2 * b + 1)
                    dve.wait_ge(rest_made, b + 1)
                    dve.tensor_tensor(pieces[2 * PIECE:, b % 2, :], rest1[:], mid16[:], ALU.subtract).then_inc(low16, 1)
                elif piece == "s3" and b == 0:
                    dve.wait_ge(sp_exp, 1)
                    dve.tensor_scalar(sp_w, sp_e, 1.0, None, ALU.add).then_inc(sp_one, 1)
                    dve.wait_ge(sp_one, 1)
                    link(dve.scalar_tensor_tensor(out=sp_e, in0=sp_w, scalar=-1.0, in1=sp_e, op0=ALU.add, op1=ALU.subtract))
                    link(dve.scalar_tensor_tensor(out=sp_e, in0=pre, scalar=0.0, in1=sp_e, op0=ALU.max, op1=ALU.subtract))
                    dve.wait_ge(sp_log, 1)
                    dve.tensor_tensor(delta[0], sp_l, sp_e, ALU.add).then_inc(sp_max, 1)
                    dve.wait_ge(sp_max, 1)
                    dve.wait_ge(u_ready, 1)
                    dve.tensor_tensor(duT[0], delta[0], uT[0], ALU.mult).then_inc(du_ready, 1)
                elif piece == "s4" and b > 0:
                    dve.wait_ge(sp_log, b + 1)
                    dve.scalar_tensor_tensor(out=sp_l, in0=pre, scalar=0.0, in1=sp_l, op0=ALU.max,
                                             op1=ALU.add).then_inc(sp_max, 1)

            def tail(b, piece):
                o = int(piece[-1]) if piece[-1].isdigit() else 0
                name = (piece, b)
                if piece in ("yt0", "yt1"):
                    wait_filled(dve, name)
                    if b >= 1:
                        wait_filled(dve, ("o1", b - 1))
                    ins = dve.scalar_tensor_tensor(out=gT[:, o, :], in0=uT[b % 2][:, o, :],
                                                   scalar=vec[:, DSK + o:DSK + o + 1], in1=at(name)[:],
                                                   op0=ALU.mult, op1=ALU.add)
                    drain_done(name, ins)
                elif piece == "ln":
                    layer_norm_stats(("o0", b), ("o1", b), var_ready)
                    dve.wait_ge(rstd_ready, b + 1)
                    for c in range(C):
                        ins = dve.tensor_scalar(x1[:, C * b + c, 0:DM], z[:, c, :], mv[:, c, 0:1], rstd[:, c:c + 1],
                                                ALU.subtract, ALU.mult)
                    link(ins)
                    if b == 0:
                        dve.wait_ge(in_w["router"], 16)
                    for c in range(C):
                        ins = dve.tensor_tensor_reduce(junk[:, c % 2, (c // 2) * DM:(c // 2 + 1) * DM], x1[:, C * b + c, 0:DM],
                                                       router[:], 1.0, 0.0, ALU.mult, ALU.add, x1[:, C * b + c, DM:DM + 1])
                    ins.then_inc(x1_ready, 1)
                elif piece == "sb":
                    wait_filled(dve, name)
                    dve.wait_ge(x1_ready, b + 1)
                    for c in range(C):
                        score = x1[:, C * b + c, DM:DM + 1]
                        link(dve.tensor_scalar(junk[:, 0, :], at(name)[:], score, 0.0, ALU.is_gt, ALU.add,
                                               accum_out=ranks[:, 0, c:c + 1]))
                        ins = dve.scalar_tensor_tensor(out=junk[:, 1, :], in0=at(name)[:], scalar=score,
                                                       in1=earlier[:, c, :], op0=ALU.is_equal, op1=ALU.mult,
                                                       accum_out=ranks[:, 1, c:c + 1])
                        if c == C - 1:
                            drain_done(name, ins)
                            wait_drained(dve, name)
                        else:
                            link(ins)
                    link(dve.tensor_tensor(ranks[:, 0, :], ranks[:, 0, :], ranks[:, 1, :], ALU.add))
                    dve.tensor_scalar(chosen[:], ranks[:, 0, :], float(K), None, ALU.is_lt).then_inc(chosen_ready, 1)
                elif piece == "pf":
                    dve.wait_ge(chosen_ready, b + 1)
                    link(dve.tensor_scalar(ranks[:, 1, :], chosen[:], -1000.0, 1000.0, ALU.mult, ALU.add))
                    wait_filled(dve, name)
                    drain_done(name, dve.tensor_tensor(place[:], at(name)[:, 0:C], ranks[:, 1, :], ALU.add))
                    wait_drained(dve, name)
                    r = K * (b % 2)
                    for c in range(C):
                        dve.tensor_scalar(onehot[:, b // 2, c, r:r + K], slot_no[:], place[:, c:c + 1], None,
                                          ALU.is_equal).then_inc(onehot_ready, 1)

            def layer_norm_stats(name0, name1, signal):
                wait_drained(dve, name0)
                wait_drained(dve, name1)
                for c in range(C):
                    ins = dve.bn_stats(stats[:, c, :], z[:, c, :])
                link(ins)
                for c in range(C):
                    ins = dve.bn_aggr(mv[:, c, :], stats[:, c, :])
                ins.then_inc(signal, 1)

            half = HEAD_DIM // 2
            dve.wait_ge(consts, N_CONST)
            dve.wait_ge(in_w["freq"], 16)
            ang, turns = (z[:, 2 * i:2 * i + 2, :].rearrange("p a b -> p (a b)").rearrange("p (c f) -> p c f", c=C)
                          for i in range(2))
            for c in range(C):
                for f0 in (0, half):
                    ins = dve.tensor_scalar(ang[:, c, f0:f0 + half], freq[:], token_no[:, c:c + 1], None, ALU.mult)
            link(ins)
            link(dve.tensor_scalar(turns[:, :, 0:half], ang[:, :, 0:half], 1.0 / TWO_PI, 0.25, ALU.mult, ALU.add))
            link(dve.tensor_scalar(turns[:, :, half:], ang[:, :, half:], 1.0 / TWO_PI, None, ALU.mult))
            link(dve.tensor_scalar(turns, turns, ROUND, None, ALU.add))
            link(dve.tensor_scalar(turns, turns, -ROUND, None, ALU.add))
            for part in two_pi_parts():
                link(dve.scalar_tensor_tensor(out=ang, in0=turns, scalar=-part, in1=ang, op0=ALU.mult, op1=ALU.add))
            link(dve.tensor_scalar(ang[:, :, 0:half], ang[:, :, 0:half], float(np.pi / 2), None, ALU.add))
            dve.tensor_scalar(ang, ang, -3.1415925, 3.1415925, ALU.max, ALU.min).then_inc(angles, 1)

            for piece in FRONT:
                front(0, piece)
            for b in range(B):
                for n in range(NST):
                    t = b * NST + n
                    scan(t)
                    if t >= 1:
                        weigh(t - 1)
                    if b >= 1:
                        for piece in TAIL_AT.get(n, ()):
                            tail(b - 1, piece)
                    if b + 1 < B:
                        for piece in FRONT_AT.get(n, ()):
                            front(b + 1, piece)
            weigh(T_LAST)
            for piece in TAIL:
                tail(B - 1, piece)

            def rms(count, src):
                for p in range(ST):
                    ins = dve.tensor_tensor_reduce(junk[:, 0, p * DM:(p + 1) * DM], src[p], src[p], 1.0, 0.0, ALU.mult,
                                                   ALU.add, ss[:, p:p + 1])
                ins.then_inc(sel_stat, 1)
                dve.wait_ge(sel_rstd, count)
                for p in range(ST):
                    dve.tensor_scalar(h_rows[:, p, :], src[p], rrms[:, p:p + 1], None, ALU.mult).then_inc(h_ready, 1)

            for b in range(B):
                wait_drained(dve, ("ga", b))
            rms(1, [sel[:, p, 0:DM] for p in range(ST)])
            for j in range(HQK // 2):
                wait_drained(dve, ("qk", j))
                if j >= 2:
                    dve.wait_ge(roped, j - 1)
                for src, tab in ((qk_raw, cosT), (qk_swap, sinT)):
                    part = src[:, j % 2]
                    dve.tensor_tensor(part, part, tab[:].unsqueeze(1).to_broadcast([P, 2, S]), ALU.mult)\
                       .then_inc(rope_parts, 1)
            scale = float(HEAD_DIM) ** -0.5
            for i in range(N_HEADS + LAG_TURN):
                if i < N_HEADS:
                    h = i
                    wait_filled(dve, ("sc", h))
                    dve.tensor_reduce(top[:, h, 0:1], at(("sc", h))[:, 0:P], AX.X, ALU.max)
                    link(dve.tensor_reduce(top[:, h, 1:2], at(("sc", h))[:, P:P + S], AX.X, ALU.max))
                    dve.tensor_scalar(bias[:, h, :], top[:, h, :], -scale, None, ALU.mult).then_inc(top_ready, 1)
                if 1 <= i <= N_HEADS:
                    h = i - 1
                    wait_drained(dve, ("sc", h))
                    dve.reciprocal(rsum[:, h, :], sums[:, h, :]).then_inc(rsum_ready, 1)
                if i >= LAG_TURN:
                    h = i - LAG_TURN
                    wait_filled(dve, ("pT", h))
                    if h >= 2:
                        wait_filled(dve, ("o", h - 2))
                    drain_done(("pT", h), dve.tensor_copy(probsT[:, h % 2, :], at(("pT", h))[:, 0:3 * P]))
            for p in range(ST):
                wait_filled(dve, ("wo", p))
                drain_done(("wo", p), dve.tensor_tensor(x_att[:, p, :], at(("wo", p))[:, 0:DM], sel[:, p, 0:DM], ALU.add))
            for p in range(ST):
                wait_drained(dve, ("wo", p))
            wait_filled(dve, "h1T")
            rms(2, [x_att[:, p, :] for p in range(ST)])
            dve.wait_ge(gate_exp, 1)
            link(dve.tensor_scalar(gate[:, :, 0:1], gate[:, :, 0:1], 1.0, None, ALU.add))
            link(dve.reciprocal(gate[:, :, 1:2], gate[:, :, 0:1]))
            for f in range(FC):
                dve.wait_ge(gate_act, f + 1)
                wait_filled(dve, ("gu", f))
                ins = dve.tensor_tensor(mT[:, f, :], gate_s[:, f % 2, :], at(("gu", f))[:, S:], ALU.mult)
                drain_done(("gu", f), ins)
                wait_drained(dve, ("gu", f))
                dve.sem_inc(m_ready, 1)
            for p in range(ST):
                wait_filled(dve, ("dn", p))
                drain_done(("dn", p), dve.tensor_tensor(x_att[:, p, :], at(("dn", p))[:, 0:DM], x_att[:, p, :], ALU.add))
                wait_drained(dve, ("dn", p))
                link(dve.tensor_tensor(x_att[:, p, :], x_att[:, p, :], sel[:, p, 0:DM], ALU.subtract))
                dve.tensor_scalar(change[:, p, :], x_att[:, p, :], gate[:, p, 1:2], None, ALU.mult)\
                   .then_inc(change_ready, 1)
            for b in range(B):
                if b >= 1:
                    dve.wait_ge(out_ready, C * b)
                for j in range(2):
                    i = 2 * b + j
                    wait_filled(dve, ("put", i))
                    src = at(("put", i))[:].rearrange("p (c d) -> p c d", c=2)
                    drain_done(("put", i), dve.scalar_tensor_tensor(
                        out=z[:, 2 * j:2 * j + 2, :], in0=x1[:, 2 * i:2 * i + 2, 0:DM], scalar=2.0, in1=src,
                        op0=ALU.mult, op1=ALU.add))
                layer_norm_stats(("put", 2 * b), ("put", 2 * b + 1), out_var)
                dve.wait_ge(out_rstd, b + 1)
                if b >= 2:
                    dve.wait_ge(stored[b % 2], 16 * (b // 2))
                for c in range(C):
                    dve.tensor_scalar(out_rows[:, b % 2, c, :], z[:, c, :], mv[:, c, 0:1], rstd[:, c:c + 1],
                                      ALU.subtract, ALU.mult).then_inc(out_ready, 1)

        @block.gpsimd
        def _(pool):
            seq = [0]

            def link(ins):
                seq[0] += 1
                ins.then_inc(pool_seq, 1)
                pool.wait_ge(pool_seq, seq[0])

            def const(ins):
                ins.then_inc(consts, 1)

            link(pool.memset(ones[:], 1.0))
            const(pool.affine_select(ident[:], ones[:], [[-1, P]], ALU.is_equal, 0.0, base=0, channel_multiplier=1))
            const(pool.affine_select(before[:], ones[:], [[1, P]], ALU.is_gt, 0.0, base=0, channel_multiplier=-1))
            const(pool.affine_select(ident16[:], ones[:], [[-1, P]], ALU.is_equal, 0.0, base=0, channel_multiplier=1))
            link(pool.memset(causal[:], 0.0))
            const(pool.affine_select(causal[:], causal[:], [[-1, P]], ALU.is_ge, NEG, base=0, channel_multiplier=1))
            link(pool.memset(earlier[:], 1.0))
            for c in range(C):
                ins = pool.affine_select(earlier[:, c, :], earlier[:, c, :], [[-1, L]], ALU.is_gt, 0.0, base=P * c,
                                         channel_multiplier=1)
            const(ins)
            const(pool.iota(slot_no[:], [[1, K]], base=0, channel_multiplier=0, allow_small_or_imprecise_dtypes=True))
            const(pool.iota(token_no[:], [[P, C]], base=0, channel_multiplier=1, allow_small_or_imprecise_dtypes=True))
            const(pool.memset(half_pow[:], -0.5))
            const(pool.memset(sums[:], 0.0))
            pool.memset(xT[:, :, 0:PAD], 0.0).then_inc(conv_pad, 1)
            pool.memset(pieces[:], 0.0).then_inc(pieces_clear, 1)
            link(pool.memset(spread[:], 0.0))
            for j in range(3):
                link(pool.affine_select(spread[:], spread[:], [[-1, NST], [0, P]], ALU.not_equal, 1.0,
                                        base=-PIECE * j, channel_multiplier=1))
            pool.sem_inc(pieces_clear, 1)

            def front(b, piece):
                if piece == "rs":
                    for name in ("xT0", "xT1", "cv0", "cv1"):
                        wait_drained(pool, (name, b))
                    if b >= 2:
                        wait_filled(pool, ("o1", b - 2))
                    pool.tensor_tensor(resT[b % 2], xT[:, :, PAD:], xsT, ALU.add).then_inc(res_ready, 1)
                elif b == 0:
                    return
                elif piece == "s2":
                    pool.wait_ge(sp_exp, b + 1)
                    pool.tensor_scalar(sp_w, sp_e, 1.0, 1.0, ALU.add, ALU.mult).then_inc(sp_one, 1)
                elif piece == "s3":
                    pool.wait_ge(sp_one, b + 1)
                    pool.wait_ge(sp_log, b + 1)
                    link(pool.tensor_scalar(sp_w, sp_w, -1.0, 1.0, ALU.add, ALU.mult))
                    link(pool.tensor_tensor(sp_e, sp_e, sp_w, ALU.subtract))
                elif piece == "s5":
                    pool.wait_ge(sp_max, b + 1)
                    link(pool.tensor_tensor(delta[b % 2], sp_l, sp_e, ALU.add))
                elif piece == "s6":
                    pool.wait_ge(u_ready, b + 1)
                    pool.tensor_tensor(duT[b % 2], delta[b % 2], uT[b % 2], ALU.mult).then_inc(du_ready, 1)

            def make_bu(t):
                b = t // NST
                wait_drained(pool, ("bb", t))
                if t % NST == 0:
                    pool.wait_ge(du_ready, b + 1)
                if t >= 2:
                    pool.wait_ge(scanned, KD * (t - 1))
                pool.tensor_tensor(bu[:, t % 2], duT[b % 2], b_wide[:, t % 2, :].unsqueeze(1).to_broadcast([P, KD, L]),
                                   ALU.mult).then_inc(bu_made, 1)

            def inv_sqrt(dst, var, eps, scale=1.0):
                link(pool.tensor_scalar(dst, var, scale, eps, ALU.mult, ALU.add))
                return pool.tensor_tensor(dst, dst, half_pow[:, 0:dst.shape[1]], ALU.pow)

            def tail(b, piece):
                if piece in ("yt0", "yt1"):
                    o = int(piece[-1])
                    wait_drained(pool, (piece, b))
                    pool.wait_ge(silu_ready, b + 1)
                    pool.tensor_tensor(gT[:, o, :], gT[:, o, :], silu_r[b % 2][:, o, :], ALU.mult).then_inc(g_ready, 1)
                elif piece == "ln":
                    pool.wait_ge(var_ready, b + 1)
                    inv_sqrt(rstd[:], mv[:, :, 1:2].rearrange("p c o -> p (c o)"), LN_EPS).then_inc(rstd_ready, 1)
                    pool.wait_ge(x1_ready, b + 1)
                    if b >= 1:
                        wait_filled(pool, ("sb", b - 1))
                    for c in range(C):
                        pool.tensor_scalar(score_diag[:, c, :], ident[:], x1[:, C * b + c, DM:DM + 1], 1.0,
                                           ALU.mult, ALU.mult).then_inc(diag_ready, 1)

            for piece in FRONT:
                front(0, piece)
            make_bu(0)
            for b in range(B):
                for n in range(NST):
                    t = b * NST + n
                    if b >= 1:
                        for piece in TAIL_AT.get(n, ()):
                            tail(b - 1, piece)
                    if b + 1 < B:
                        for piece in FRONT_AT.get(n, ()):
                            front(b + 1, piece)
                    if t < T_LAST:
                        make_bu(t + 1)
            for piece in TAIL:
                tail(B - 1, piece)

            def rms(count):
                pool.wait_ge(sel_stat, count)
                inv_sqrt(rrms[:], ss[:], RMS_EPS, 1.0 / DM).then_inc(sel_rstd, 1)

            rms(1)
            for j in range(HQK // 2):
                pool.wait_ge(rope_parts, 2 * (j + 1))
                pool.tensor_tensor(qkT[:, 2 * j:2 * j + 2, :], qk_raw[:, j % 2], qk_swap[:, j % 2], ALU.add).then_inc(roped, 1)
            for h in range(N_HEADS):
                pool.wait_ge(rsum_ready, h + 1)
                pool.tensor_scalar(probs[:, h % 3, 0:P], probs[:, h % 3, 0:P], rsum[:, h, 0:1], 1.0, ALU.mult,
                                   ALU.mult).then_inc(normed, 1)
                pool.tensor_scalar(probs[:, h % 3, P:], probs[:, h % 3, P:], rsum[:, h, 1:2], 1.0, ALU.mult,
                                   ALU.mult).then_inc(normed, 1)
            rms(2)
            for b in range(B):
                pool.wait_ge(out_var, b + 1)
                inv_sqrt(rstd[:], mv[:, :, 1:2].rearrange("p c o -> p (c o)"), LN_EPS).then_inc(out_rstd, 1)


_OUTS = [((4, 512, 256), "float32")]


def kernel(**inputs):
    import concourse.bacc as _bacc
    from concourse.bass_utils import run_bass_kernel_spmd as _run

    nc = _bacc.Bacc("TRN2", target_bir_lowering=False, num_devices=1)
    order = ["L0_attn_" + n for n in ("x", "W_in", "conv_w", "conv_b", "W_x", "W_dt", "b_dt", "A_log", "D", "W_out")]
    order += ["L0_ffn_" + n for n in ("w_router", "wq", "bq", "wk", "bk", "wv", "bv", "wo", "w_gate", "w_up", "w_down",
                                      "ln1_w", "ln2_w")]
    arrays, args = {}, []
    for name in order:
        a = np.ascontiguousarray(inputs[name])
        arrays[f"in_{name}"] = a
        args.append(nc.dram_tensor(f"in_{name}", a.shape, mybir.dt.from_np(a.dtype), kind="ExternalInput").ap())
    freq = (1.0 / ROPE_THETA ** (np.arange(0, HEAD_DIM, 2, dtype=np.float32) / HEAD_DIM)).astype(np.float32)
    arrays["in_inv_freq"] = freq
    args.append(nc.dram_tensor("in_inv_freq", freq.shape, F32, kind="ExternalInput").ap())
    shape, dtype = _OUTS[0]
    args.append(nc.dram_tensor("out_0", shape, mybir.dt.from_np(np.dtype(dtype)), kind="ExternalOutput").ap())
    block_kernel(nc, *args)
    r = _run(nc, [arrays], core_ids=[0])
    return r.results[0]["out_0"]
```

```python
from contextlib import ExitStack

import numpy as np

import concourse.bass as bass
from concourse import mybir

F32 = mybir.dt.float32
BF16 = mybir.dt.bfloat16
ALU = mybir.AluOpType
ACT = mybir.ActivationFunctionType
AX = mybir.AxisListType

P = 128
HEAD_DIM = 128
N_HEADS = 16
N_KV = 8
CAPACITY = 0.125
ROPE_THETA = 10000.0
LN_EPS = 1e-5
RMS_EPS = 1e-6
ROUND = 1.5 * 2.0**23
TWO_PI = 2.0 * np.pi
BU_LEAD, WIDE_LEAD = 3, 4
LAG_TURN, LAG_MIX = 2, 3
LAG_OUT = (4, 9)
NEG = -1.0e38

FRONT_AT = {
    -24: ("xT0", "xT1"), -23: ("cv0a",), -22: ("cv0b",), -21: ("cv0c",), -20: ("cv0d",), -19: ("cv1a",),
    -18: ("cv1b",), -17: ("cv1c",), -16: ("r0", "cv1d"), -14: ("r1",), -13: ("su", "sr"), -11: ("dt",),
    -10: ("bc", "rs"), -9: ("cr", "dl0", "dl1"), -8: ("b0", "s1", "b1", "b2"), -7: ("s2",), -6: ("b3", "s3"),
    -5: ("s4",), -4: ("s5", "s6"),
}
FIRST_FRONT = ("xT0", "xT1", "cv0a", "cv0b", "cv0c", "cv0d", "cv1a", "cv1b", "cv1c", "cv1d", "su", "dt", "bc", "b0",
               "b1", "cr", "b2", "b3", "dl0", "dl1", "rs", "s1", "r0", "r1", "s3")
EARLY = ("xT0", "xT1", "cv0a", "cv0b", "cv0c", "cv0d", "cv1a")
WIDEN_BEFORE = ("xT0", "cv0b", "cv0d")
TAIL_AT = {
    1: ("yt0", "yt1"), 2: ("g0", "g1"), 3: ("o0",), 4: ("o1",), 5: ("ls0", "ls1"), 6: ("lp0", "lp1"),
    7: ("la0", "la1"), 8: ("lx0", "lx1", "ld0", "ld1"), 9: ("sb",), 10: ("k0",), 11: ("k1",), 12: ("k2", "k3"),
    13: ("pf",), 14: ("ga",), 15: ("cs",),
}
NORM_AT = {5: "hs", 6: "hp", 7: "hr", 8: "ht"}
LAST_TAIL = (
    "yt0", "yt1", "g0", "g1", "q0", "q1", "o0", "q2", "ls0", "q3", "lp0", "ls1", "q4", "o1", "lp1", "q5", "q6",
    "la0", "la1", "lx0", "lx1", "ld0", "ld1", "q7", "q8", "sb", "k0", "k1", "k2", "k3", "v0", "q9", "q10", "pf",
    "q11", "ga", "v1", "cs",
)
NO_FILL = (
    "su", "sr", "s1", "s2", "s3", "s4", "s5", "s6", "rs", "b0", "b1", "b2", "b3", "g0", "g1", "ls0", "ls1",
    "la0", "la1", "lp0", "lp1", "lx0", "lx1", "ld0", "ld1", "k0", "k1", "k2", "k3",
)


class Fills:

    def __init__(self):
        self.at = {}
        self.uses = [0] * 8

    def add(self, name, bank):
        self.at[name] = (bank, self.uses[bank])
        self.uses[bank] += 1


def two_pi_parts():
    a = float(np.float32(np.round(TWO_PI * 2**8) / 2**8))
    b = float(np.float32(np.round((TWO_PI - a) * 2**20) / 2**20))
    return a, b, float(np.float32(TWO_PI - a - b))


def block_kernel(nc, x, W_in, conv_w, conv_b, W_x, W_dt, b_dt, A_log, D, W_out, w_router, wq, bq, wk, bk, wv, bv,
                 wo, w_gate, w_up, w_down, ln1_w, ln2_w, inv_freq, out):
    B, L, DM = x.shape
    DIN, NST = A_log.shape
    TAPS = conv_w.shape[2]
    DTR = W_dt.shape[0]
    FF = w_gate.shape[1]
    C = L // P
    KD = DM // P
    K = max(1, int(L * CAPACITY))
    S = B * K
    ST = S // P
    PAD = TAPS - 1
    NCOL = DM + 1
    HQK = N_HEADS + N_KV
    FC = FF // P
    assert DIN == DM and C == 4 and KD == 2 and DTR == P and K == 64 and ST == 2

    fills = Fills()
    rest = [0]

    def add_rest(name):
        fills.add(name, 6 + rest[0] % 2)
        rest[0] += 1

    def add_pieces(b, pieces):
        for piece in pieces:
            if piece == "cs" and b % 2 == 0:
                continue
            if piece[:2] == "cv":
                if piece[-1] == "a":
                    fills.add((piece[:3], b), 1)
            elif piece not in NO_FILL:
                add_rest((piece, b))

    for i in range(TAPS):
        add_rest(("cw", i))
    add_rest("wT")
    add_rest("vec")
    for i in range(4):
        add_rest(("vc", i))
    T_LAST = B * NST - 1

    def tails(t):
        b, n = t // NST, t % NST
        return [(b - 1, piece) for piece in TAIL_AT.get(n, ())] if b >= 1 else []

    def fronts(t):
        late = {"cv1b": -16, "cv1c": -15, "cv1d": -14, "r1": -12, "su": -12, "sr": -12, "s5": -4}
        return [(b, piece) for b in range(B - 1, 0, -1) for off in sorted(FRONT_AT) for piece in FRONT_AT[off]
                if b * NST + (late.get(piece, off) if b == 1 else off) == t and not (b == 1 and piece in EARLY)]

    def norms(t):
        return NORM_AT.get(t - (B - 1) * NST)

    add_pieces(0, FIRST_FRONT)
    for t in range(WIDE_LEAD):
        fills.add(("bb", t), 0)
    add_pieces(1, EARLY)
    for t in range(B * NST):
        if t + WIDE_LEAD <= T_LAST:
            fills.add(("bb", t + WIDE_LEAD), 0)
        if t >= 1:
            for cp in range(2):
                fills.add(("hT", t - 1, cp), 2 + 2 * ((t - 1) % 2) + cp)
        for b, piece in tails(t) + fronts(t):
            add_pieces(b, (piece,))
        if norms(t) == "ht":
            add_rest(("h1T", 0))
    for cp in range(2):
        fills.add(("hT", T_LAST, cp), 2 + 2 * (T_LAST % 2) + cp)
    for piece in LAST_TAIL:
        if piece[0] == "q":
            fills.add(("qk", 0, int(piece[1:])), int(piece[1:]) % 4)
        elif piece[0] == "v":
            fills.add(("v", int(piece[1:])), 4 + int(piece[1:]))
        else:
            add_pieces(B - 1, (piece,))
    fills.add(("h1T", 1), 4)
    for j in range(HQK // 2):
        fills.add(("qk", 1, j), j % 4)
    for p in range(ST):
        fills.add(("selT", p), 4 + p)
    for v in range(2, 4):
        fills.add(("v", v), 6 + v % 2)
    for i in range(N_HEADS + LAG_MIX):
        if i < N_HEADS:
            fills.add(("sc", i), i % 3)
        if 0 <= i - LAG_TURN < N_HEADS:
            fills.add(("pT", i - LAG_TURN), 3 + (i - LAG_TURN) % 2)
        if 0 <= i - LAG_MIX < N_HEADS:
            fills.add(("o", i - LAG_MIX), 5)
    for p in range(ST):
        fills.add(("wo", p), 6 + p)
    fills.add(("h2T", 0), 0)
    PUTS = B * C // 2 // ST
    put_banks = ((5, 0, 6, 7), (1, 2, 3, 4))
    for p in range(ST):
        for f in range(FC):
            if (p, f) == (0, FC - 1):
                fills.add(("h2T", 1), 0)
            fills.add(("gu", p, f), 1 + f % 4)
        fills.add(("dn", p), 6 + p)
        for i in range(PUTS):
            fills.add(("put", PUTS * p + i), put_banks[p][i])

    with ExitStack() as ctx:
        def sb(name, shape, dt=F32):
            return ctx.enter_context(nc.sbuf_tensor(name, shape, dt))

        def sem(name):
            return ctx.enter_context(nc.semaphore(name))

        bank = [ctx.enter_context(nc.psum_tensor(f"bank{i}", [P, 512], F32)) for i in range(8)]
        filled = [sem(f"filled{i}") for i in range(8)]
        drained = [sem(f"drained{i}") for i in range(8)]

        def at(name):
            return bank[fills.at[name][0]]

        def wait_free(pe, name):
            i, k = fills.at[name]
            if k:
                pe.wait_ge(drained[i], k)

        def fill_done(name, ins):
            ins.then_inc(filled[fills.at[name][0]], 1)

        def wait_filled(eng, name):
            i, k = fills.at[name]
            eng.wait_ge(filled[i], k + 1)

        def drain_done(name, ins):
            ins.then_inc(drained[fills.at[name][0]], 1)

        def wait_drained(eng, name):
            i, k = fills.at[name]
            eng.wait_ge(drained[i], k + 1)

        ident = sb("ident", [P, P])
        ident16 = sb("ident16", [P, P], BF16)
        ones = sb("ones", [P, P])
        before = sb("before", [P, P])
        earlier = sb("earlier", [P, P], BF16)
        causal = sb("causal", [P, P], BF16)
        slot_no = sb("slot_no", [P, K])
        token_no = sb("token_no", [P, C])
        half_pow = sb("half_pow", [P, C])
        def parts(name, shapes):
            whole = sb(name, [P, sum(int(np.prod(s)) for s in shapes)])
            cut, a = [], 0
            for s in shapes:
                n = int(np.prod(s))
                ap = whole[:, a:a + n]
                if len(s) == 2:
                    ap = ap.rearrange("p (a b) -> p a b", a=s[0])
                elif len(s) == 3:
                    ap = ap.rearrange("p (a b c) -> p a b c", a=s[0], b=s[1])
                cut.append(ap)
                a += n
            return whole, cut

        conv_raw = sb("conv_raw", [P, KD, DIN * TAPS])
        front_a, (conv_t, w_in_s, w_inT, _) = parts("front_a", [(TAPS, KD, DIN), (KD, 2 * DIN), (KD, DM), (KD, DM)])
        conv_x = conv_raw[:].rearrange("p a b -> p (a b)").rearrange("p (t k o) -> p t k o", t=TAPS, k=KD)
        front_b, (rT, pre, sp_e, sp_l, xsT) = parts("front_b", [(KD, L)] * 5)
        front_c, (xT, sp_w) = parts("front_c", [(KD, PAD + L), (KD, L)])
        w_x_s = sb("w_x_s", [P, KD, DTR + 2 * NST])
        w_dt_s = sb("w_dt_s", [P, DIN])
        w_out_s = sb("w_out_s", [P, KD, DM])
        NVEC = 5 * KD + N_HEADS + 2 * N_KV
        vec_rows = sb("vec_rows", [NVEC, P])
        vec = sb("vec", [P, NVEC])
        CB, BDT, DSK, LN1, LN2 = (i * KD for i in range(5))
        BQ = 5 * KD
        BV = BQ + HQK
        a_neg = sb("a_neg", [P, KD, NST])
        a_exp = sb("a_exp", [P, KD, NST])
        router = sb("router", [P, DM])
        freq = sb("freq", [P, HEAD_DIM // 2])
        cos_tab = sb("cos_tab", [P, C, HEAD_DIM])
        sin_tab = sb("sin_tab", [P, C, HEAD_DIM])
        copies = [parts(f"copy{i}", [(KD, L)] * 5 + [(C, DM)]) for i in range(2)]
        silu_r, uT, resT, delta, duT, x_rows = ([copies[i][1][j] for i in range(2)] for j in range(6))
        dtT = sb("dtT", [P, L])
        c_rows = sb("c_rows", [P, 2, C, NST])
        NDA = 8
        NDA_HERE = 6
        NBU = BU_LEAD + 1
        scan_in = sb("scan_in", [P, NDA_HERE * L + 2 * KD * L + 2 * L])
        decay = [scan_in[:, i * KD * L:(i + 1) * KD * L] for i in range(NDA_HERE // KD)]
        decay += [front_a[:, 3 * KD * L:4 * KD * L]]
        assert len(decay) == NDA // KD
        bu = [scan_in[:, (NDA_HERE + KD * i) * L:(NDA_HERE + KD * (i + 1)) * L] for i in range(2)]
        bu += [front_a[:, KD * L * i:KD * L * (i + 1)] for i in range(2)]
        bu = [slot.rearrange("p (k l) -> p k l", k=KD) for slot in bu]
        assert NBU == 4 and TAPS * KD * DIN == 2 * KD * L
        PIECE = 32
        NPIECE = 2 * PIECE + NST
        pieces = sb("pieces", [NPIECE, 2, L], BF16)
        spread = sb("spread", [NPIECE, NST, P], BF16)
        bcT = sb("bcT", [2 * NST, L])
        rest1 = sb("rest1", [NST, L])
        mid16 = sb("mid16", [NST, L], BF16)
        b_wide = scan_in[:, (NDA_HERE + 2 * KD) * L:].rearrange("p (s l) -> p s l", s=2)
        state_buf = sb("state", [P, 4 * L])
        state = state_buf[:].rearrange("p (s l) -> p s l", s=4)
        y_buf = sb("y", [P, 2 * C * DM])
        y_rows = y_buf[:].rearrange("p (s c d) -> p s c d", s=2, c=C)
        compared = y_buf[:].bitcast(BF16).rearrange("p (s c j) -> p s c j", s=2, c=C)
        gT_buf = sb("gT", [P, KD * L])
        gT = gT_buf[:].rearrange("p (k l) -> p k l", k=KD)
        z = sb("z", [P, C, DM])
        stats = sb("stats", [P, C, 6])
        mv = sb("mv", [P, B, C, 2])
        rstd = sb("rstd", [P, B, C])
        shift = sb("shift", [P, B, C])
        x1 = sb("x1", [P, B * C, NCOL])
        junk = sb("junk", [P, 2, L], BF16)
        h_buf = sb("h", [P, ST * DM + KD * S])
        score_diag = sb("score_diag", [P, C, P])
        ranks = sb("ranks", [P, 3, C])
        offset = sb("offset", [P, C])
        chosen = sb("chosen", [P, C])
        place = sb("place", [P, C])
        onehot = sb("onehot", [P, B // 2, C, 2 * K])
        sel = sb("sel", [P, ST, NCOL])
        cosT = sb("cosT", [P, S])
        sinT = sb("sinT", [P, S])
        ss = sb("ss", [P, ST])
        rrms = sb("rrms", [P, ST])
        top = sb("top", [P, N_HEADS, 2])
        bias = sb("bias", [P, N_HEADS, 2])
        sums = sb("sums", [P, N_HEADS, 2])
        rsum = sb("rsum", [P, N_HEADS, 2])
        gate = sb("gate", [P, ST, 2])
        w_dn = conv_raw[:].rearrange("p a b -> p (a b)").rearrange("p (f n) -> p f n", f=FC)
        w_gu = front_a[:].rearrange("p (k n) -> p k n", k=KD)
        w_o = front_b[:, 0:N_HEADS * DM].rearrange("p (h n) -> p h n", h=N_HEADS)
        w_v = front_c[:, 0:KD * N_KV * HEAD_DIM].rearrange("p (k n) -> p k n", k=KD)
        w_qk = copies[0][0][:].rearrange("p (k n) -> p k n", k=KD)
        qkT = scan_in[:].rearrange("p (h s) -> p h s", h=HQK)
        mT = scan_in[:, 0:FC * S].rearrange("p (f s) -> p f s", f=FC)
        oT = copies[1][0][:, 0:N_HEADS * S].rearrange("p (h s) -> p h s", h=N_HEADS)
        v_rows = copies[1][0][:, N_HEADS * S:].rearrange("p (t n) -> p t n", t=ST)
        NQK = 4
        qk_raw = state_buf[:, 0:2 * NQK * P].rearrange("p (a b s) -> p a b s", a=NQK, b=2)
        qk_swap = state_buf[:, 2 * NQK * P:].rearrange("p (a b s) -> p a b s", a=NQK, b=2)
        probs = y_buf[:, 0:9 * P].rearrange("p (a s) -> p a s", a=3)
        probsT = y_buf[:, 9 * P:15 * P].rearrange("p (a s) -> p a s", a=2)
        x_att = state_buf[:, 0:ST * DM].rearrange("p (t d) -> p t d", t=ST)
        gate_s = state_buf[:, ST * DM:ST * DM + 2 * S].rearrange("p (a s) -> p a s", a=2)
        total = scan_in[:, FC * S:FC * S + B * C * DM].rearrange("p (b c d) -> p b c d", b=B, c=C)
        out_rows = total
        selT = gT_buf[:].rearrange("p (t l) -> p t l", t=ST)
        change = score_diag[:].rearrange("p a b -> p (a b)").rearrange("p (t d) -> p t d", t=ST)
        h_rows = h_buf[:, 0:ST * DM].rearrange("p (t d) -> p t d", t=ST)
        hT = h_buf[:, ST * DM:].rearrange("p (k s) -> p k s", k=KD)

        in_x = [sem(f"in_x{i}") for i in range(2)]
        in_w = {n: sem(f"in_{n}") for n in ("w_in", "conv0", "conv1", "vec", "w_x", "w_dt", "w_out", "a", "router", "freq",
                                            "w_qk", "w_v", "w_o", "w_gu", "w_dn")}
        consts = sem("consts")
        conv_pad = sem("conv_pad")
        a_ready = sem("a_ready")
        tables = sem("tables")
        angles = sem("angles")
        dve_seq = sem("dve_seq")
        act_seq = sem("act_seq")
        pool_seq = sem("pool_seq")
        u_ready = sem("u_ready")
        silu_ready = sem("silu_ready")
        res_ready = sem("res_ready")
        sp_exp = sem("sp_exp")
        sp_one = sem("sp_one")
        sp_log = sem("sp_log")
        sp_max = sem("sp_max")
        sp_rest = sem("sp_rest")
        sum_ready = sem("sum_ready")
        du_ready = sem("du_ready")
        bu_made = sem("bu_made")
        scanned = sem("scanned")
        pieces_clear = sem("pieces_clear")
        top16 = sem("top16")
        rest_made = sem("rest_made")
        mid_made = sem("mid_made")
        low16 = sem("low16")
        decay_zeroed = sem("decay_zeroed")
        decay_made = sem("decay_made")
        g_ready = sem("g_ready")
        var_ready = sem("var_ready")
        rstd_ready = sem("rstd_ready")
        rows_ready = sem("rows_ready")
        x1_ready = sem("x1_ready")
        diag_ready = sem("diag_ready")
        chosen_ready = sem("chosen_ready")
        onehot_ready = sem("onehot_ready")
        sel_stat = sem("sel_stat")
        sel_rstd = sem("sel_rstd")
        h_ready = sem("h_ready")
        swapped = sem("swapped")
        rope_parts = sem("rope_parts")
        roped = sem("roped")
        top_ready = sem("top_ready")
        rsum_ready = sem("rsum_ready")
        normed = sem("normed")
        gate_act = sem("gate_act")
        gate_exp = sem("gate_exp")
        m_ready = sem("m_ready")
        change_ready = sem("change_ready")
        out_var = sem("out_var")
        out_rstd = sem("out_rstd")
        shift_ready = sem("shift_ready")
        out_ready = sem("out_ready")
        last_ready = sem("last_ready")
        stored = sem("stored")

        N_CONST = 10

        block = ctx.enter_context(nc.Block())

        @block.sync
        def _(sp):
            def load_x(b):
                if b >= 2:
                    wait_filled(sp, ("xT1", b - 2))
                sp.dma_start(x_rows[b % 2], x[b].rearrange("(c p) d -> p c d", p=P)).then_inc(in_x[b % 2], 16)

            def load(name, dst, src):
                sp.dma_start(dst, src).then_inc(in_w[name], 16)

            for k in range(KD):
                load(f"conv{k}", conv_raw[:, k, :], conv_w[k * P:(k + 1) * P].rearrange("p i t -> p (i t)"))
            load("w_in", w_in_s, W_in.rearrange("(k p) n -> p k n", p=P))
            load_x(0)
            row = 0
            for v, n in ((conv_b, KD), (b_dt, KD), (D, KD), (ln1_w, KD), (ln2_w, KD), (bq, N_HEADS), (bk, N_KV), (bv, N_KV)):
                load("vec", vec_rows[row:row + n, :], v.rearrange("(r p) -> r p", p=P))
                row += n
            load("w_x", w_x_s[:], W_x.rearrange("(k p) n -> p k n", p=P))
            load("w_dt", w_dt_s[:], W_dt)
            load("a", a_exp[:], A_log.rearrange("(k p) n -> p k n", p=P))
            load("freq", freq[:], inv_freq.rearrange("(o n) -> o n", o=1).partition_broadcast(P))
            load("w_out", w_out_s[:], W_out.rearrange("(k p) n -> p k n", p=P))
            load_x(1)
            load("router", router[:], w_router.rearrange("(o n) -> o n", o=1).partition_broadcast(P))
            for b in range(2, B):
                load_x(b)
            wait_filled(sp, ("r1", B - 1))
            wait_filled(sp, ("dl1", B - 1))
            sp.wait_ge(silu_ready, B)
            sp.wait_ge(sp_max, KD * B)
            sp.wait_ge(du_ready, KD * B)
            sp.wait_ge(res_ready, B)
            load("w_v", w_v, wv.rearrange("(k p) n -> p k n", p=P))
            load("w_o", w_o, wo.rearrange("(h p) n -> p h n", p=P))
            load("w_dn", w_dn, w_down.rearrange("(f p) n -> p f n", p=P))
            wait_drained(sp, ("o1", B - 2))
            load("w_qk", w_qk[:, :, 0:N_HEADS * HEAD_DIM], wq.rearrange("(k p) n -> p k n", p=P))
            load("w_qk", w_qk[:, :, N_HEADS * HEAD_DIM:], wk.rearrange("(k p) n -> p k n", p=P))
            sp.wait_ge(scanned, KD * (T_LAST + 1))
            load("w_gu", w_gu[:, :, 0:FF], w_gate.rearrange("(k p) n -> p k n", p=P))
            load("w_gu", w_gu[:, :, FF:], w_up.rearrange("(k p) n -> p k n", p=P))
            for b in range(B):
                sp.wait_ge(out_ready, b + 1)
                if b < B - 1:
                    sp.dma_start(out[b].rearrange("(c p) d -> p c d", p=P), out_rows[:, b]).then_inc(stored, 16)
            for i in range(2):
                if i == 1:
                    sp.wait_ge(last_ready, 1)
                rows = out[B - 1, 2 * i * P:2 * (i + 1) * P].rearrange("(c p) d -> p c d", p=P)
                sp.dma_start(rows, out_rows[:, B - 1, 2 * i:2 * i + 2]).then_inc(stored, 16)
            sp.wait_ge(stored, 16 * (B + 1))

        @block.tensor
        def _(pe):
            def turn(dst, src):
                return pe.transpose(dst, src, ident[:])

            pe.wait_ge(consts, 1)

            def convolve(b, o, quarter):
                name = (f"cv{o}", b)
                if quarter == 0:
                    wait_free(pe, name)
                    wait_drained(pe, ("xT0", b))
                    wait_drained(pe, ("xT1", b))
                    pe.wait_ge(conv_pad, 1)
                for j in range(2 * quarter, 2 * quarter + 2):
                    k, i = j // KD, j % KD
                    if b == 0:
                        wait_drained(pe, ("vc", 2 * i + k // 2))
                    mm = pe.matmul(at(name)[:], conv_x[:, k, i, o * P:(o + 1) * P], xT[:, i, k:k + L],
                                   start=(j == 0), stop=(j == TAPS * KD - 1))
                if quarter == 3:
                    fill_done(name, mm)

            def front(b, piece):
                o = int(piece[-1]) if piece[-1].isdigit() else 0
                name = (piece, b)
                if piece in NO_FILL:
                    return
                if piece[:2] == "cv":
                    return convolve(b, int(piece[2]), "abcd".index(piece[3]))
                wait_free(pe, name)
                t = at(name)
                if piece in ("xT0", "xT1"):
                    pe.wait_ge(in_x[b % 2], 16 * (b // 2 + 1))
                    for c in range(C):
                        mm = turn(t[:, c * P:(c + 1) * P], x_rows[b % 2][:, c, o * P:(o + 1) * P])
                elif piece in ("r0", "r1"):
                    wait_drained(pe, ("xT0", b))
                    wait_drained(pe, ("xT1", b))
                    for k in range(KD):
                        mm = pe.matmul(t[:], w_in_s[:, k, DIN + o * P:DIN + (o + 1) * P], xT[:, k, PAD:],
                                       start=(k == 0), stop=(k == KD - 1))
                elif piece == "dt":
                    pe.wait_ge(in_w["w_x"], 16)
                    pe.wait_ge(u_ready, b + 1)
                    for k in range(KD):
                        mm = pe.matmul(t[:], w_x_s[:, k, 0:DTR], uT[b % 2][:, k, :], start=(k == 0), stop=(k == KD - 1))
                elif piece == "bc":
                    for k in range(KD):
                        mm = pe.matmul(t[0:2 * NST, :], w_x_s[:, k, DTR:DTR + 2 * NST], uT[b % 2][:, k, :],
                                       start=(k == 0), stop=(k == KD - 1))
                elif piece == "cr":
                    wait_drained(pe, ("bc", b))
                    for c in range(C):
                        mm = pe.transpose(t[:, c * 2 * NST:(c + 1) * 2 * NST], bcT[:, c * P:(c + 1) * P],
                                          ident[0:2 * NST, 0:2 * NST])
                elif piece in ("dl0", "dl1"):
                    pe.wait_ge(in_w["w_dt"], 16)
                    wait_drained(pe, ("dt", b))
                    mm = pe.matmul(t[:], w_dt_s[:, o * P:(o + 1) * P], dtT[:], start=True, stop=True)
                fill_done(name, mm)

            def tail(b, piece):
                o = int(piece[-1]) if piece[-1].isdigit() else 0
                name = (piece, b)
                if piece in NO_FILL or (piece == "cs" and b % 2 == 0):
                    return
                wait_free(pe, name)
                t = at(name)
                if piece in ("yt0", "yt1"):
                    wait_drained(pe, ("hT", (b + 1) * NST - 1, o))
                    for k in range(KD):
                        for i in range(2):
                            a = k * 2 * P + i * P
                            mm = turn(t[:, a:a + P], y_rows[:, b % 2, 2 * o + i, k * P:(k + 1) * P])
                elif piece in ("o0", "o1"):
                    pe.wait_ge(in_w["w_out"], 16)
                    pe.wait_ge(g_ready, 2 * b + o + 1)
                    pe.wait_ge(res_ready, b + 1)
                    for i in range(2):
                        cols = slice((2 * o + i) * P, (2 * o + i + 1) * P)
                        for k in range(KD):
                            mm = pe.matmul(t[:, i * DM:(i + 1) * DM], gT[:, k, cols], w_out_s[:, k, :],
                                           start=(k == 0), stop=(k == KD - 1))
                        for k in range(KD):
                            a = i * DM + k * P
                            mm = pe.matmul(t[:, a:a + P], resT[b % 2][:, k, cols], ident[:], start=False,
                                           stop=True, skip_group_check=True)
                elif piece == "sb":
                    for i in range(2):
                        pe.wait_ge(diag_ready, C * b + 2 * (i + 1))
                        mm = pe.matmul(t[:, 2 * P * i:2 * P * (i + 1)], ones[:],
                                       score_diag[:, 2 * i:2 * i + 2, :].rearrange("p c j -> p (c j)"), start=True, stop=True)
                elif piece == "pf":
                    pe.wait_ge(chosen_ready, b + 1)
                    mm = pe.matmul(t[:, 0:C], before[:], chosen[:], start=True, stop=True)
                    for w in range(1, C):
                        mm = pe.matmul(t[:, w:C], ones[:], chosen[:, 0:C - w], start=False, stop=True,
                                       skip_group_check=True)
                elif piece == "ga":
                    pe.wait_ge(onehot_ready, C * (b + 1))
                    r = K * (b % 2)
                    for c in range(C):
                        mm = pe.matmul(t[r:r + K, 0:NCOL], onehot[:, b // 2, c, r:r + K], x1[:, C * b + c, :],
                                       start=(c == 0), stop=(c == C - 1))
                elif piece == "cs":
                    pe.wait_ge(tables, 4)
                    for i, tab in enumerate((cos_tab, sin_tab)):
                        for c in range(C):
                            mm = pe.matmul(t[:, i * P:(i + 1) * P], tab[:, c, :], onehot[:, b // 2, c, :],
                                           start=(c == 0), stop=(c == C - 1))
                fill_done(name, mm)

            def widen(t):
                b, n = t // NST, t % NST
                name = ("bb", t)
                wait_free(pe, name)
                if n == 0:
                    pe.wait_ge(mid_made, 2 * (b + 1))
                    pe.wait_ge(low16, b + 1)
                fill_done(name, pe.matmul(at(name)[:], spread[:, n, :], pieces[:, b % 2, :], start=True, stop=True))

            def turn_state(t):
                pe.wait_ge(scanned, KD * (t + 1))
                for cp in range(2):
                    name = ("hT", t, cp)
                    wait_free(pe, name)
                    for i in range(2):
                        for h in range(KD):
                            a = i * DM + h * P
                            c = 2 * cp + i
                            mm = turn(at(name)[:, a:a + P], state[:, 2 * (t % 2) + h, c * P:(c + 1) * P])
                    fill_done(name, mm)

            def rows_to_T(name, count):
                p = name[1]
                wait_free(pe, name)
                pe.wait_ge(h_ready, count)
                for k in range(KD):
                    mm = turn(at(name)[:, k * P:(k + 1) * P], h_rows[:, p, k * P:(k + 1) * P])
                fill_done(name, mm)

            def make_qk(p, j):
                name = ("qk", p, j)
                wait_free(pe, name)
                if j == 0:
                    pe.wait_ge(in_w["w_qk"], 32)
                    wait_drained(pe, ("h1T", p))
                for i in range(2):
                    head = 2 * j + i
                    for k in range(KD):
                        mm = pe.matmul(at(name)[:, i * P:(i + 1) * P], w_qk[:, k, head * P:(head + 1) * P],
                                       hT[:, k, p * P:(p + 1) * P], start=(k == 0), stop=(k == KD - 1))
                fill_done(name, mm)

            def make_v(v):
                p, half = v // 2, v % 2
                wait_free(pe, ("v", v))
                pe.wait_ge(in_w["w_v"], 16)
                for k in range(KD):
                    mm = pe.matmul(at(("v", v))[:], hT[:, k, p * P:(p + 1) * P], w_v[:, k, half * 512:(half + 1) * 512],
                                   start=(k == 0), stop=(k == KD - 1))
                fill_done(("v", v), mm)

            taps = conv_raw[:].rearrange("p o (i t) -> p o i t", t=TAPS)
            for v in range(4):
                o, k0 = v // 2, 2 * (v % 2)
                wait_free(pe, ("cw", v))
                pe.wait_ge(in_w[f"conv{o}"], 16)
                for k in range(2):
                    for i in range(KD):
                        a = (k * KD + i) * P
                        mm = turn(at(("cw", v))[:, a:a + P], taps[:, o, i * P:(i + 1) * P, k0 + k])
                fill_done(("cw", v), mm)
            wait_free(pe, "wT")
            pe.wait_ge(in_w["w_in"], 16)
            for i in range(KD):
                for j in range(KD):
                    a = i * DM + j * P
                    mm = turn(at("wT")[:, a:a + P], w_in_s[:, j, i * P:(i + 1) * P])
            fill_done("wT", mm)
            wait_free(pe, "vec")
            pe.wait_ge(in_w["vec"], 16 * 8)
            fill_done("vec", pe.transpose(at("vec")[:, 0:NVEC], vec_rows[:], ident[0:NVEC, 0:NVEC]))
            wait_drained(pe, "wT")
            for v in range(4):
                j, k = v // 2, 2 * (v % 2)
                wait_free(pe, ("vc", v))
                wait_drained(pe, ("cw", v % 2))
                wait_drained(pe, ("cw", 2 + v % 2))
                for i in range(KD):
                    mm = pe.matmul(at(("vc", v))[:].rearrange("p (t o) -> p t o", t=2), w_inT[:, i, j * P:(j + 1) * P],
                                   conv_t[:, k:k + 2, i, :], start=(i == 0), stop=(i == KD - 1))
                fill_done(("vc", v), mm)
            for piece in FIRST_FRONT:
                front(0, piece)
            pe.wait_ge(consts, N_CONST)
            pe.wait_ge(pieces_clear, 2)
            for piece in EARLY:
                if piece in WIDEN_BEFORE:
                    widen(WIDEN_BEFORE.index(piece))
                front(1, piece)
            for t in range(len(WIDEN_BEFORE), WIDE_LEAD):
                widen(t)
            for t in range(B * NST):
                if t >= 1:
                    turn_state(t - 1)
                if t + WIDE_LEAD <= T_LAST:
                    widen(t + WIDE_LEAD)
                for b, piece in tails(t):
                    tail(b, piece)
                for b, piece in fronts(t):
                    front(b, piece)
                if norms(t) == "ht":
                    rows_to_T(("h1T", 0), 1)
            turn_state(T_LAST)
            for piece in LAST_TAIL:
                if piece[0] == "q":
                    make_qk(0, int(piece[1:]))
                elif piece[0] == "v":
                    make_v(int(piece[1:]))
                else:
                    tail(B - 1, piece)

            rows_to_T(("h1T", 1), 2)
            for j in range(HQK // 2):
                make_qk(1, j)
            for p in range(ST):
                wait_free(pe, ("selT", p))
                for c in range(C):
                    mm = turn(at(("selT", p))[:, c * P:(c + 1) * P], onehot[:, p, c, :])
                fill_done(("selT", p), mm)
            for v in range(2, 4):
                make_v(v)

            def scores(h):
                name = ("sc", h)
                t = at(name)
                q, k = h, N_HEADS + h // (N_HEADS // N_KV)
                wait_free(pe, name)
                pe.wait_ge(roped, HQK // 2 + k // 2 + 1)
                pe.matmul(t[:, 0:P], qkT[:, q, 0:P], qkT[:, k, 0:P], start=True, stop=False)
                pe.matmul(t[:, 0:P], ident16[:], causal[:], start=False, stop=True)
                pe.matmul(t[:, P:P + S], qkT[:, q, P:S], qkT[:, k, :], start=True, stop=True)
                mm = pe.matmul(t[:, S:S + P], ident16[:], causal[:], start=False, stop=True, skip_group_check=True)
                fill_done(name, mm)

            def turn_probs(h):
                name = ("pT", h)
                wait_free(pe, name)
                pe.wait_ge(normed, 2 * (h + 1))
                for i, a in enumerate((0, P, S)):
                    mm = turn(at(name)[:, i * P:(i + 1) * P], probs[:, h % 3, a:a + P])
                fill_done(name, mm)

            def mix(h):
                name = ("o", h)
                kv = h // (N_HEADS // N_KV)
                wait_free(pe, name)
                wait_drained(pe, ("pT", h))
                if h == 0:
                    for v in range(4):
                        wait_drained(pe, ("v", v))
                pe.matmul(at(name)[:, 0:S], v_rows[:, 0, kv * P:(kv + 1) * P], probsT[:, h % 2, 0:S], start=True, stop=True)
                mm = pe.matmul(at(name)[:, P:S], v_rows[:, 1, kv * P:(kv + 1) * P], probsT[:, h % 2, S:S + P],
                               start=False, stop=True, skip_group_check=True)
                fill_done(name, mm)

            def project(h, p):
                wait_drained(pe, ("o", h))
                if h == 0:
                    wait_free(pe, ("wo", p))
                mm = pe.matmul(at(("wo", p))[:, 0:DM], oT[:, h, p * P:(p + 1) * P], w_o[:, h, :],
                               start=(h == 0), stop=(h == N_HEADS - 1))
                if h == N_HEADS - 1:
                    fill_done(("wo", p), mm)

            pe.wait_ge(in_w["w_o"], 16)
            for i in range(N_HEADS + max(LAG_OUT)):
                if i < N_HEADS:
                    scores(i)
                if 0 <= i - LAG_TURN < N_HEADS:
                    turn_probs(i - LAG_TURN)
                if 0 <= i - LAG_MIX < N_HEADS:
                    mix(i - LAG_MIX)
                for p in range(ST):
                    if 0 <= i - LAG_OUT[p] < N_HEADS:
                        project(i - LAG_OUT[p], p)
            def gate_up(p, f):
                name = ("gu", p, f)
                wait_free(pe, name)
                if f == 0:
                    wait_drained(pe, ("h2T", p))
                for i in range(2):
                    col = i * FF + f * P
                    for k in range(KD):
                        mm = pe.matmul(at(name)[:, i * P:(i + 1) * P], w_gu[:, k, col:col + P],
                                       hT[:, k, p * P:(p + 1) * P], start=(k == 0), stop=(k == KD - 1))
                fill_done(name, mm)

            def down(p):
                wait_free(pe, ("dn", p))
                for f in range(FC):
                    pe.wait_ge(m_ready, p * FC + f + 1)
                    mm = pe.matmul(at(("dn", p))[:, 0:DM], mT[:, f, p * P:(p + 1) * P], w_dn[:, f, :],
                                   start=(f == 0), stop=(f == FC - 1))
                fill_done(("dn", p), mm)

            def put_back(i):
                b, p = 2 * i // C, i // PUTS
                r = K * (b % 2)
                name = ("put", i)
                wait_free(pe, name)
                wait_drained(pe, ("selT", p))
                pe.wait_ge(change_ready, p + 1)
                for j in range(2):
                    c = (2 * i + j) % C
                    mm = pe.matmul(at(name)[:, j * DM:(j + 1) * DM], selT[r:r + K, p, c * P:(c + 1) * P],
                                   change[r:r + K, p, :], start=True, stop=True)
                fill_done(name, mm)

            rows_to_T(("h2T", 0), ST + 1)
            pe.wait_ge(in_w["w_gu"], 32)
            pe.wait_ge(in_w["w_dn"], 16)
            for p in range(ST):
                for f in range(FC):
                    if (p, f) == (0, FC - 1):
                        rows_to_T(("h2T", 1), ST + 2)
                    gate_up(p, f)
                down(p)
                for i in range(PUTS):
                    put_back(PUTS * p + i)

        @block.scalar
        def _(act):
            seq = [0]

            def link(ins):
                seq[0] += 1
                ins.then_inc(act_seq, 1)
                act.wait_ge(act_seq, seq[0])

            def copy_out(name, dst, src=None, func=ACT.Copy, **kw):
                wait_filled(act, name)
                drain_done(name, act.activation(dst, at(name)[:] if src is None else src, func, **kw))

            def flat(ap):
                return ap.rearrange("p a b -> p (a b)")

            def front(b, piece):
                o = int(piece[-1]) if piece[-1].isdigit() else 0
                name = (piece, b)
                if piece in ("xT0", "xT1"):
                    if b >= 1:
                        act.wait_ge(res_ready, b)
                    copy_out(name, xT[:, o, PAD:])
                elif piece in ("r0", "r1"):
                    if b >= 2:
                        act.wait_ge(silu_ready, b)
                    copy_out(name, (rT if b else silu_r[0])[:, o, :])
                elif piece in ("cv0d", "cv1d"):
                    o = int(piece[2])
                    if b == 0 and o == 0:
                        wait_drained(act, "vec")
                    if b >= 1:
                        act.wait_ge(res_ready, b)
                    copy_out((piece[:3], b), xsT[:, o, :], func=ACT.Identity, bias=vec[:, CB + o:CB + o + 1])
                    if b == 0 and o == 0:
                        act.preload_act_table_set("silu_and_others")
                        rope_tables()
                elif piece == "su":
                    wait_drained(act, ("cv1", b))
                    act.activation(uT[b % 2], xsT, ACT.Silu).then_inc(u_ready, 1)
                    if b == 0:
                        act.preload_act_table_set("natural_log_exp_and_others")
                elif piece == "sr":
                    if b == 1:
                        wait_drained(act, ("r1", 0))
                        act.activation(silu_r[0], silu_r[0], ACT.Silu).then_inc(silu_ready, 1)
                    wait_drained(act, ("r1", b))
                    wait_drained(act, ("r0", b))
                    if b >= 2:
                        act.wait_ge(g_ready, 2 * (b - 1))
                    act.activation(silu_r[b % 2], rT, ACT.Silu).then_inc(silu_ready, 1)
                    act.preload_act_table_set("natural_log_exp_and_others")
                elif piece == "dt":
                    copy_out(name, dtT[:])
                elif piece == "bc":
                    copy_out(name, bcT[:], at(name)[0:2 * NST, :])
                elif piece == "b0":
                    wait_drained(act, ("bc", b))
                    if b == 0:
                        act.wait_ge(pieces_clear, 1)
                    act.activation(pieces[0:NST, b % 2, :], bcT[0:NST, :], ACT.Copy).then_inc(top16, 1)
                elif piece == "cr":
                    copy_out(name, c_rows[:, b % 2], at(name)[:, 0:C * 2 * NST].rearrange("p (c n) -> p c n", c=C)[:, :, NST:])
                elif piece == "b2":
                    act.wait_ge(rest_made, b + 1)
                    act.activation(mid16[:], rest1[:], ACT.Copy).then_inc(mid_made, 1)
                    act.activation(pieces[PIECE:PIECE + NST, b % 2, :], rest1[:], ACT.Copy).then_inc(mid_made, 1)
                elif piece in ("dl0", "dl1"):
                    if b >= 1:
                        act.wait_ge(sp_max, KD * b)
                    copy_out(name, pre[:, o, :], func=ACT.Identity, bias=vec[:, BDT + o:BDT + o + 1])
                elif piece == "s1":
                    wait_drained(act, ("dl0", b))
                    if b == 0:
                        for h in range(KD):
                            wait_drained(act, (f"dl{h}", 0))
                            link(act.activation(sp_l[:, h, :], pre[:, h, :], ACT.Abs))
                            act.activation(sp_e[:, h, :], sp_l[:, h, :], ACT.Exp, scale=-1.0).then_inc(sp_exp, 1)
                        return
                    wait_drained(act, ("dl1", b))
                    act.wait_ge(du_ready, KD * b)
                    link(act.activation(sp_l, pre, ACT.Abs))
                    act.activation(sp_e, sp_l, ACT.Exp, scale=-1.0).then_inc(sp_exp, KD)
                elif piece == "s3":
                    if b == 0:
                        for h in range(KD):
                            act.wait_ge(sp_one, h + 1)
                            act.activation(sp_l[:, h, :], sp_w[:, h, :], ACT.Ln).then_inc(sp_log, 1)
                        return
                    act.wait_ge(sp_one, KD * (b + 1))
                    act.wait_ge(sp_exp, KD * (b + 1))
                    act.activation(sp_l, sp_w, ACT.Ln).then_inc(sp_log, KD)

            def rope_tables():
                half = HEAD_DIM // 2
                act.wait_ge(angles, 1)
                ang = z[:, 0:2, :].rearrange("p a b -> p (a b)").rearrange("p (c f) -> p c f", c=C)
                for tab, f0, sign in ((cos_tab, 0, 1.0), (sin_tab, half, -1.0)):
                    act.activation(tab[:, :, 0:half], ang[:, :, f0:f0 + half], ACT.Sin, scale=sign).then_inc(tables, 1)
                    act.activation(tab[:, :, half:], ang[:, :, f0:f0 + half], ACT.Sin).then_inc(tables, 1)

            def tail(b, piece):
                name = (piece, b)
                if piece in ("o0", "o1"):
                    o = int(piece[-1])
                    if b >= 1:
                        act.wait_ge(x1_ready, 2 * b)
                    copy_out(name, flat(z[:, 2 * o:2 * o + 2, :]))
                elif piece in ("la0", "la1"):
                    o = int(piece[-1])
                    act.wait_ge(rstd_ready, 2 * b + o + 1)
                    wait_drained(act, (f"o{o}", b))
                    for c in range(2 * o, 2 * o + 2):
                        ins = act.activation(x1[:, C * b + c, 0:DM], z[:, c, :], ACT.Identity, scale=rstd[:, 0, c:c + 1],
                                             bias=shift[:, 0, c:c + 1])
                    ins.then_inc(rows_ready, 1)
                elif piece == "ga":
                    r = K * (b % 2)
                    wait_filled(act, name)
                    drain_done(name, act.activation(sel[r:r + K, b // 2, :], at(name)[r:r + K, 0:NCOL], ACT.Copy))
                elif piece == "cs" and b % 2 == 1:
                    wait_filled(act, name)
                    act.activation(cosT[:, (b // 2) * P:(b // 2 + 1) * P], at(name)[:, 0:P], ACT.Copy)
                    drain_done(name, act.activation(sinT[:, (b // 2) * P:(b // 2 + 1) * P], at(name)[:, P:2 * P], ACT.Copy))

            def copy_wide(t):
                if t >= 2:
                    act.wait_ge(bu_made, t - 1)
                copy_out(("bb", t), b_wide[:, t % 2, :])

            def make_decay(t):
                b, n = t // NST, t % NST
                for h in range(KD):
                    u = KD * t + h
                    if n == 0 and h == 0:
                        act.wait_ge(sp_max, KD * (b + 1))
                        if b >= 1:
                            act.wait_ge(du_ready, KD * (b + 1))
                    if u >= NDA:
                        act.wait_ge(scanned, u - NDA + 1)
                    act.activation(decay[t % (NDA // KD)][:, h * L + 1:(h + 1) * L], delta[b % 2][:, h, 1:], ACT.Exp,
                                   scale=a_neg[:, h, n:n + 1]).then_inc(decay_made, 1)

            def rows_to_T(name, w):
                p = name[1]
                wait_filled(act, name)
                for k in range(KD):
                    last = act.activation(hT[:, k, p * P:(p + 1) * P], at(name)[:, k * P:(k + 1) * P], ACT.Copy,
                                          scale=vec[:, w + k:w + k + 1])
                drain_done(name, last)

            def exchange(p, j):
                name = ("qk", p, j)
                i0 = p * HQK // 2 + j
                wait_filled(act, name)
                if i0 == 0:
                    wait_filled(act, ("hT", T_LAST, 1))
                if i0 >= NQK:
                    act.wait_ge(roped, i0 - NQK + 1)
                mid = HEAD_DIM // 2
                for i in range(2):
                    w = BQ + 2 * j + i
                    src = at(name)[:, i * P:(i + 1) * P]
                    act.activation(qk_swap[0:mid, i0 % NQK, i, :], src[mid:, :], ACT.Identity, bias=vec[mid:, w:w + 1])
                    last = act.activation(qk_swap[mid:, i0 % NQK, i, :], src[0:mid, :], ACT.Identity,
                                          bias=vec[0:mid, w:w + 1])
                last.then_inc(swapped, 1)

            def copy_v(v):
                if v == 0:
                    act.wait_ge(bu_made, T_LAST + 1)
                copy_out(("v", v), v_rows[:, v // 2, (v % 2) * 512:(v % 2 + 1) * 512])

            for v in range(4):
                o, k = v // 2, 2 * (v % 2)
                for t in range(2):
                    name = ("cw", v)
                    wait_filled(act, name)
                    ins = act.activation(conv_t[:, k + t, :, o * P:(o + 1) * P],
                                         at(name)[:, t * KD * P:(t + 1) * KD * P].rearrange("p (i o) -> p i o", i=KD), ACT.Copy)
                drain_done(name, ins)
            copy_out("wT", flat(w_inT))
            copy_out("vec", vec[:], at("vec")[:, 0:NVEC])
            act.wait_ge(in_w["a"], 16)
            link(act.activation(a_exp[:], a_exp[:], ACT.Exp))
            act.activation(a_neg[:], a_exp[:], ACT.Copy, scale=-1.0).then_inc(a_ready, 1)
            for v in range(4):
                j, k = v // 2, 2 * (v % 2)
                copy_out(("vc", v), conv_x[:, k:k + 2, j, :], at(("vc", v))[:].rearrange("p (t o) -> p t o", t=2))
            LEAD = NDA // KD - 1
            for piece in FIRST_FRONT:
                if piece == "s3":
                    front(1, "xT0")
                    front(1, "xT1")
                front(0, piece)
            act.wait_ge(a_ready, 1)
            for t in range(2):
                copy_wide(t)
                make_decay(t)
            front(1, "cv0d")
            for t in range(2, WIDE_LEAD):
                copy_wide(t)
                if t < LEAD:
                    make_decay(t)
            for t in range(B * NST):
                if t + WIDE_LEAD <= T_LAST:
                    copy_wide(t + WIDE_LEAD)
                if t + LEAD <= T_LAST:
                    make_decay(t + LEAD)
                for b, piece in fronts(t):
                    front(b, piece)
                for b, piece in tails(t):
                    tail(b, piece)
                if norms(t) == "ht":
                    rows_to_T(("h1T", 0), LN1)
            for piece in LAST_TAIL:
                if piece[0] == "q":
                    exchange(0, int(piece[1:]))
                elif piece[0] == "v":
                    copy_v(int(piece[1:]))
                else:
                    tail(B - 1, piece)

            rows_to_T(("h1T", 1), LN1)
            for j in range(HQK // 2):
                exchange(1, j)
            for p in range(ST):
                copy_out(("selT", p), selT[:, p, :])
            for v in range(2, 4):
                copy_v(v)
            scale = float(HEAD_DIM) ** -0.5
            for i in range(N_HEADS + LAG_MIX):
                if i < N_HEADS:
                    h = i
                    act.wait_ge(top_ready, h + 1)
                    wait_filled(act, ("sc", h))
                    if h >= 3:
                        wait_filled(act, ("pT", h - 3))
                    act.activation(probs[:, h % 3, 0:P], at(("sc", h))[:, 0:P], ACT.Exp, bias=bias[:, h, 0:1],
                                   scale=scale, accum_out=sums[:, h, 0:1])
                    drain_done(("sc", h), act.activation(probs[:, h % 3, P:], at(("sc", h))[:, P:P + S], ACT.Exp,
                                                         bias=bias[:, h, 1:2], scale=scale, accum_out=sums[:, h, 1:2]))
                if i >= LAG_MIX:
                    h = i - LAG_MIX
                    w = BV + h // (N_HEADS // N_KV)
                    copy_out(("o", h), oT[:, h, :], at(("o", h))[:, 0:S], func=ACT.Identity, bias=vec[:, w:w + 1])
            act.activation(gate[:, :, 0:1], sel[:, :, DM:DM + 1], ACT.Exp, scale=-1.0).then_inc(gate_exp, 1)
            rows_to_T(("h2T", 0), LN2)
            for p in range(ST):
                for f in range(FC):
                    if (p, f) == (0, FC - 1):
                        rows_to_T(("h2T", 1), LN2)
                    i = p * FC + f
                    wait_filled(act, ("gu", p, f))
                    if i >= 2:
                        act.wait_ge(m_ready, i - 1)
                    act.activation(gate_s[:, i % 2, 0:P], at(("gu", p, f))[:, 0:P], ACT.Silu).then_inc(gate_act, 1)
            for b in range(B):
                act.wait_ge(shift_ready, b + 1)
                act.wait_ge(out_rstd, b + 1)
                for c in range(C if b < B - 1 else 2):
                    ins = act.activation(out_rows[:, b, c, :], total[:, b, c, :], ACT.Identity,
                                         scale=rstd[:, b, c:c + 1], bias=shift[:, b, c:c + 1])
                ins.then_inc(out_ready, 1)

        @block.vector
        def _(dve):
            seq = [0]

            def link(ins):
                seq[0] += 1
                ins.then_inc(dve_seq, 1)
                dve.wait_ge(dve_seq, seq[0])

            def scan(t):
                dve.wait_ge(bu_made, t + 1)
                dve.wait_ge(decay_made, KD * (t + 1))
                if t == 0:
                    dve.wait_ge(decay_zeroed, 2)
                if t >= 2:
                    wait_filled(dve, ("hT", t - 2, 1))
                dve.tensor_tensor_scan(state_buf[:, (t % 2) * KD * L:(t % 2 + 1) * KD * L], decay[t % (NDA // KD)],
                                       bu[t % NBU].rearrange("p k l -> p (k l)"), 0.0, ALU.mult, ALU.add)\
                   .then_inc(scanned, KD)

            def weigh(t):
                b, n = t // NST, t % NST
                for c in range(C):
                    name = ("hT", t, c // 2)
                    src = at(name)[:, (c % 2) * DM:(c % 2 + 1) * DM]
                    y = y_rows[:, b % 2, c, :]
                    weight = c_rows[:, b % 2, c, n:n + 1]
                    wait_filled(dve, name)
                    if n == 0:
                        if b >= 2:
                            wait_filled(dve, ("yt1", b - 2))
                            wait_drained(dve, ("sb", b - 2))
                        last = dve.tensor_scalar(y, src, weight, None, ALU.mult)
                    else:
                        wait_drained(dve, ("hT", t - 1, c // 2))
                        last = dve.scalar_tensor_tensor(out=y, in0=src, scalar=weight, in1=y, op0=ALU.mult, op1=ALU.add)
                    if c % 2:
                        drain_done(name, last)

            def front(b, piece):
                if piece == "b1":
                    dve.wait_ge(top16, b + 1)
                    if b >= 1:
                        dve.wait_ge(mid_made, 2 * b)
                    dve.tensor_tensor(rest1[:], bcT[0:NST, :], pieces[0:NST, b % 2, :], ALU.subtract).then_inc(rest_made, 1)
                elif piece == "b3":
                    dve.wait_ge(mid_made, 2 * b + 1)
                    dve.wait_ge(rest_made, b + 1)
                    dve.tensor_tensor(pieces[2 * PIECE:, b % 2, :], rest1[:], mid16[:], ALU.subtract).then_inc(low16, 1)
                elif piece == "s3" and b == 0:
                    for h in range(KD):
                        w, e, v = sp_w[:, h, :], sp_e[:, h, :], pre[:, h, :]
                        dve.wait_ge(sp_exp, h + 1)
                        dve.tensor_scalar(w, e, 1.0, None, ALU.add).then_inc(sp_one, 1)
                        dve.wait_ge(sp_one, h + 1)
                        link(dve.scalar_tensor_tensor(out=e, in0=w, scalar=-1.0, in1=e, op0=ALU.add, op1=ALU.subtract))
                        link(dve.scalar_tensor_tensor(out=e, in0=v, scalar=0.0, in1=e, op0=ALU.max, op1=ALU.subtract))
                    for h in range(KD):
                        dve.wait_ge(sp_log, h + 1)
                        dve.tensor_tensor(delta[0][:, h, :], sp_l[:, h, :], sp_e[:, h, :], ALU.add).then_inc(sp_max, 1)
                        dve.wait_ge(sp_max, h + 1)
                        dve.wait_ge(u_ready, 1)
                        dve.tensor_tensor(duT[0][:, h, :], delta[0][:, h, :], uT[0][:, h, :], ALU.mult).then_inc(du_ready, 1)
                elif piece == "s4" and b > 0:
                    dve.wait_ge(sp_log, KD * (b + 1))
                    dve.scalar_tensor_tensor(out=sp_l, in0=pre, scalar=0.0, in1=sp_l, op0=ALU.max,
                                             op1=ALU.add).then_inc(sp_max, KD)

                elif piece == "s5" and b == 1:
                    dve.wait_ge(sp_max, KD * (b + 1))
                    dve.wait_ge(sp_rest, b)
                    dve.tensor_tensor(delta[b % 2], sp_l, sp_e, ALU.add).then_inc(sum_ready, 1)
                elif piece == "s6" and b == 1:
                    dve.wait_ge(sum_ready, 1)
                    dve.wait_ge(u_ready, b + 1)
                    dve.tensor_tensor(duT[b % 2], delta[b % 2], uT[b % 2], ALU.mult).then_inc(du_ready, KD)

            def tail(b, piece):
                o = int(piece[-1]) if piece[-1].isdigit() else 0
                name = (piece, b)
                if piece in ("yt0", "yt1"):
                    wait_filled(dve, name)
                    if b >= 1:
                        wait_filled(dve, ("o1", b - 1))
                    tokens = slice(o * 2 * P, (o + 1) * 2 * P)
                    for k in range(KD):
                        ins = dve.scalar_tensor_tensor(out=gT[:, k, tokens], in0=uT[b % 2][:, k, tokens],
                                                       scalar=vec[:, DSK + k:DSK + k + 1],
                                                       in1=at(name)[:, k * 2 * P:(k + 1) * 2 * P], op0=ALU.mult, op1=ALU.add)
                    drain_done(name, ins)
                elif piece in ("ls0", "ls1"):
                    wait_drained(dve, (f"o{o}", b))
                    layer_norm_stats(z[:, 2 * o:2 * o + 2, :], 2 * o, var_ready)
                elif piece in ("lx0", "lx1"):
                    dve.wait_ge(rows_ready, 2 * b + o + 1)
                    if b == 0:
                        dve.wait_ge(in_w["router"], 16)
                    for c in range(2 * o, 2 * o + 2):
                        ins = dve.tensor_tensor_reduce(junk[:, c % 2, (c // 2) * DM:(c // 2 + 1) * DM], x1[:, C * b + c, 0:DM],
                                                       router[:], 1.0, 0.0, ALU.mult, ALU.add, x1[:, C * b + c, DM:DM + 1])
                    ins.then_inc(x1_ready, 1)
                elif piece in ("k0", "k1", "k2", "k3"):
                    c = o
                    name = ("sb", b)
                    wait_filled(dve, name)
                    dve.wait_ge(x1_ready, 2 * (b + 1))
                    score = x1[:, C * b + c, DM:DM + 1]
                    a = c * P
                    if c:
                        dve.tensor_scalar(compared[:, b % 2, c, 0:a], at(name)[:, 0:a], score, 0.0, ALU.is_ge, ALU.add,
                                          accum_out=ranks[:, 0, c:c + 1])
                    dve.tensor_scalar(compared[:, b % 2, c, a:], at(name)[:, a:], score, 0.0, ALU.is_gt, ALU.add,
                                      accum_out=ranks[:, 1, c:c + 1])
                    ins = dve.scalar_tensor_tensor(out=junk[:, 1, a:a + P], in0=at(name)[:, a:a + P], scalar=score,
                                                   in1=earlier[:], op0=ALU.is_equal, op1=ALU.mult,
                                                   accum_out=ranks[:, 2, c:c + 1])
                    if c < C - 1:
                        return
                    drain_done(name, ins)
                    wait_drained(dve, name)
                    link(dve.tensor_tensor(ranks[:, 0, :], ranks[:, 0, :], ranks[:, 1, :], ALU.add))
                    link(dve.tensor_tensor(ranks[:, 2, :], ranks[:, 0, :], ranks[:, 2, :], ALU.add))
                    dve.tensor_scalar(chosen[:], ranks[:, 2, :], float(K), None, ALU.is_lt).then_inc(chosen_ready, 1)
                    dve.wait_ge(chosen_ready, b + 1)
                    link(dve.tensor_scalar(offset[:], chosen[:], -1000.0, 1000.0, ALU.mult, ALU.add))
                    link(dve.memset(ranks[:, 0, 0:1], 0.0))
                elif piece == "pf":
                    wait_filled(dve, name)
                    drain_done(name, dve.tensor_tensor(place[:], at(name)[:, 0:C], offset[:], ALU.add))
                    wait_drained(dve, name)
                    r = K * (b % 2)
                    for c in range(C):
                        dve.tensor_scalar(onehot[:, b // 2, c, r:r + K], slot_no[:], place[:, c:c + 1], None,
                                          ALU.is_equal).then_inc(onehot_ready, 1)

            def layer_norm_stats(rows, first, signal, slot=0):
                chunks = range(first, first + rows.shape[1])
                for c in chunks:
                    ins = dve.bn_stats(stats[:, c, :], rows[:, c - first, :])
                link(ins)
                for c in chunks:
                    ins = dve.bn_aggr(mv[:, slot, c, :], stats[:, c, :])
                ins.then_inc(signal, 1)

            def norm_sum(p):
                for b in (2 * p, 2 * p + 1):
                    wait_drained(dve, ("ga", b))
                dve.tensor_tensor_reduce(h_rows[:, p, :], sel[:, p, 0:DM], sel[:, p, 0:DM], 1.0, 0.0, ALU.mult, ALU.add,
                                         ss[:, p:p + 1]).then_inc(sel_stat, 1)

            def norm_rows(p):
                dve.wait_ge(sel_stat, p + 1)
                dve.wait_ge(sel_rstd, p + 1)
                dve.tensor_scalar(h_rows[:, p, :], sel[:, p, 0:DM], rrms[:, p:p + 1], None, ALU.mult).then_inc(h_ready, 1)

            def rotate(p, j):
                name = ("qk", p, j)
                i0 = p * HQK // 2 + j
                if j == 0:
                    wait_drained(dve, ("cs", 2 * p + 1))
                dve.wait_ge(swapped, i0 + 1)
                wait_filled(dve, name)
                if i0 == 0:
                    wait_filled(dve, ("hT", T_LAST, 1))
                if i0 >= NQK:
                    dve.wait_ge(roped, i0 - NQK + 1)
                tokens = slice(p * P, (p + 1) * P)
                for i in range(2):
                    w = BQ + 2 * j + i
                    ins = dve.scalar_tensor_tensor(out=qk_raw[:, i0 % NQK, i, :], in0=at(name)[:, i * P:(i + 1) * P],
                                                   scalar=vec[:, w:w + 1], in1=cosT[:, tokens], op0=ALU.add, op1=ALU.mult)
                drain_done(name, ins)
                part = qk_swap[:, i0 % NQK]
                dve.tensor_tensor(part, part, sinT[:, tokens].unsqueeze(1).to_broadcast([P, 2, P]), ALU.mult)\
                   .then_inc(rope_parts, 1)

            half = HEAD_DIM // 2
            dve.wait_ge(consts, N_CONST)
            dve.wait_ge(in_w["freq"], 16)
            ang, turns = (z[:, 2 * i:2 * i + 2, :].rearrange("p a b -> p (a b)").rearrange("p (c f) -> p c f", c=C)
                          for i in range(2))
            for c in range(C):
                for f0 in (0, half):
                    ins = dve.tensor_scalar(ang[:, c, f0:f0 + half], freq[:], token_no[:, c:c + 1], None, ALU.mult)
            link(ins)
            link(dve.tensor_scalar(turns[:, :, 0:half], ang[:, :, 0:half], 1.0 / TWO_PI, 0.25, ALU.mult, ALU.add))
            link(dve.tensor_scalar(turns[:, :, half:], ang[:, :, half:], 1.0 / TWO_PI, None, ALU.mult))
            link(dve.tensor_scalar(turns, turns, ROUND, None, ALU.add))
            link(dve.tensor_scalar(turns, turns, -ROUND, None, ALU.add))
            for part in two_pi_parts():
                link(dve.scalar_tensor_tensor(out=ang, in0=turns, scalar=-part, in1=ang, op0=ALU.mult, op1=ALU.add))
            link(dve.tensor_scalar(ang[:, :, 0:half], ang[:, :, 0:half], float(np.pi / 2), None, ALU.add))
            dve.tensor_scalar(ang, ang, -3.1415925, 3.1415925, ALU.max, ALU.min).then_inc(angles, 1)

            for piece in FIRST_FRONT:
                front(0, piece)
            for t in range(B * NST):
                scan(t)
                if t >= 1:
                    weigh(t - 1)
                for b, piece in tails(t):
                    tail(b, piece)
                for b, piece in fronts(t):
                    front(b, piece)
                if norms(t) == "hs":
                    norm_sum(0)
                elif norms(t) == "hr":
                    norm_rows(0)
            weigh(T_LAST)
            for piece in LAST_TAIL:
                if piece[0] == "q":
                    rotate(0, int(piece[1:]))
                elif piece[0] != "v":
                    tail(B - 1, piece)

            norm_sum(1)
            norm_rows(1)
            for j in range(HQK // 2):
                rotate(1, j)
            scale = float(HEAD_DIM) ** -0.5
            for i in range(N_HEADS + LAG_TURN):
                if i < N_HEADS:
                    h = i
                    wait_filled(dve, ("sc", h))
                    dve.tensor_reduce(top[:, h, 0:1], at(("sc", h))[:, 0:P], AX.X, ALU.max)
                    link(dve.tensor_reduce(top[:, h, 1:2], at(("sc", h))[:, P:P + S], AX.X, ALU.max))
                    dve.tensor_scalar(bias[:, h, :], top[:, h, :], -scale, None, ALU.mult).then_inc(top_ready, 1)
                if 1 <= i <= N_HEADS:
                    h = i - 1
                    wait_drained(dve, ("sc", h))
                    dve.reciprocal(rsum[:, h, :], sums[:, h, :]).then_inc(rsum_ready, 1)
                if i >= LAG_TURN:
                    h = i - LAG_TURN
                    wait_filled(dve, ("pT", h))
                    if h >= 2:
                        wait_filled(dve, ("o", h - 2))
                    drain_done(("pT", h), dve.tensor_copy(probsT[:, h % 2, :], at(("pT", h))[:, 0:3 * P]))
            for p in range(ST):
                wait_filled(dve, ("wo", p))
                drain_done(("wo", p), dve.tensor_tensor(x_att[:, p, :], at(("wo", p))[:, 0:DM], sel[:, p, 0:DM], ALU.add))
                wait_drained(dve, ("wo", p))
                dve.wait_ge(h_ready, ST + p)
                wait_filled(dve, ("h1T", p))
                dve.tensor_tensor_reduce(h_rows[:, p, :], x_att[:, p, :], x_att[:, p, :], 1.0, 0.0, ALU.mult, ALU.add,
                                         ss[:, p:p + 1]).then_inc(sel_stat, 1)
                if p == 0:
                    dve.wait_ge(gate_exp, 1)
                    link(dve.tensor_scalar(gate[:, :, 0:1], gate[:, :, 0:1], 1.0, None, ALU.add))
                    link(dve.reciprocal(gate[:, :, 1:2], gate[:, :, 0:1]))
                dve.wait_ge(sel_stat, ST + p + 1)
                dve.wait_ge(sel_rstd, ST + p + 1)
                dve.tensor_scalar(h_rows[:, p, :], x_att[:, p, :], rrms[:, p:p + 1], None, ALU.mult).then_inc(h_ready, 1)
            dve.wait_ge(h_ready, 2 * ST)
            for p in range(ST):
                ins = dve.tensor_tensor(x_att[:, p, :], x_att[:, p, :], sel[:, p, 0:DM], ALU.subtract)
            link(ins)
            for p in range(ST):
                ins = dve.tensor_scalar(x_att[:, p, :], x_att[:, p, :], gate[:, p, 1:2], None, ALU.mult)
            link(ins)
            def gated(p, f):
                i = p * FC + f
                name = ("gu", p, f)
                dve.wait_ge(gate_act, i + 1)
                wait_filled(dve, name)
                drain_done(name, dve.tensor_tensor(mT[:, f, p * P:(p + 1) * P], gate_s[:, i % 2, 0:P],
                                                   at(name)[:, P:2 * P], ALU.mult))
                wait_drained(dve, name)
                dve.sem_inc(m_ready, 1)

            def make_change(p):
                wait_filled(dve, ("dn", p))
                drain_done(("dn", p), dve.scalar_tensor_tensor(
                    out=change[:, p, :], in0=at(("dn", p))[:, 0:DM], scalar=gate[:, p, 1:2], in1=x_att[:, p, :],
                    op0=ALU.mult, op1=ALU.add))
                wait_drained(dve, ("dn", p))
                dve.sem_inc(change_ready, 1)

            def add_up(i):
                b, c = i // 2, 2 * (i % 2)
                wait_filled(dve, ("put", i))
                src = at(("put", i))[:].rearrange("p (c d) -> p c d", c=2)
                drain_done(("put", i), dve.scalar_tensor_tensor(
                    out=total[:, b, c:c + 2, :], in0=x1[:, 2 * i:2 * i + 2, 0:DM], scalar=2.0, in1=src,
                    op0=ALU.mult, op1=ALU.add))

            def sum_up(i):
                b, c = i // 2, 2 * (i % 2)
                wait_drained(dve, ("put", i))
                layer_norm_stats(total[:, b, c:c + 2, :], c, out_var, b)

            def make_shift(b, chunks=slice(0, C)):
                dve.scalar_tensor_tensor(out=shift[:, b, chunks], in0=mv[:, b, chunks, 0], scalar=-1.0,
                                         in1=rstd[:, b, chunks], op0=ALU.mult, op1=ALU.mult).then_inc(shift_ready, 1)

            for f in range(FC):
                gated(0, f)
            make_change(0)
            for i in range(2):
                add_up(i)
            for i in range(2):
                sum_up(i)
            for f in range(FC):
                gated(1, f)
                if f in (0, 1):
                    add_up(2 + f)
                elif f in (3, 4):
                    sum_up(f - 1)
                elif f == 5:
                    dve.wait_ge(out_rstd, 1)
                    make_shift(0)
            dve.wait_ge(out_rstd, 2)
            make_shift(1)
            make_change(1)
            for i in range(4, 8):
                add_up(i)
                sum_up(i)
                if i == 6:
                    dve.wait_ge(out_rstd, 3)
                    make_shift(2)
            dve.wait_ge(out_rstd, 4)
            make_shift(3, slice(0, 2))
            dve.wait_ge(out_rstd, 5)
            for c in range(2, C):
                ins = dve.tensor_scalar(out_rows[:, B - 1, c, :], total[:, B - 1, c, :], mv[:, B - 1, c, 0:1],
                                        rstd[:, B - 1, c:c + 1], ALU.subtract, ALU.mult)
            ins.then_inc(last_ready, 1)

        @block.gpsimd
        def _(pool):
            seq = [0]

            def link(ins):
                seq[0] += 1
                ins.then_inc(pool_seq, 1)
                pool.wait_ge(pool_seq, seq[0])

            def const(ins):
                ins.then_inc(consts, 1)

            link(pool.memset(ones[:], 1.0))
            const(pool.affine_select(ident[:], ones[:], [[-1, P]], ALU.is_equal, 0.0, base=0, channel_multiplier=1))
            const(pool.affine_select(before[:], ones[:], [[1, P]], ALU.is_gt, 0.0, base=0, channel_multiplier=-1))
            const(pool.affine_select(ident16[:], ones[:], [[-1, P]], ALU.is_equal, 0.0, base=0, channel_multiplier=1))
            link(pool.memset(causal[:], 0.0))
            const(pool.affine_select(causal[:], causal[:], [[-1, P]], ALU.is_ge, NEG, base=0, channel_multiplier=1))
            const(pool.affine_select(earlier[:], ones[:], [[-1, P]], ALU.is_gt, 0.0, base=0, channel_multiplier=1))
            const(pool.iota(slot_no[:], [[1, K]], base=0, channel_multiplier=0, allow_small_or_imprecise_dtypes=True))
            const(pool.iota(token_no[:], [[P, C]], base=0, channel_multiplier=1, allow_small_or_imprecise_dtypes=True))
            const(pool.memset(half_pow[:], -0.5))
            const(pool.memset(sums[:], 0.0))
            const(pool.memset(ranks[:, 0, 0:1], 0.0))
            pool.memset(xT[:, :, 0:PAD], 0.0).then_inc(conv_pad, 1)
            pool.memset(pieces[:], 0.0).then_inc(pieces_clear, 1)
            link(pool.memset(spread[:], 0.0))
            for j in range(3):
                link(pool.affine_select(spread[:], spread[:], [[-1, NST], [0, P]], ALU.not_equal, 1.0,
                                        base=-PIECE * j, channel_multiplier=1))
            pool.sem_inc(pieces_clear, 1)
            pool.memset(scan_in[:, 0:NDA_HERE * L].rearrange("p (s l) -> p s l", s=NDA_HERE)[:, :, 0:1], 0.0)\
                .then_inc(decay_zeroed, 1)

            def front(b, piece):
                if piece == "rs":
                    for name in ("xT0", "xT1", "cv0", "cv1"):
                        wait_drained(pool, (name, b))
                    if b >= 2:
                        wait_filled(pool, ("o1", b - 2))
                    pool.tensor_tensor(resT[b % 2], xT[:, :, PAD:], xsT, ALU.add).then_inc(res_ready, 1)
                elif b == 0:
                    return
                elif piece == "s2":
                    pool.wait_ge(sp_exp, KD * (b + 1))
                    pool.tensor_scalar(sp_w, sp_e, 1.0, 1.0, ALU.add, ALU.mult).then_inc(sp_one, KD)
                elif piece == "s3":
                    pool.wait_ge(sp_one, KD * (b + 1))
                    pool.wait_ge(sp_log, KD * (b + 1))
                    link(pool.tensor_scalar(sp_w, sp_w, -1.0, 1.0, ALU.add, ALU.mult))
                    pool.tensor_tensor(sp_e, sp_e, sp_w, ALU.subtract).then_inc(sp_rest, 1)
                elif piece == "s5" and b > 1:
                    pool.wait_ge(sp_rest, b)
                    pool.wait_ge(sp_max, KD * (b + 1))
                    link(pool.tensor_tensor(delta[b % 2], sp_l, sp_e, ALU.add))
                elif piece == "s6" and b > 1:
                    pool.wait_ge(u_ready, b + 1)
                    pool.tensor_tensor(duT[b % 2], delta[b % 2], uT[b % 2], ALU.mult).then_inc(du_ready, KD)

            def make_bu(t):
                b = t // NST
                wait_drained(pool, ("bb", t))
                if t % NST == 0:
                    pool.wait_ge(du_ready, KD * (b + 1))
                if t >= NBU:
                    pool.wait_ge(scanned, KD * (t - NBU + 1))
                pool.tensor_tensor(bu[t % NBU], duT[b % 2], b_wide[:, t % 2, :].unsqueeze(1).to_broadcast([P, KD, L]),
                                   ALU.mult).then_inc(bu_made, 1)

            def inv_sqrt(dst, var, eps, scale=1.0):
                link(pool.tensor_scalar(dst, var, scale, eps, ALU.mult, ALU.add))
                return pool.tensor_tensor(dst, dst, half_pow[:, 0:dst.shape[1]], ALU.pow)

            def rms(count, halves):
                pool.wait_ge(sel_stat, count)
                inv_sqrt(rrms[:, halves], ss[:, halves], RMS_EPS, 1.0 / DM).then_inc(sel_rstd, 1)

            def add_rotated(p, j):
                name = ("qk", p, j)
                i0 = p * HQK // 2 + j
                wait_drained(pool, name)
                pool.wait_ge(rope_parts, i0 + 1)
                pool.tensor_tensor(qkT[:, 2 * j:2 * j + 2, p * P:(p + 1) * P], qk_raw[:, i0 % NQK], qk_swap[:, i0 % NQK],
                                   ALU.add).then_inc(roped, 1)

            def tail(b, piece):
                if piece in ("g0", "g1"):
                    o = int(piece[-1])
                    wait_drained(pool, (f"yt{o}", b))
                    pool.wait_ge(silu_ready, b + 1)
                    tokens = slice(o * 2 * P, (o + 1) * 2 * P)
                    pool.tensor_tensor(gT[:, :, tokens], gT[:, :, tokens], silu_r[b % 2][:, :, tokens], ALU.mult).then_inc(g_ready, 1)
                elif piece in ("lp0", "lp1"):
                    o = int(piece[-1])
                    chunks = slice(2 * o, 2 * o + 2)
                    pool.wait_ge(var_ready, 2 * b + o + 1)
                    if b >= 1:
                        pool.wait_ge(rows_ready, 2 * b)
                    mean, var = (mv[:, 0, chunks, i:i + 1].rearrange("p c o -> p (c o)") for i in range(2))
                    pool.tensor_scalar(shift[:, 0, chunks], mean, -1.0, 1.0, ALU.mult, ALU.mult)
                    link(inv_sqrt(rstd[:, 0, chunks], var, LN_EPS))
                    pool.tensor_tensor(shift[:, 0, chunks], shift[:, 0, chunks], rstd[:, 0, chunks], ALU.mult)\
                        .then_inc(rstd_ready, 1)
                elif piece in ("ld0", "ld1"):
                    o = int(piece[-1])
                    pool.wait_ge(x1_ready, 2 * b + o + 1)
                    if b >= 1:
                        wait_filled(pool, ("sb", b - 1))
                    for c in range(2 * o, 2 * o + 2):
                        pool.tensor_scalar(score_diag[:, c, :], ident[:], x1[:, C * b + c, DM:DM + 1], 1.0,
                                           ALU.mult, ALU.mult).then_inc(diag_ready, 1)

            for piece in FIRST_FRONT:
                front(0, piece)
            wait_filled(pool, ("vc", 3))
            pool.memset(decay[-1].rearrange("p (k l) -> p k l", k=KD)[:, :, 0:1], 0.0).then_inc(decay_zeroed, 1)
            for t in range(BU_LEAD):
                make_bu(t)
            for t in range(B * NST):
                if t + BU_LEAD <= T_LAST:
                    make_bu(t + BU_LEAD)
                for b, piece in tails(t):
                    tail(b, piece)
                for b, piece in fronts(t):
                    front(b, piece)
                if norms(t) == "hp":
                    rms(1, slice(0, 1))
            for piece in LAST_TAIL:
                if piece[0] == "q":
                    add_rotated(0, int(piece[1:]))
                elif piece[0] != "v":
                    tail(B - 1, piece)

            rms(2, slice(1, 2))
            for j in range(HQK // 2):
                add_rotated(1, j)
            for h in range(N_HEADS):
                pool.wait_ge(rsum_ready, h + 1)
                pool.tensor_scalar(probs[:, h % 3, 0:P], probs[:, h % 3, 0:P], rsum[:, h, 0:1], 1.0, ALU.mult,
                                   ALU.mult).then_inc(normed, 1)
                pool.tensor_scalar(probs[:, h % 3, P:], probs[:, h % 3, P:], rsum[:, h, 1:2], 1.0, ALU.mult,
                                   ALU.mult).then_inc(normed, 1)
            for p in range(ST):
                rms(ST + p + 1, slice(p, p + 1))
            for b, c0, c1 in [(b, 0, C) for b in range(B - 1)] + [(B - 1, 0, 2), (B - 1, 2, C)]:
                pool.wait_ge(out_var, 2 * b + c1 // 2)
                inv_sqrt(rstd[:, b, c0:c1], mv[:, b, c0:c1, 1:2].rearrange("p c o -> p (c o)"), LN_EPS).then_inc(out_rstd, 1)


_OUTS = [((4, 512, 256), "float32")]


def kernel(**inputs):
    import concourse.bacc as _bacc
    from concourse.bass_utils import run_bass_kernel_spmd as _run

    nc = _bacc.Bacc("TRN2", target_bir_lowering=False, num_devices=1)
    order = ["L0_attn_" + n for n in ("x", "W_in", "conv_w", "conv_b", "W_x", "W_dt", "b_dt", "A_log", "D", "W_out")]
    order += ["L0_ffn_" + n for n in ("w_router", "wq", "bq", "wk", "bk", "wv", "bv", "wo", "w_gate", "w_up", "w_down",
                                      "ln1_w", "ln2_w")]
    arrays, args = {}, []
    for name in order:
        a = np.ascontiguousarray(inputs[name])
        arrays[f"in_{name}"] = a
        args.append(nc.dram_tensor(f"in_{name}", a.shape, mybir.dt.from_np(a.dtype), kind="ExternalInput").ap())
    freq = (1.0 / ROPE_THETA ** (np.arange(0, HEAD_DIM, 2, dtype=np.float32) / HEAD_DIM)).astype(np.float32)
    arrays["in_inv_freq"] = freq
    args.append(nc.dram_tensor("in_inv_freq", freq.shape, F32, kind="ExternalInput").ap())
    shape, dtype = _OUTS[0]
    args.append(nc.dram_tensor("out_0", shape, mybir.dt.from_np(np.dtype(dtype)), kind="ExternalOutput").ap())
    block_kernel(nc, *args)
    r = _run(nc, [arrays], core_ids=[0])
    return r.results[0]["out_0"]
```
